# Optimizing a Trainium2 kernel written in Bass

```python
import numpy as np
import jax
import jax.numpy as jnp

def _softmax(x, axis=-1):
    return jax.nn.softmax(x, axis=axis)

def _gelu(x):
    return jax.nn.gelu(x, approximate=True)

def _silu(x):
    return jax.nn.silu(x)

def _sigmoid(x):
    return jax.nn.sigmoid(x)

def _layernorm(x, axis=-1, eps=1e-05):
    m = jnp.mean(x, axis=axis, keepdims=True)
    v = jnp.var(x, axis=axis, keepdims=True)
    return (x - m) / jnp.sqrt(v + eps)

def _scatter_add(tgt, idx, src, axis=0):
    return tgt.at[idx].add(src)

def _segment_sum(src, seg, n):
    return jax.ops.segment_sum(src, seg, n)
kernel_name = 'mk_macaron_d1_jaxref_r4_7b093c'

def setup_inputs(seed: int=0):
    np.random.seed(seed)
    _w = jnp.asarray

    def _L0_attn_setup():
        import jax, jax.numpy as jnp
        import numpy as np
        import math
        D_MODEL = 256
        N_HEADS = 16
        HEAD_DIM = D_MODEL // N_HEADS
        CTX_LEN = 256
        POOL_OUT = 64

        def _heads(x):
            B, S, _ = x.shape
            return x.reshape(B, S, N_HEADS, HEAD_DIM)

        def _cross_attn(seq, ctx, Wq, Wk, Wv, Wo):
            B, S, _ = seq.shape
            Q = _heads(seq @ Wq)
            K = _heads(ctx @ Wk)
            V = _heads(ctx @ Wv)
            scale = 1.0 / math.sqrt(HEAD_DIM)
            scores = jnp.einsum('bqhd,bkhd->bhqk', Q, K) * scale
            probs = jax.nn.softmax(scores, axis=-1)
            out = jnp.einsum('bhqk,bkhd->bqhd', probs, V).reshape(B, S, D_MODEL)
            return out @ Wo

        def _causal_self_attn(x, Wq, Wk, Wv, Wo):
            B, S, _ = x.shape
            Q = _heads(x @ Wq)
            K = _heads(x @ Wk)
            V = _heads(x @ Wv)
            scale = 1.0 / math.sqrt(HEAD_DIM)
            scores = jnp.einsum('bqhd,bkhd->bhqk', Q, K) * scale
            causal = jnp.tril(jnp.ones((S, S), dtype=bool))
            scores = jnp.where(causal[None, None], scores, -jnp.inf)
            probs = jax.nn.softmax(scores, axis=-1)
            out = jnp.einsum('bhqk,bkhd->bqhd', probs, V).reshape(B, S, D_MODEL)
            return out @ Wo
        key = jax.random.key(seed)
        ks = jax.random.split(key, 8)
        s = 1.0 / math.sqrt(D_MODEL)
        return {'hidden_states': jax.random.normal(ks[0], (2, 4096, D_MODEL), dtype=jnp.float32), 'Wq': jax.random.normal(ks[1], (D_MODEL, D_MODEL), dtype=jnp.float32) * s, 'Wk': jax.random.normal(ks[2], (D_MODEL, D_MODEL), dtype=jnp.float32) * s, 'Wv': jax.random.normal(ks[3], (D_MODEL, D_MODEL), dtype=jnp.float32) * s, 'Wo': jax.random.normal(ks[4], (D_MODEL, D_MODEL), dtype=jnp.float32) * s, 'W1': jax.random.normal(ks[5], (D_MODEL, D_MODEL // 2), dtype=jnp.float32) * s, 'b1': jnp.zeros((D_MODEL // 2,), dtype=jnp.float32), 'W2': jax.random.normal(ks[6], (D_MODEL // 2, D_MODEL), dtype=jnp.float32) * (1.0 / math.sqrt(D_MODEL // 2)), 'b2': jnp.zeros((D_MODEL,), dtype=jnp.float32)}
    _L0_attn_in = _L0_attn_setup()

    def _L0_ffn_setup():
        import jax, jax.numpy as jnp
        import numpy as np
        DIM = 256
        EXPERT_DIM = 128
        N_EXPERTS = 16
        TOPK = 2
        SHARED_HIDDEN = EXPERT_DIM * TOPK
        B, T = (4, 256)

        def _moe_forward(x, router_w, router_bias, up_proj, gate_proj, down_proj, sh_gate, sh_up, sh_down):
            Bb, Tt, D = x.shape
            flat = x.reshape(Bb * Tt, D)
            N = flat.shape[0]
            logits = flat @ router_w.T
            topk_scores, topk_idx = jax.lax.top_k(logits + router_bias, TOPK)
            topk_scores = jax.nn.softmax(topk_scores, axis=-1)
            combine = jnp.zeros((N, N_EXPERTS), flat.dtype)
            combine = combine.at[jnp.arange(N)[:, None], topk_idx].add(topk_scores)
            up_all = jnp.einsum('nd,kde->nke', flat, up_proj)
            gate_all = jnp.einsum('nd,kde->nke', flat, gate_proj)
            hidden = jax.nn.silu(gate_all) * up_all
            down_all = jnp.einsum('nke,ked->nkd', hidden, down_proj)
            out = jnp.einsum('nk,nkd->nd', combine, down_all)
            sh_hidden = jax.nn.silu(flat @ sh_gate.T) * (flat @ sh_up.T)
            out = out + sh_hidden @ sh_down.T
            return out.reshape(Bb, Tt, D)
        key = jax.random.key(seed)
        ks = jax.random.split(key, 9)
        std = 0.02
        return {'x': jax.random.normal(ks[0], (B, T, DIM), jnp.float32), 'router_w': jax.random.normal(ks[1], (N_EXPERTS, DIM), jnp.float32) * std, 'router_bias': jnp.zeros((N_EXPERTS,), jnp.float32), 'up_proj': jax.random.normal(ks[2], (N_EXPERTS, DIM, EXPERT_DIM), jnp.float32) * std, 'gate_proj': jax.random.normal(ks[3], (N_EXPERTS, DIM, EXPERT_DIM), jnp.float32) * std, 'down_proj': jax.random.normal(ks[4], (N_EXPERTS, EXPERT_DIM, DIM), jnp.float32) * std, 'sh_gate': jax.random.normal(ks[5], (SHARED_HIDDEN, DIM), jnp.float32) * std, 'sh_up': jax.random.normal(ks[6], (SHARED_HIDDEN, DIM), jnp.float32) * std, 'sh_down': jax.random.normal(ks[7], (DIM, SHARED_HIDDEN), jnp.float32) * std}
    _L0_ffn_in = _L0_ffn_setup()
    _d = {'L0_attn_hidden_states': _L0_attn_in['hidden_states'], 'L0_attn_Wq': _L0_attn_in['Wq'], 'L0_attn_Wk': _L0_attn_in['Wk'], 'L0_attn_Wv': _L0_attn_in['Wv'], 'L0_attn_Wo': _L0_attn_in['Wo'], 'L0_attn_W1': _L0_attn_in['W1'], 'L0_attn_b1': _L0_attn_in['b1'], 'L0_attn_W2': _L0_attn_in['W2'], 'L0_attn_b2': _L0_attn_in['b2'], 'L0_ffn_router_w': _L0_ffn_in['router_w'], 'L0_ffn_router_bias': _L0_ffn_in['router_bias'], 'L0_ffn_up_proj': _L0_ffn_in['up_proj'], 'L0_ffn_gate_proj': _L0_ffn_in['gate_proj'], 'L0_ffn_down_proj': _L0_ffn_in['down_proj'], 'L0_ffn_sh_gate': _L0_ffn_in['sh_gate'], 'L0_ffn_sh_up': _L0_ffn_in['sh_up'], 'L0_ffn_sh_down': _L0_ffn_in['sh_down']}
    _x0 = _d['L0_attn_hidden_states']
    _d['L0_attn_hidden_states'] = jax.random.normal(jax.random.fold_in(jax.random.key(seed), 1), (4, 2048, 256), dtype=_x0.dtype)
    del _x0
    return _d

def reference(L0_attn_hidden_states, L0_attn_Wq, L0_attn_Wk, L0_attn_Wv, L0_attn_Wo, L0_attn_W1, L0_attn_b1, L0_attn_W2, L0_attn_b2, L0_ffn_router_w, L0_ffn_router_bias, L0_ffn_up_proj, L0_ffn_gate_proj, L0_ffn_down_proj, L0_ffn_sh_gate, L0_ffn_sh_up, L0_ffn_sh_down):

    def _L0_attn_ref(hidden_states, Wq, Wk, Wv, Wo, W1, b1, W2, b2):
        import jax, jax.numpy as jnp
        import numpy as np
        import math
        D_MODEL = 256
        N_HEADS = 16
        HEAD_DIM = D_MODEL // N_HEADS
        CTX_LEN = 256
        POOL_OUT = 64

        def _heads(x):
            B, S, _ = x.shape
            return x.reshape(B, S, N_HEADS, HEAD_DIM)

        def _cross_attn(seq, ctx, Wq, Wk, Wv, Wo):
            B, S, _ = seq.shape
            Q = _heads(seq @ Wq)
            K = _heads(ctx @ Wk)
            V = _heads(ctx @ Wv)
            scale = 1.0 / math.sqrt(HEAD_DIM)
            scores = jnp.einsum('bqhd,bkhd->bhqk', Q, K) * scale
            probs = jax.nn.softmax(scores, axis=-1)
            out = jnp.einsum('bhqk,bkhd->bqhd', probs, V).reshape(B, S, D_MODEL)
            return out @ Wo

        def _causal_self_attn(x, Wq, Wk, Wv, Wo):
            B, S, _ = x.shape
            Q = _heads(x @ Wq)
            K = _heads(x @ Wk)
            V = _heads(x @ Wv)
            scale = 1.0 / math.sqrt(HEAD_DIM)
            scores = jnp.einsum('bqhd,bkhd->bhqk', Q, K) * scale
            causal = jnp.tril(jnp.ones((S, S), dtype=bool))
            scores = jnp.where(causal[None, None], scores, -jnp.inf)
            probs = jax.nn.softmax(scores, axis=-1)
            out = jnp.einsum('bhqk,bkhd->bqhd', probs, V).reshape(B, S, D_MODEL)
            return out @ Wo
        B, S, D = hidden_states.shape
        initial = hidden_states[:, :CTX_LEN]
        remaining = hidden_states[:, CTX_LEN:]
        comp = jax.nn.relu(initial @ W1 + b1) @ W2 + b2
        comp = comp.reshape(B, POOL_OUT, CTX_LEN // POOL_OUT, D).mean(axis=2)
        remaining_out = _cross_attn(remaining, comp, Wq, Wk, Wv, Wo)
        initial_out = _causal_self_attn(initial, Wq, Wk, Wv, Wo)
        return jnp.concatenate([initial_out, remaining_out], axis=1)

    def _L0_ffn_ref(x, router_w, router_bias, up_proj, gate_proj, down_proj, sh_gate, sh_up, sh_down):
        import jax, jax.numpy as jnp
        import numpy as np
        DIM = 256
        EXPERT_DIM = 128
        N_EXPERTS = 16
        TOPK = 2
        SHARED_HIDDEN = EXPERT_DIM * TOPK
        B, T = (4, 256)

        def _moe_forward(x, router_w, router_bias, up_proj, gate_proj, down_proj, sh_gate, sh_up, sh_down):
            Bb, Tt, D = x.shape
            flat = x.reshape(Bb * Tt, D)
            N = flat.shape[0]
            logits = flat @ router_w.T
            topk_scores, topk_idx = jax.lax.top_k(logits + router_bias, TOPK)
            topk_scores = jax.nn.softmax(topk_scores, axis=-1)
            combine = jnp.zeros((N, N_EXPERTS), flat.dtype)
            combine = combine.at[jnp.arange(N)[:, None], topk_idx].add(topk_scores)
            up_all = jnp.einsum('nd,kde->nke', flat, up_proj)
            gate_all = jnp.einsum('nd,kde->nke', flat, gate_proj)
            hidden = jax.nn.silu(gate_all) * up_all
            down_all = jnp.einsum('nke,ked->nkd', hidden, down_proj)
            out = jnp.einsum('nk,nkd->nd', combine, down_all)
            sh_hidden = jax.nn.silu(flat @ sh_gate.T) * (flat @ sh_up.T)
            out = out + sh_hidden @ sh_down.T
            return out.reshape(Bb, Tt, D)
        return _moe_forward(x, router_w, router_bias, up_proj, gate_proj, down_proj, sh_gate, sh_up, sh_down)
    x = L0_attn_hidden_states
    x = x + 0.5 * _L0_ffn_ref(_layernorm(x, axis=-1), L0_ffn_router_w, L0_ffn_router_bias, L0_ffn_up_proj, L0_ffn_gate_proj, L0_ffn_down_proj, L0_ffn_sh_gate, L0_ffn_sh_up, L0_ffn_sh_down)
    x = x + _L0_attn_ref(_layernorm(x, axis=-1), L0_attn_Wq, L0_attn_Wk, L0_attn_Wv, L0_attn_Wo, L0_attn_W1, L0_attn_b1, L0_attn_W2, L0_attn_b2)
    x = x + 0.5 * _L0_ffn_ref(_layernorm(x, axis=-1), L0_ffn_router_w, L0_ffn_router_bias, L0_ffn_up_proj, L0_ffn_gate_proj, L0_ffn_down_proj, L0_ffn_sh_gate, L0_ffn_sh_up, L0_ffn_sh_down)
    return x

_drawn_inputs = setup_inputs


def setup_inputs(seed=0):
    import zlib

    import numpy as np

    out = dict(_drawn_inputs(seed))
    spreads = {'L0_attn_b1': (0.0, 0.1), 'L0_attn_b2': (0.0, 0.1), 'L0_ffn_router_bias': (0.0, 0.8)}
    factors = {'L0_ffn_router_w': 8.0,
     'L0_ffn_up_proj': 7.934,
     'L0_ffn_gate_proj': 8.0,
     'L0_ffn_down_proj': 7.925,
     'L0_ffn_sh_gate': 3.824,
     'L0_ffn_sh_up': 3.765,
     'L0_ffn_sh_down': 3.765}
    for name, (base, spread) in spreads.items():
        noise = np.random.default_rng([zlib.crc32(name.encode()), seed]).standard_normal(out[name].shape)
        drawn = base * np.exp(spread * noise) if base else spread * noise
        out[name] = jnp.asarray(drawn.astype(out[name].dtype))
    for name, factor in factors.items():
        out[name] = (out[name] * factor).astype(out[name].dtype)
    return out
```

```python
from contextlib import ExitStack

import concourse.bass as bass
from concourse import mybir

F32 = mybir.dt.float32
F32R = mybir.dt.float32r
BF16 = mybir.dt.bfloat16
I32 = mybir.dt.int32
U32 = mybir.dt.uint32
ALU = mybir.AluOpType
ACT = mybir.ActivationFunctionType
AX = mybir.AxisListType
ds = bass.ds

P = 128
B, S, D = 4, 2048, 256
KC = D // P
NE = 16
EH = 128
SH = 256
TB = S // P
PB = TB // 2
ET = 2 * S // P + NE
EP = ET // 2
H, HD = 16, 16
CTX = 256
CK = 64
EPS = 1e-5
SCALE = HD ** -0.5
MASKED = -1.0e30
RSQRT_GUESS = float(0x5F3759DF)
NEWTON = 3
ROUND = 8388608.0
NS = 4


class Signal:

    def __init__(self, sem, per=1, head=4):
        self.sem, self.per, self.head = sem, per, head

    def done(self, g, k=None):
        return (g + self.head) * self.per + (self.per if k is None else k)

    def freed(self, g, n):
        return (g - n + self.head + 1) * self.per


def steps(eng, n, todo):
    last = max(lag for lag, _ in todo)
    head = (last + NS - 1) // NS * NS
    loops = (n - head) // NS

    def turn(i, r, inside):
        for lag, step in todo:
            if inside or 0 <= i - lag < n:
                step(i - lag, (r - lag) % NS)

    for i in range(head):
        turn(i, i, False)
    if loops > 1:
        with eng.Fori(0, loops) as j:
            for r in range(NS):
                turn(j * NS + (head + r), r, True)
    elif loops == 1:
        for r in range(NS):
            turn(head + r, r, True)
    for i in range(head + loops * NS, n + last):
        turn(i, i, False)


def macaron_kernel(nc, x_in, wq, wk, wv, wo, w1, b1, w2, b2, rw_t, rbias, up, gate, down,
                   shg_t, shu_t, shd_t, out, plan, dbg=None):
    ctx = ExitStack()
    with ctx:
        def sb(name, shape, dt=F32):
            return ctx.enter_context(nc.sbuf_tensor(name, shape, dt))

        def signal(name, per=1, head=4):
            return Signal(ctx.enter_context(nc.semaphore(name)), per, head)

        xs = [nc.dram_tensor(f"slot_rows{i}", [ET * P, D], F32).ap() for i in range(2)]
        ys = [nc.dram_tensor(f"slot_results{i}", [ET * P, D], F32).ap() for i in range(2)]
        acc_d = nc.dram_tensor("partial_sums", [B * S, D], F32).ap()
        acc_v = acc_d.rearrange("(g t p) d -> g p t d", t=2, p=P)
        x_v = x_in.rearrange("b (g t p) d -> (b g) p t d", t=2, p=P)
        out_v = out.rearrange("b (g t p) d -> (b g) p t d", t=2, p=P)
        xs_v = [a.rearrange("(g t p) d -> g p t d", t=2, p=P) for a in xs]
        ys_v = [a.rearrange("(g t p) d -> g p t d", t=2, p=P) for a in ys]

        raw = sb("raw_weights", [P, 4, KC, 2 * EH])
        eg_h = sb("expert_gate_up_high", [P, NE, KC, 2 * EH], F32R)
        eg_l = sb("expert_gate_up_low", [P, NE, KC, 2 * EH], F32R)
        ed = sb("expert_down", [P, NE, D])
        sg_h = sb("shared_gate_up_high", [P, 2, KC, SH], F32R)
        sg_l = sb("shared_gate_up_low", [P, 2, KC, SH], F32R)
        sd = sb("shared_down", [P, SH // P, D])
        rw = sb("router_weights", [P, KC, NE])
        rw_h = sb("router_high", [P, KC, NE], F32R)
        rw_l = sb("router_low", [P, KC, NE], F32R)
        rb = sb("router_bias", [P, NE])
        wq_h = sb("wq_high", [P, KC, D], F32R)
        wq_l = sb("wq_low", [P, KC, D], F32R)
        wk_s = sb("wk", [P, KC, D])
        wv_s = sb("wv", [P, KC, D])
        wo_s = sb("wo", [P, KC, D])
        w1_s = sb("w1", [P, KC, P])
        w2_s = sb("w2", [P, D])
        b1_s = sb("b1", [P, 1])
        b2_s = sb("b2", [P, KC])
        ident = sb("identity", [P, P])
        ones_f = sb("ones", [P, NE])
        below = sb("strictly_below", [P, P], BF16)
        ones_b = sb("ones_bf16", [P, P], BF16)
        iota_i = sb("iota_int", [P, ET], I32)
        iota_f = sb("iota", [P, ET])
        restart = sb("restart", [P, NE, TB])
        ident_b = sb("identity_bf16", [P, P], BF16)
        mask_q = sb("mask_query_key", [P, P], BF16)
        mask_k = sb("mask_key_query", [P, P], BF16)
        minus = sb("minus_by_head", [P, H * CK], F32R)
        cmask = sb("identity_of_even_heads", [P, P])
        parity = sb("head_parity", [P, 2])
        rows = sb("rows", [P, NS, 2, D])
        outs = sb("result_rows", [P, NS, 2, D])
        xn = sb("normalised_rows", [P, 2, TB, D])
        xt_h = sb("rows_transposed_high", [P, 2, KC, 2 * P], F32R)
        xt_l = sb("rows_transposed_low", [P, 2, KC, 2 * P], F32R)
        work = sb("hidden_work", [P, 3, 2, 2 * P])
        th, hid, ht = work[:, 0], work[:, 1], work[:, 2]
        gath = raw.rearrange("p (s t) k d -> p s t k d", s=2)
        xa = raw[:, 2]
        xf = raw[:, 3]
        xt_f = xf
        q_h = sb("queries_high", [P, 2, KC, 2 * P], F32R)
        q_l = sb("queries_low", [P, 2, KC, 2 * P], F32R)
        k_h = sb("keys_high", [P, KC, CTX], F32R)
        k_l = sb("keys_low", [P, KC, CTX], F32R)
        kc_h = sb("compressed_keys_high", [P, KC, 2 * CK], F32R)
        kc_l = sb("compressed_keys_low", [P, KC, 2 * CK], F32R)
        va = sb("values_and_ones", [P, 2, H, HD + 1])
        vc = sb("compressed_values_and_ones", [P, H // 2, 2, HD + 1])
        hc = sb("compress_hidden", [P, CTX])
        zeros = hc
        hm = sb("compress_hidden_sums", [P, CK])
        cm = sb("compressed_transposed", [P, KC, 2, CK])
        mx = sb("score_maxima", [P, 2, P])
        mt = sb("score_maxima_transposed", [P, 2 * P], F32R)
        pt = raw[:, 0:2].rearrange("p a b c -> p a (b c)")
        rden = sb("reciprocal_sums", [P, 2, H])
        bst = sb("bn_stats", [P, NS, 2, 6])
        lnd = sb("mean_difference", [P, 2, 2])
        lnm = sb("mean", [P, 2, 2])
        lnv = sb("variance", [P, 2, 2])
        lnw = sb("variance_of_halves", [P, 2, 2])
        rstd = sb("rstd", [P, 2, 2])
        rsq = sb("rsqrt_steps", [P, 2, 2])
        logits = sb("logits", [P, TB, NE])
        top = sb("top_values", [P, TB, 8])
        topi = sb("top_indices", [P, TB, 8], U32)
        topf = sb("top_indices_float", [P, 2, TB])
        route_work = work.rearrange("p a b c -> p (a b c)")
        onehot = route_work[:, 0:2 * NE * TB].rearrange("p (k e t) -> p k e t", k=2, e=NE)
        rank, tot, incl = (route_work[:, n * NE * TB:(n + 1) * NE * TB].rearrange("p (e t) -> p e t", e=NE) for n in (2, 3, 4))
        cmpb = route_work[0:1, 0:ET * NE].rearrange("p (t e) -> p t e", e=NE)
        picked = sb("picked", [P, NE, TB], BF16)
        tiles_of = sb("tiles_of_expert", [P, NE])
        tiles_in = sb("tiles_up_to_expert", [P, NE])
        base = sb("first_tile_of_expert", [P, NE])
        slotf = sb("slot_float", [P, 2, TB])
        slot = sb("slot", [P, 2, 2, TB], U32)
        wexp = sb("weight_exp", [P, 3, TB])
        wts = sb("weights", [P, 2, 2, TB])
        texp = sb("expert_of_tile_float", [1, ET])
        table = sb("expert_of_tile", [1, 2, ET], I32)

        bank = [ctx.enter_context(nc.psum_tensor(f"bank{i}", [P, 512], F32)) for i in range(8)]

        weights_in = signal("weights_in", 16, 0)
        raw_in = [signal(f"raw_in{i}", 16, 0) for i in range(4)]
        raw_split = signal("raw_split", 2, 4)
        router_split = signal("router_split", 2, 0)
        consts = signal("constants_ready", 1, 0)
        gp_step = signal("gpsimd_constant_steps", 1, 0)
        xs_zeroed = signal("slot_rows_zeroed", 16, 0)
        phase_done = {e: signal(f"phase_done_{e}", 1, 0) for e in ("pe", "act", "dve")}
        rows_in = [signal(f"rows_in{i}", 16, 0) for i in range(NS)]
        outs_stored = [signal(f"results_stored{i}", 16, 0) for i in range(NS)]
        ln_stats = signal("ln_stats", 2)
        ln_small = signal("ln_small_steps", 9 + 3 * NEWTON)
        ln_rows = signal("ln_rows_normalised", 2)
        tr_pe = signal("rows_transposed")
        tr_high = signal("transposed_high_split")
        tr_low = signal("transposed_low_split")
        logits_pe = signal("logits_multiplied")
        logits_dve = signal("logits_biased")
        gu_pe = signal("shared_gate_up_multiplied")
        gu_tanh = signal("shared_tanh")
        gu_hid = signal("shared_hidden", 2)
        dn_pe = signal("shared_down_multiplied")
        t_out = signal("token_sums_ready")
        route = signal("route_steps", 1, 0)
        route_pe = signal("ranks_counted", 1, 0)
        route_act = signal("route_exp", 1, 0)
        routed = signal("slots_ready", 1, 0)
        table_ready = signal("expert_table_ready", 1, 0)
        scattered = [signal(f"scattered{i}", 16 * 2 * TB, 0) for i in range(2)]
        gathered = [signal(f"gathered{i}", 64, 0) for i in range(2)]
        e_tr = signal("slot_rows_transposed")
        e_high = signal("slot_high_split")
        e_low = signal("slot_low_split")
        e_gu = signal("expert_gate_up_multiplied")
        e_tanh = signal("expert_tanh")
        e_hid = signal("expert_hidden", 2)
        e_htr = signal("expert_hidden_transposed")
        e_ht = signal("expert_hidden_evacuated")
        e_dn = signal("expert_down_multiplied")
        e_out = signal("expert_rows_ready")
        c_out = signal("combined_rows", 4)
        a_tr = signal("attention_rows_transposed")
        a_high = signal("attention_high_split")
        a_low = signal("attention_low_split")
        a_q = signal("queries_multiplied")
        a_qh = signal("queries_high_split", 2)
        a_ql = signal("queries_low_split", 2)
        a_mtr = signal("maxima_transposed")
        a_mt = signal("maxima_evacuated")
        a_pv = signal("values_multiplied", 2)
        a_den = signal("sums_inverted", 2)
        a_norm = signal("heads_normalised", 2)
        a_otr = signal("heads_transposed")
        a_ot = signal("heads_evacuated")
        a_wo = signal("output_multiplied")
        a_out = signal("attention_sums_ready")
        x_sm = signal("cross_scores", 4)
        x_mx = signal("cross_maxima", 4)
        x_st = signal("cross_scores_transposed", 4)
        x_exp = signal("cross_exp", 4)
        x_pv = signal("cross_values_steps", 4)
        s_xf = signal("context_evacuated")
        s_kv = signal("context_keys_values_multiplied", 2)
        s_kh = signal("context_keys_high")
        s_kl = signal("context_keys_low")
        s_va = signal("context_values_evacuated")
        s_h = signal("compress_hidden_multiplied")
        s_hc = signal("compress_relu")
        s_hm = signal("compress_summed")
        s_cp = signal("compress_multiplied")
        s_cm = signal("compressed_evacuated")
        s_ckv = signal("compressed_keys_values_multiplied", 2)
        s_ckh = signal("compressed_keys_high")
        s_ckl = signal("compressed_keys_low")
        s_vc = signal("compressed_values_evacuated")
        s_sm = signal("self_scores", 12)
        s_mx = signal("self_maxima", 12)
        s_st = signal("self_scores_transposed", H)
        s_exp = signal("self_exp", H)
        s_pv = signal("self_values_steps", H)
        attn_in = signal("attention_weights_in", 16, 0)
        parity_step = signal("head_parity_steps", 2, 0)

        count = {"T": 0, "E": 0, "C": 0, "R": 0, "A": 0}
        all_pairs = 0
        phases = []
        for n, (kind, layer, b) in enumerate(plan):
            ph = {"kind": kind, "layer": layer, "b": b, "n": n, "ring": all_pairs, "par": b % 2}
            ph["ln"] = count["T"] + count["A"]
            if kind == "T":
                ph.update(t=count["T"], r=count["R"])
                count["T"] += PB
                count["R"] += 1
                all_pairs += PB
            elif kind == "E":
                ph.update(e=count["E"], r=sum(1 for k, l, c in plan[:n] if k == "E"))
                count["E"] += EP
                all_pairs += EP
            elif kind == "C":
                ph.update(c=count["C"])
                count["C"] += PB
                all_pairs += PB
            elif kind == "A":
                ph.update(a=count["A"])
                count["A"] += PB
                all_pairs += PB
            phases.append(ph)

        def fence(eng, me, n):
            for other in phase_done:
                if other != me and n:
                    eng.wait_ge(phase_done[other].sem, n)

        block = ctx.enter_context(nc.Block())

        def used(ph, i, s):
            return (i - s + ph["ring"]) * (16 // NS) + 16

        @block.sync
        def _(sp):
            for m, w in enumerate((shg_t, shu_t)):
                sp.dma_start(raw[:, m, :, :], w.rearrange("(k p) h -> p k h", p=P)).then_inc(raw_in[m].sem, 16)
            sp.dma_start(rw[:], rw_t.rearrange("(k p) e -> p k e", p=P)).then_inc(weights_in.sem, 16)
            sp.dma_start(rb[:], rbias.rearrange("(a e) -> a e", a=1).broadcast_to([P, NE])).then_inc(weights_in.sem, 16)
            sp.dma_start(sd[:], shd_t.rearrange("(k p) d -> p k d", p=P)).then_inc(weights_in.sem, 16)

            for dst, src in ((wk_s, wk), (wv_s, wv), (wo_s, wo), (w1_s, w1)):
                sp.dma_start(dst[:], src.rearrange("(k p) n -> p k n", p=P)).then_inc(attn_in.sem, 16)
            sp.dma_start(w2_s[:], w2).then_inc(attn_in.sem, 16)
            sp.dma_start(b1_s[:], b1.rearrange("(p a) -> p a", a=1)).then_inc(attn_in.sem, 16)
            for k in range(KC):
                sp.dma_start(b2_s[:, k:k + 1], b2[k * P:(k + 1) * P].rearrange("(p a) -> p a", a=1))\
                    .then_inc(attn_in.sem, 16)

            def load(ph):
                src = {"T": x_v if ph["layer"] == 0 else acc_v, "C": acc_v, "A": acc_v}.get(ph["kind"])
                first = ph["b"] * PB
                if ph["kind"] == "E":
                    src, first = xs_v[ph["par"]], 0

                def step(i, s):
                    if ph["kind"] == "T":
                        sp.wait_ge(t_out.sem, t_out.freed(ph["t"] + i, NS))
                    elif ph["kind"] == "E":
                        sp.wait_ge(e_tr.sem, e_tr.freed(ph["e"] + i, NS))
                    elif ph["kind"] == "A":
                        sp.wait_ge(a_out.sem, a_out.freed(ph["a"] + i, NS))
                    else:
                        sp.wait_ge(c_out.sem, c_out.freed(ph["c"] + i, NS))
                    sp.dma_start(rows[:, s, :, :], src[ds(first + i, 1)].rearrange("a p t d -> p (a t) d"))\
                        .then_inc(rows_in[s].sem, 16)
                return step

            def store(ph):
                dst = {"T": acc_v, "A": acc_v, "C": out_v if ph["layer"] else acc_v}.get(ph["kind"])
                first = ph["b"] * PB
                if ph["kind"] == "E":
                    dst, first = ys_v[ph["par"]], 0

                def step(i, s):
                    if ph["kind"] == "T":
                        sp.wait_ge(t_out.sem, t_out.done(ph["t"] + i))
                    elif ph["kind"] == "E":
                        sp.wait_ge(e_out.sem, e_out.done(ph["e"] + i))
                    elif ph["kind"] == "A":
                        sp.wait_ge(a_out.sem, a_out.done(ph["a"] + i))
                    else:
                        sp.wait_ge(c_out.sem, c_out.done(ph["c"] + i))
                    sp.dma_start(dst[ds(first + i, 1)].rearrange("a p t d -> p (a t) d"), outs[:, s, :, :])\
                        .then_inc(outs_stored[s].sem, 16)
                return step

            experts_left = list(range(NE))

            def load_expert(e):
                k = e + 2
                sp.wait_ge(raw_split.sem, raw_split.freed(k, 4))
                for m, w in enumerate((gate, up)):
                    sp.dma_start(raw[:, k % 4, :, m * EH:(m + 1) * EH],
                                 w[e].rearrange("(k p) h -> p k h", p=P)).then_inc(raw_in[k % 4].sem, 16)

            for ph in phases:
                if ph["n"]:
                    for other in phase_done:
                        sp.wait_ge(phase_done[other].sem, ph["n"])
                if ph["kind"] == "E":
                    sp.wait_ge(scattered[ph["par"]].sem, 16 * 2 * TB * (ph["r"] // 2 + 1))
                if ph["kind"] in "CA" or (ph["kind"] == "T" and ph["layer"]):
                    for s in range(NS):
                        sp.wait_ge(outs_stored[s].sem, ph["ring"] * (16 // NS))
                steps(sp, EP if ph["kind"] == "E" else PB, [(0, load(ph)), ({"T": 4, "E": 5, "C": 3, "A": 3}[ph["kind"]], store(ph))])
                if ph["n"] == 0:
                    for e in experts_left:
                        load_expert(e)
                    k = NE + 2
                    sp.wait_ge(raw_split.sem, raw_split.freed(k, 4))
                    sp.dma_start(raw[:, k % 4], wq.rearrange("(k p) n -> p k n", p=P)).then_inc(raw_in[k % 4].sem, 16)
                    sp.dma_start(ed[:], down.rearrange("e p d -> p e d")).then_inc(weights_in.sem, 16)
            for s in range(NS):
                sp.wait_ge(outs_stored[s].sem, all_pairs * (16 // NS))

        @block.gpsimd
        def _(gp):
            def made(ins):
                ins.then_inc(gp_step.sem, 1)
                made.n += 1
                gp.wait_ge(gp_step.sem, made.n)
            made.n = 0
            gp.sem_inc(raw_split.sem, raw_split.head * raw_split.per)
            made(gp.memset(ident[:], 0.0))
            made(gp.affine_select(out=ident[:], in_=ident[:], compare_op=ALU.not_equal, fill=1.0, base=0,
                                  pattern=[[-1, P]], channel_multiplier=1))
            made(gp.memset(zeros[:], 0.0))
            gp.memset(ones_b[:], 1.0).then_inc(consts.sem, 1)
            made(gp.memset(ones_f[:], 1.0))
            made(gp.memset(below[:], 1.0))
            made(gp.affine_select(out=below[:], in_=below[:], compare_op=ALU.is_gt, fill=0.0, base=0,
                                  pattern=[[1, P]], channel_multiplier=-1))
            made(gp.memset(restart[:], 1.0))
            made(gp.memset(restart[:, :, 0:1], 0.0))
            made(gp.iota(iota_i[:], pattern=[[1, ET]], base=0, channel_multiplier=0))
            made(gp.tensor_copy(iota_f[:], iota_i[:]))
            gp.memset(zeros[:], 0.0).then_inc(consts.sem, 1)
            made(gp.tensor_copy(ident_b[:], ident[:]))
            made(gp.memset(mask_q[:], MASKED))
            made(gp.affine_select(out=mask_q[:], in_=mask_q[:], compare_op=ALU.is_gt, fill=0.0, base=0,
                                  pattern=[[1, P]], channel_multiplier=-1))
            made(gp.memset(mask_k[:], MASKED))
            made(gp.affine_select(out=mask_k[:], in_=mask_k[:], compare_op=ALU.is_gt, fill=0.0, base=0,
                                  pattern=[[-1, P]], channel_multiplier=1))
            made(gp.tensor_scalar(minus[:].rearrange("p (h k) -> p h k", h=H),
                                  ident[:, 0:H].unsqueeze(2).broadcast_to([P, H, CK]), -1.0, None, ALU.mult))
            made(gp.memset(mx[:], 0.0))
            made(gp.memset(va[:], 1.0))
            made(gp.memset(vc[:], 0.0))
            made(gp.memset(vc[0:CK, :, 0, HD:HD + 1], 1.0))
            made(gp.memset(vc[CK:P, :, 1, HD:HD + 1], 1.0))
            made(gp.memset(cmask[:], 1.0))
            made(gp.memset(cmask[:].rearrange("p (g m r) -> p g m r", m=2, r=HD)[:, :, 1, :], 0.0))
            made(gp.tensor_tensor(cmask[:], cmask[:], ident[:], ALU.mult))

            gp.wait_ge(consts.sem, 2)
            for i in range(2):
                gp.dma_start(xs[i].rearrange("(t p) d -> p t d", p=P),
                             zeros[:].rearrange("p (a d) -> p a d", a=1).broadcast_to([P, ET, D]))\
                    .then_inc(xs_zeroed.sem, 16)

            gp.wait_ge(weights_in.sem, 16 * 3)
            gp.tensor_copy(rw_h[:], rw[:]).then_inc(router_split.sem, 1)
            gp.wait_ge(router_split.sem, 1)
            gp.tensor_tensor(rw_l[:], rw[:], rw_h[:].bitcast(F32), ALU.subtract).then_inc(router_split.sem, 1)
            for k in range(NE + 3):
                e = k - 2
                gp.wait_ge(raw_in[k % 4].sem, 16 * (1 if k < 2 else (2 * ((k - 2) // 4 + 1) + (1 if k % 4 < 2 else 0)) - (1 if k == NE + 2 else 0)))
                hi, lo = (sg_h[:, k], sg_l[:, k]) if k < 2 else (eg_h[:, e], eg_l[:, e]) if e < NE else (wq_h[:], wq_l[:])
                gp.tensor_copy(hi, raw[:, k % 4]).then_inc(raw_split.sem, 1)
                gp.wait_ge(raw_split.sem, raw_split.done(k, 1))
                gp.tensor_tensor(lo, raw[:, k % 4], hi.bitcast(F32), ALU.subtract).then_inc(raw_split.sem, 1)

            gp.wait_ge(xs_zeroed.sem, 32)

            def scatter(ph):
                gp.wait_ge(routed.sem, ph["r"] + 1)
                par = ph["par"]
                for t in range(TB):
                    for k in range(2):
                        gp.indirect_dma_start(xs[par], bass.IndirectOffsetOnAxis(ap=slot[:, par, k, t:t + 1], axis=0),
                                              xn[:, par, t, :], None).then_inc(scattered[par].sem, 16)

            def gather(ph):
                par = ph["par"]
                fence(gp, "gp", ph["n"])
                gp.wait_ge(raw_split.sem, raw_split.done(NE + 2))
                before = max(q["ring"] + EP for q in phases[:ph["n"]] if q["kind"] == "E" and q["b"] == ph["b"])
                for s in range(NS):
                    gp.wait_ge(outs_stored[s].sem, before * (16 // NS))
                for i in range(PB):
                    c = ph["c"] + i
                    gp.wait_ge(c_out.sem, c_out.freed(c, 2))
                    for t in range(2):
                        for k in range(2):
                            gp.indirect_dma_start(
                                gath[:, c % 2, t, k, :], None, ys[par],
                                bass.IndirectOffsetOnAxis(ap=slot[:, par, k, 2 * i + t:2 * i + t + 1], axis=0))\
                                .then_inc(gathered[c % 2].sem, 16)

            for ph in phases:
                if ph["kind"] == "T":
                    scatter(ph)
                elif ph["kind"] == "C":
                    gather(ph)

        @block.scalar
        def _(act):
            for sig in (tr_high, gu_tanh, e_high, e_tanh, e_out, a_high, a_qh, a_mt, a_ot, x_exp, s_xf, s_kh, s_va,
                        s_hc, s_cm, s_ckh, s_vc, s_exp):
                act.sem_inc(sig.sem, sig.head * sig.per)

            def tokens(ph):
                def high(i, s):
                    g, k = ph["t"] + i, s % 2
                    act.wait_ge(tr_pe.sem, tr_pe.done(g))
                    act.wait_ge(gu_pe.sem, gu_pe.freed(g, 2))
                    act.activation(flat(xt_h[:, k]), bank[k][:], ACT.Copy)\
                        .then_inc(tr_high.sem, 1)

                def tanh(i, s):
                    g = ph["t"] + i
                    act.wait_ge(gu_pe.sem, gu_pe.done(g))
                    act.wait_ge(gu_hid.sem, gu_hid.freed(g, 1))
                    act.activation(flat(th[:]), bank[2][:], ACT.Tanh, scale=0.5)\
                        .then_inc(gu_tanh.sem, 1)

                steps(act, PB, [(1, high), (2, tanh)])
                act.wait_ge(route.sem, ph["r"] * ROUTE + ROUTE_D)
                act.activation(wexp[:, 1, :], wexp[:, 0, :], ACT.Exp).then_inc(route_act.sem, 1)

            def experts(ph):
                def high(i, s):
                    g, k = ph["e"] + i, s % 2
                    act.wait_ge(e_tr.sem, e_tr.done(g))
                    act.wait_ge(e_gu.sem, e_gu.freed(g, 2))
                    act.activation(flat(xt_h[:, k]), bank[k][:], ACT.Copy)\
                        .then_inc(e_high.sem, 1)

                def tanh(i, s):
                    g, k = ph["e"] + i, s % 2
                    act.wait_ge(e_gu.sem, e_gu.done(g))
                    act.wait_ge(e_hid.sem, e_hid.freed(g, 2))
                    act.activation(th[:, k].rearrange("p (t n) -> p t n", t=2),
                                   bank[2 + k][:].rearrange("p (t m n) -> p t m n", t=2, m=2)[:, :, 0, :],
                                   ACT.Tanh, scale=0.5).then_inc(e_tanh.sem, 1)

                def result(i, s):
                    g = ph["e"] + i
                    act.wait_ge(e_dn.sem, e_dn.done(g))
                    act.wait_ge(outs_stored[s].sem, used(ph, i, s) - 16)
                    act.activation(flat(outs[:, s]), bank[6 + s % 2][:], ACT.Copy)\
                        .then_inc(e_out.sem, 1)

                steps(act, EP, [(0, high), (1, tanh), (3, result)])

            def attention(ph):
                for i in range(PB):
                    a, b = ph["a"] + i, ph["a"] // PB
                    x = a - b - 1
                    act.wait_ge(a_tr.sem, a_tr.done(a))
                    act.activation(flat(xt_h[:, 0]), bank[0][:], ACT.Copy).then_inc(a_high.sem, 1)
                    if i == 0:
                        act.activation(flat(xf), bank[0][:], ACT.Copy).then_inc(s_xf.sem, 1)
                        act.wait_ge(a_q.sem, a_q.done(a))
                        for m in range(2):
                            act.activation(flat(q_h[:, m]), bank[1][:], ACT.Copy, scale=parity[:, m:m + 1])\
                                .then_inc(a_qh.sem, 1)
                        act.wait_ge(s_kv.sem, s_kv.done(b, 1))
                        act.activation(flat(k_h[:]), bank[2][:], ACT.Copy).then_inc(s_kh.sem, 1)
                        act.wait_ge(s_kv.sem, s_kv.done(b, 2))
                        act.activation(va[:, :, :, 0:HD], bank[3][:].rearrange("p (t h d) -> p t h d", t=2, d=HD),
                                       ACT.Copy).then_inc(s_va.sem, 1)
                        act.wait_ge(s_h.sem, s_h.done(b))
                        act.activation(hc[:], bank[4][:, 0:CTX], ACT.Relu, bias=b1_s[:, 0:1]).then_inc(s_hc.sem, 1)
                        act.wait_ge(s_cp.sem, s_cp.done(b))
                        for k in range(KC):
                            for m in range(2):
                                ins = act.activation(cm[:, k, m, :], bank[5][:, k * CK:(k + 1) * CK], ACT.Identity,
                                                     bias=b2_s[:, k:k + 1], scale=0.25)
                        ins.then_inc(s_cm.sem, 1)
                        act.wait_ge(s_ckv.sem, s_ckv.done(b, 1))
                        keys = bank[6][:, 0:KC * CK].rearrange("p (k n) -> p k n", k=KC)
                        for m in range(2):
                            ins = act.activation(kc_h[:, :, m * CK:(m + 1) * CK], keys, ACT.Copy, scale=parity[:, m:m + 1])
                        ins.then_inc(s_ckh.sem, 1)
                        act.wait_ge(s_ckv.sem, s_ckv.done(b, 2))
                        for m in range(2):
                            ins = act.activation(vc[m * CK:(m + 1) * CK, :, m, 0:HD],
                                                 bank[7][m * CK:(m + 1) * CK, 0:D]
                                                 .rearrange("p (g m d) -> p g m d", m=2, d=HD)[:, :, m, :], ACT.Copy)
                        ins.then_inc(s_vc.sem, 1)
                    else:
                        act.wait_ge(a_q.sem, a_q.done(a))
                        act.activation(flat(q_h[:, 0]), bank[1][:], ACT.Copy).then_inc(a_qh.sem, 2)
                    act.wait_ge(a_mtr.sem, a_mtr.done(a))
                    act.activation(mt[:], bank[MT_BANK][:, 0:2 * P], ACT.Copy).then_inc(a_mt.sem, 1)
                    if i == 0:
                        for h in range(H):
                            act.wait_ge(s_st.sem, s_st.done(b, h + 1))
                            act.wait_ge(s_pv.sem, s_pv.done(b, h + 1) - 2)
                            act.activation(pt[:, h % 2, 0:3 * P], bank[h % 4][:, 0:3 * P], ACT.Exp, scale=SCALE)\
                                .then_inc(s_exp.sem, 1)
                    else:
                        for n in range(4):
                            act.wait_ge(x_st.sem, x_st.done(x, n + 1))
                            act.wait_ge(x_pv.sem, x_pv.done(x, n + 1) - 2)
                            act.activation(pt[:, n % 2, :], bank[2 + n][:], ACT.Exp, scale=SCALE).then_inc(x_exp.sem, 1)
                    act.wait_ge(a_otr.sem, a_otr.done(a))
                    act.activation(flat(xt_f), bank[0][:], ACT.Copy).then_inc(a_ot.sem, 1)

            for ph in phases:
                fence(act, "act", ph["n"])
                {"T": tokens, "E": experts, "C": lambda ph: None, "A": attention}[ph["kind"]](ph)
                act.drain().then_inc(phase_done["act"].sem, 1)

        @block.vector
        def _(dve):
            for sig in (ln_stats, ln_small, ln_rows, tr_low, logits_dve, gu_hid, t_out, e_low, e_hid, e_ht, c_out, a_low,
                        a_ql, a_den, a_norm, a_out, x_mx, s_kl, s_hm, s_ckl, s_mx):
                dve.sem_inc(sig.sem, sig.head * sig.per)

            def tokens(ph):
                par = ph["par"]

                def norm(i, s):
                    g, k = ph["ln"] + i, s % 2
                    dve.wait_ge(rows_in[s].sem, used(ph, i, s))
                    for t in range(2):
                        dve.bn_stats(bst[:, k, t, :], rows[:, s, t, :]).then_inc(ln_stats.sem, 1)
                    dve.wait_ge(ln_stats.sem, ln_stats.done(g))
                    layer_norm(g, k, lambda t: rows[:, s, t, :],
                               lambda t: xn[:, par, ds(2 * i + t, 1), :].rearrange("p a d -> p (a d)"))

                def low(i, s):
                    g, k = ph["t"] + i, s % 2
                    dve.wait_ge(tr_high.sem, tr_high.done(g))
                    dve.tensor_tensor(flat(xt_l[:, k]), bank[k][:], flat(xt_h[:, k]).bitcast(F32), ALU.subtract)\
                        .then_inc(tr_low.sem, 1)

                def bias(i, s):
                    g = ph["t"] + i
                    dve.wait_ge(logits_pe.sem, logits_pe.done(g))
                    dve.tensor_tensor(logits[:, ds(2 * i, 2), :],
                                      bank[4][:, 0:2 * NE].rearrange("p (t e) -> p t e", t=2),
                                      rb[:].unsqueeze(1).broadcast_to([P, 2, NE]), ALU.add)\
                        .then_inc(logits_dve.sem, 1)

                def hidden(i, s):
                    g = ph["t"] + i
                    dve.wait_ge(gu_tanh.sem, gu_tanh.done(g))
                    dve.scalar_tensor_tensor(flat(th[:]), flat(th[:]), 1.0, bank[2][:], ALU.add, ALU.mult)\
                        .then_inc(gu_hid.sem, 1)
                    dve.wait_ge(gu_hid.sem, gu_hid.done(g, 1))
                    dve.wait_ge(dn_pe.sem, dn_pe.freed(g, 1))
                    dve.tensor_tensor(flat(hid[:]), flat(th[:]), bank[3][:], ALU.mult).then_inc(gu_hid.sem, 1)

                def sums(i, s):
                    g = ph["t"] + i
                    dve.wait_ge(dn_pe.sem, dn_pe.done(g))
                    dve.wait_ge(outs_stored[s].sem, used(ph, i, s) - 16)
                    dve.scalar_tensor_tensor(flat(outs[:, s]), bank[6 + s % 2][:], 0.25, flat(rows[:, s]),
                                             ALU.mult, ALU.add).then_inc(t_out.sem, 1)

                steps(dve, PB, [(1, low), (2, bias), (2, hidden), (3, sums), (0, norm)])
                routing(ph)

            def layer_norm(g, k, src, dst):
                even, odd = bst[:, k, :, 0:3], bst[:, k, :, 3:6]

                def small(n, ins):
                    ins.then_inc(ln_small.sem, 1)

                def after(n):
                    dve.wait_ge(ln_small.sem, ln_small.done(g, n))

                small(1, dve.tensor_tensor(lnd[:, k, :], even[:, :, 1], odd[:, :, 1], ALU.subtract))
                small(2, dve.tensor_tensor(lnm[:, k, :], even[:, :, 1], odd[:, :, 1], ALU.add))
                small(3, dve.tensor_tensor(lnv[:, k, :], even[:, :, 2], odd[:, :, 2], ALU.add))
                after(1)
                small(4, dve.scalar_tensor_tensor(lnw[:, k, :], lnd[:, k, :], 0.25, lnd[:, k, :], ALU.mult, ALU.mult))
                after(2)
                small(5, dve.tensor_scalar(lnm[:, k, :], lnm[:, k, :], 0.5, None, ALU.mult))
                after(4)
                small(6, dve.scalar_tensor_tensor(lnv[:, k, :], lnv[:, k, :], 1.0 / D, lnw[:, k, :], ALU.mult, ALU.add))
                after(6)
                small(7, dve.tensor_scalar(lnv[:, k, :], lnv[:, k, :], EPS, None, ALU.add))
                after(7)
                small(8, dve.tensor_scalar(rsq[:, k, :].bitcast(I32), lnv[:, k, :].bitcast(I32), 1, None,
                                           ALU.logical_shift_right))
                after(8)
                small(9, dve.tensor_scalar(rstd[:, k, :].bitcast(I32), rsq[:, k, :].bitcast(I32), -1.0, RSQRT_GUESS,
                                           ALU.mult, ALU.add))
                n = 9
                for _ in range(NEWTON):
                    after(n)
                    small(n + 1, dve.tensor_tensor(rsq[:, k, :], rstd[:, k, :], rstd[:, k, :], ALU.mult))
                    after(n + 1)
                    small(n + 2, dve.scalar_tensor_tensor(rsq[:, k, :], rsq[:, k, :], -0.5, lnv[:, k, :],
                                                          ALU.mult, ALU.mult))
                    after(n + 2)
                    small(n + 3, dve.scalar_tensor_tensor(rstd[:, k, :], rsq[:, k, :], 1.5, rstd[:, k, :],
                                                          ALU.add, ALU.mult))
                    n += 3
                after(n)
                for t in range(2):
                    dve.tensor_scalar(dst(t), src(t), lnm[:, k, t:t + 1], rstd[:, k, t:t + 1],
                                      ALU.subtract, ALU.mult).then_inc(ln_rows.sem, 1)

            def routing(ph):
                par = ph["par"]
                start = ph["r"] * ROUTE
                n = [0]

                def step(ins):
                    n[0] += 1
                    ins.then_inc(route.sem, 1)
                    return n[0]

                def after(k):
                    dve.wait_ge(route.sem, start + k)

                dve.wait_ge(logits_dve.sem, logits_dve.done(ph["t"] + PB - 1))
                for t in range(TB):
                    a = step(dve.max(top[:, t, :], logits[:, t, :]))
                after(a)
                for t in range(TB):
                    a = step(dve.max_index(topi[:, t, :], top[:, t, :], logits[:, t, :]))
                d = step(dve.tensor_tensor(wexp[:, 0, :], top[:, :, 1], top[:, :, 0], ALU.subtract))
                assert d == ROUTE_D
                after(a)
                a = step(dve.tensor_copy(topf[:].rearrange("p k t -> p t k"), topi[:, :, 0:2]))
                after(a)
                for k in range(2):
                    a = step(dve.tensor_tensor(onehot[:, k], iota_f[:, 0:NE].unsqueeze(2).broadcast_to([P, NE, TB]),
                                               topf[:, k, :].unsqueeze(1).broadcast_to([P, NE, TB]), ALU.is_equal))
                after(a)
                a = step(dve.tensor_tensor(flat(picked[:]), flat(onehot[:, 0]), flat(onehot[:, 1]), ALU.add))
                assert a == ROUTE_PICKED
                dve.wait_ge(route_pe.sem, ph["r"] + 1)
                before, totals = bank[4][:, 0:NE * TB], bank[4][:, NE * TB:2 * NE * TB]
                a = step(dve.tensor_copy(flat(tot[:]), totals))
                after(a)
                step(dve.tensor_tensor(flat(rank[:]), before, flat(tot[:]), ALU.subtract))
                a = step(dve.tensor_tensor_scan(flat(incl[:]), flat(restart[:]), flat(tot[:]), 0.0, ALU.mult, ALU.add))
                after(a)
                step(dve.tensor_tensor(flat(rank[:]), flat(rank[:]), flat(incl[:]), ALU.add))
                a = step(dve.tensor_scalar(tiles_of[:], incl[:, :, TB - 1], (P - 1) / 2, 1.0 / P, ALU.add, ALU.mult))
                after(a)
                a = step(dve.tensor_scalar(tiles_of[:], tiles_of[:], ROUND, None, ALU.add))
                after(a)
                a = step(dve.tensor_scalar(tiles_of[:], tiles_of[:], -ROUND, None, ALU.add))
                after(a)
                a = step(dve.tensor_tensor_scan(tiles_in[:], ones_f[:, 0:NE], tiles_of[:], 0.0, ALU.mult, ALU.add))
                after(a)
                a = step(dve.tensor_tensor(base[:], tiles_in[:], tiles_of[:], ALU.subtract))
                after(a)
                a = step(dve.scalar_tensor_tensor(rank[:], base[:].unsqueeze(2).broadcast_to([P, NE, TB]), float(P),
                                                  rank[:], ALU.mult, ALU.add))
                after(a)
                for k in range(2):
                    a = step(dve.tensor_tensor(flat(onehot[:, k]), flat(onehot[:, k]), flat(rank[:]), ALU.mult))
                after(a)
                for k in range(2):
                    a = step(dve.tensor_reduce(slotf[:, k, :], onehot[:, k].rearrange("p e t -> p t e"), AX.X, ALU.add))
                after(a)
                dve.tensor_copy(slot[:, par], slotf[:]).then_inc(routed.sem, 1)
                dve.wait_ge(route_act.sem, ph["r"] + 1)
                a = step(dve.tensor_scalar(wexp[:, 2, :], wexp[:, 1, :], 1.0, None, ALU.add))
                after(a)
                a = step(dve.reciprocal(wexp[:, 2, :], wexp[:, 2, :]))
                after(a)
                step(dve.tensor_scalar(wts[:, par, 0, :], wexp[:, 2, :], 0.25, None, ALU.mult))
                step(dve.scalar_tensor_tensor(wts[:, par, 1, :], wexp[:, 1, :], 0.25, wexp[:, 2, :], ALU.mult, ALU.mult))
                a = step(dve.tensor_tensor(cmpb[:], iota_f[0:1, :].unsqueeze(2).broadcast_to([1, ET, NE]),
                                           tiles_in[0:1, :].unsqueeze(1).broadcast_to([1, ET, NE]), ALU.is_ge))
                after(a)
                a = step(dve.tensor_reduce(texp[:], cmpb[:], AX.X, ALU.add))
                after(a)
                dve.tensor_scalar(table[:, par, :], texp[:], NE - 1.0, None, ALU.min).then_inc(table_ready.sem, 1)
                assert n[0] == ROUTE

            def experts(ph):
                def low(i, s):
                    g, k = ph["e"] + i, s % 2
                    dve.wait_ge(e_high.sem, e_high.done(g))
                    dve.tensor_tensor(flat(xt_l[:, k]), bank[k][:], flat(xt_h[:, k]).bitcast(F32), ALU.subtract)\
                        .then_inc(e_low.sem, 1)

                def hidden(i, s):
                    g, k = ph["e"] + i, s % 2
                    gu = bank[2 + k][:].rearrange("p (t m n) -> p t m n", t=2, m=2)
                    t_ = th[:, k].rearrange("p (t n) -> p t n", t=2)
                    dve.wait_ge(e_tanh.sem, e_tanh.done(g))
                    dve.scalar_tensor_tensor(t_, t_, 1.0, gu[:, :, 0, :], ALU.add, ALU.mult).then_inc(e_hid.sem, 1)
                    dve.wait_ge(e_hid.sem, e_hid.done(g, 1))
                    dve.wait_ge(e_htr.sem, e_htr.freed(g, 2))
                    dve.tensor_tensor(hid[:, k].rearrange("p (t n) -> p t n", t=2), t_, gu[:, :, 1, :], ALU.mult)\
                        .then_inc(e_hid.sem, 1)

                def turned(i, s):
                    g, k = ph["e"] + i, s % 2
                    dve.wait_ge(e_htr.sem, e_htr.done(g))
                    dve.wait_ge(e_dn.sem, e_dn.freed(g, 2))
                    dve.tensor_copy(ht[:, k], bank[4 + k][:, 0:2 * P]).then_inc(e_ht.sem, 1)

                steps(dve, EP, [(0, low), (1, hidden), (2, turned)])

            def combine(ph):
                par = ph["par"]

                def step(i, s):
                    g = ph["c"] + i
                    dve.wait_ge(rows_in[s].sem, used(ph, i, s))
                    dve.wait_ge(gathered[s % 2].sem, (g - s % 2) * 32 + 64)
                    for t in range(2):
                        dve.scalar_tensor_tensor(rows[:, s, t, :], gath[:, s % 2, t, 0, :],
                                                 wts[:, par, 0, ds(2 * i + t, 1)], rows[:, s, t, :],
                                                 ALU.mult, ALU.add).then_inc(c_out.sem, 1)
                    dve.wait_ge(outs_stored[s].sem, used(ph, i, s) - 16)
                    for t in range(2):
                        dve.wait_ge(c_out.sem, c_out.done(g, 1 + t))
                        dve.scalar_tensor_tensor(outs[:, s, t, :], gath[:, s % 2, t, 1, :],
                                                 wts[:, par, 1, ds(2 * i + t, 1)], rows[:, s, t, :],
                                                 ALU.mult, ALU.add).then_inc(c_out.sem, 1)

                steps(dve, PB, [(0, step)])

            def attention(ph):
                for i in range(PB):
                    a, b = ph["a"] + i, ph["a"] // PB
                    x, g = a - b - 1, ph["ln"] + i
                    s = i % NS
                    dve.wait_ge(rows_in[s].sem, used(ph, i, s))
                    for t in range(2):
                        dve.bn_stats(bst[:, s % 2, t, :], rows[:, s, t, :]).then_inc(ln_stats.sem, 1)
                    dve.wait_ge(ln_stats.sem, ln_stats.done(g))
                    dve.wait_ge(a_otr.sem, a_otr.freed(a, 1))
                    layer_norm(g, s % 2, lambda t: rows[:, s, t, :], lambda t: xa[:, t, :])
                    dve.wait_ge(a_high.sem, a_high.done(a))
                    if i == 0:
                        dve.wait_ge(s_xf.sem, s_xf.done(b))
                    dve.tensor_tensor(flat(xt_l[:, 0]), bank[0][:], flat(xt_h[:, 0]).bitcast(F32), ALU.subtract)\
                        .then_inc(a_low.sem, 1)
                    dve.wait_ge(a_qh.sem, a_qh.done(a))
                    if i == 0:
                        for m in range(2):
                            dve.scalar_tensor_tensor(flat(q_l[:, m]), bank[1][:], parity[:, m:m + 1],
                                                     flat(q_h[:, m]).bitcast(F32), ALU.mult, ALU.subtract)\
                                .then_inc(a_ql.sem, 1)
                        dve.wait_ge(s_kh.sem, s_kh.done(b))
                        dve.tensor_tensor(flat(k_l[:]), bank[2][:], flat(k_h[:]).bitcast(F32), ALU.subtract)\
                            .then_inc(s_kl.sem, 1)
                        dve.wait_ge(s_hc.sem, s_hc.done(b))
                        dve.tensor_reduce(hm[:], hc[:].rearrange("p (n r) -> p n r", r=CTX // CK), AX.X, ALU.add)\
                            .then_inc(s_hm.sem, 1)
                        dve.wait_ge(s_ckh.sem, s_ckh.done(b))
                        keys = bank[6][:, 0:KC * CK].rearrange("p (k n) -> p k n", k=KC)
                        for m in range(2):
                            ins = dve.scalar_tensor_tensor(kc_l[:, :, m * CK:(m + 1) * CK], keys, parity[:, m:m + 1],
                                                           kc_h[:, :, m * CK:(m + 1) * CK].bitcast(F32),
                                                           ALU.mult, ALU.subtract)
                        ins.then_inc(s_ckl.sem, 1)
                        dve.wait_ge(a_mtr.sem, a_mtr.freed(a, 1))
                        for n in range(12):
                            t, w = (0, 4) if n < 4 else (1, 2)
                            h0 = 4 * (n % 4) + (2 * (n // 8))
                            dve.wait_ge(s_sm.sem, s_sm.done(b, n + 1))
                            dve.tensor_reduce(mx[:, t, h0:h0 + w], bank[n % 4][:].rearrange("p (h k) -> p h k", h=w),
                                              AX.X, ALU.max).then_inc(s_mx.sem, 1)
                    else:
                        dve.tensor_tensor(flat(q_l[:, 0]), bank[1][:], flat(q_h[:, 0]).bitcast(F32), ALU.subtract)\
                            .then_inc(a_ql.sem, 2)
                        dve.wait_ge(a_mtr.sem, a_mtr.freed(a, 1))
                        for n in range(4):
                            dve.wait_ge(x_sm.sem, x_sm.done(x, n + 1))
                            dve.tensor_reduce(mx[:, :, 4 * n:4 * n + 4],
                                              bank[2 + n][:].rearrange("p (t h k) -> p t h k", t=2, h=4),
                                              AX.X, ALU.max).then_inc(x_mx.sem, 1)
                    dve.wait_ge(a_pv.sem, a_pv.done(a))
                    for t in range(2):
                        o = bank[6 + t][:, 0:H * (HD + 1)].rearrange("p (h d) -> p h d", d=HD + 1)
                        dve.reciprocal(rden[:, t, :], o[:, :, HD]).then_inc(a_den.sem, 1)
                        dve.wait_ge(a_den.sem, a_den.done(a, t + 1))
                        dve.tensor_tensor(xa[:, t, :].rearrange("p (h d) -> p h d", d=HD), o[:, :, 0:HD],
                                          rden[:, t, :].unsqueeze(2).broadcast_to([P, H, HD]), ALU.mult)\
                            .then_inc(a_norm.sem, 1)
                    dve.wait_ge(a_wo.sem, a_wo.done(a))
                    dve.wait_ge(outs_stored[s].sem, used(ph, i, s) - 16)
                    dve.tensor_tensor(flat(outs[:, s]), bank[1][:], flat(rows[:, s]), ALU.add).then_inc(a_out.sem, 1)

            dve.wait_ge(gp_step.sem, GP_STEPS)
            dve.tensor_reduce(parity[:, 0:1], cmask[:], AX.X, ALU.add).then_inc(parity_step.sem, 1)
            dve.wait_ge(parity_step.sem, 1)
            dve.tensor_scalar(parity[:, 1:2], parity[:, 0:1], -1.0, 1.0, ALU.mult, ALU.add).then_inc(parity_step.sem, 1)

            for ph in phases:
                fence(dve, "dve", ph["n"])
                {"T": tokens, "E": experts, "C": combine, "A": attention}[ph["kind"]](ph)
                dve.drain().then_inc(phase_done["dve"].sem, 1)

        @block.tensor
        def _(pe):
            for sig in (tr_pe, logits_pe, gu_pe, dn_pe, e_tr, e_gu, e_htr, e_dn, a_tr, a_q, a_mtr, a_pv, a_otr,
                        a_wo, x_sm, x_st, x_pv, s_kv, s_h, s_cp, s_ckv, s_sm, s_st, s_pv):
                pe.sem_inc(sig.sem, sig.head * sig.per)
            pe.wait_ge(gp_step.sem, GP_STEPS)
            pe.wait_ge(consts.sem, 1)

            def turn_pair(src, b, last_sem):
                for k in range(KC):
                    for t in range(2):
                        m = pe.transpose(bank[b][:, (2 * k + t) * P:(2 * k + t + 1) * P], src(t, k), ident[:])
                m.then_inc(last_sem, 1)

            def three(out_, lh, ll, rh, rl, first, last):
                pe.matmul(out_, lh, rh, start=first, stop=False)
                pe.matmul(out_, lh, rl, start=False, stop=False)
                return pe.matmul(out_, ll, rh, start=False, stop=last)

            def tokens(ph):
                par = ph["par"]

                def turn(i, s):
                    g, k = ph["t"] + i, s % 2
                    pe.wait_ge(ln_rows.sem, ln_rows.done(ph["ln"] + i))
                    pe.wait_ge(tr_low.sem, tr_low.freed(g, 2))
                    turn_pair(lambda t, c: xn[:, par, ds(2 * i + t, 1), c * P:(c + 1) * P].rearrange("p a d -> p (a d)"),
                              k, tr_pe.sem)

                def gate_up(i, s):
                    g, k = ph["t"] + i, s % 2
                    pe.wait_ge(tr_low.sem, tr_low.done(g))
                    if isinstance(i, int) and i == 0:
                        pe.wait_ge(raw_split.sem, raw_split.done(1))
                        pe.wait_ge(router_split.sem, 2)
                        pe.wait_ge(weights_in.sem, 16 * 3)
                    pe.wait_ge(logits_dve.sem, logits_dve.freed(g, 1))
                    for t in range(2):
                        for c in range(KC):
                            m = three(bank[4][:, t * NE:(t + 1) * NE],
                                      xt_h[:, k, c, t * P:(t + 1) * P], xt_l[:, k, c, t * P:(t + 1) * P],
                                      rw_h[:, c, :], rw_l[:, c, :], c == 0, c == KC - 1)
                    m.then_inc(logits_pe.sem, 1)
                    pe.wait_ge(gu_hid.sem, gu_hid.freed(g, 1))
                    for m_ in range(2):
                        for h in range(SH // P):
                            for c in range(KC):
                                m = three(bank[2 + m_][:, h * 2 * P:(h + 1) * 2 * P],
                                          sg_h[:, m_, c, h * P:(h + 1) * P], sg_l[:, m_, c, h * P:(h + 1) * P],
                                          xt_h[:, k, c, :], xt_l[:, k, c, :], c == 0, c == KC - 1)
                    m.then_inc(gu_pe.sem, 1)

                def down_(i, s):
                    g = ph["t"] + i
                    pe.wait_ge(gu_hid.sem, gu_hid.done(g))
                    pe.wait_ge(t_out.sem, t_out.freed(g, 2))
                    for t in range(2):
                        for h in range(SH // P):
                            m = pe.matmul(bank[6 + s % 2][:, t * D:(t + 1) * D], hid[:, h, t * P:(t + 1) * P],
                                          sd[:, h, :], start=h == 0, stop=h == SH // P - 1)
                    m.then_inc(dn_pe.sem, 1)

                steps(pe, PB, [(1, turn), (3, down_), (2, gate_up)])
                pe.wait_ge(route.sem, ph["r"] * ROUTE + ROUTE_PICKED)
                pe.matmul(bank[4][:, 0:NE * TB], below[:], flat(picked[:]), start=True, stop=True)
                pe.matmul(bank[4][:, NE * TB:2 * NE * TB], ones_b[:], flat(picked[:]), start=True, stop=True)\
                    .then_inc(route_pe.sem, 1)

            def experts(ph):
                par = ph["par"]
                pe.wait_ge(table_ready.sem, ph["r"] + 1)
                if ph["r"] == 0:
                    pe.wait_ge(raw_split.sem, raw_split.done(NE + 1))
                    pe.wait_ge(weights_in.sem, 16 * 4)

                def experts_of(i):
                    return nc.values_load_multi_w_load_instructions(
                        table[0:1, par, ds(2 * i, 2)], engines=[mybir.EngineType.PE], min_val=0, max_val=NE - 1)[1]

                def turn(i, s):
                    g, k = ph["e"] + i, s % 2
                    pe.wait_ge(rows_in[s].sem, used(ph, i, s))
                    pe.wait_ge(e_low.sem, e_low.freed(g, 2))
                    turn_pair(lambda t, c: rows[:, s, t, c * P:(c + 1) * P], k, e_tr.sem)

                def gate_up(i, s):
                    g, k = ph["e"] + i, s % 2
                    mine = experts_of(i)
                    pe.wait_ge(e_low.sem, e_low.done(g))
                    pe.wait_ge(e_hid.sem, e_hid.freed(g, 2))
                    for t, e in enumerate(mine):
                        wh = eg_h[:, ds(e, 1)].rearrange("p a k n -> p (a k) n")
                        wl = eg_l[:, ds(e, 1)].rearrange("p a k n -> p (a k) n")
                        for c in range(KC):
                            m = three(bank[2 + k][:, t * 2 * EH:(t + 1) * 2 * EH],
                                      xt_h[:, k, c, t * P:(t + 1) * P], xt_l[:, k, c, t * P:(t + 1) * P],
                                      wh[:, c, :], wl[:, c, :], c == 0, c == KC - 1)
                    m.then_inc(e_gu.sem, 1)

                def turn_hidden(i, s):
                    g, k = ph["e"] + i, s % 2
                    pe.wait_ge(e_hid.sem, e_hid.done(g))
                    pe.wait_ge(e_ht.sem, e_ht.freed(g, 2))
                    for t in range(2):
                        m = pe.transpose(bank[4 + k][:, t * P:(t + 1) * P], hid[:, k, t * P:(t + 1) * P], ident[:])
                    m.then_inc(e_htr.sem, 1)

                def down_(i, s):
                    g, k = ph["e"] + i, s % 2
                    mine = experts_of(i)
                    pe.wait_ge(e_ht.sem, e_ht.done(g))
                    pe.wait_ge(e_out.sem, e_out.freed(g, 2))
                    for t, e in enumerate(mine):
                        m = pe.matmul(bank[6 + k][:, t * D:(t + 1) * D], ht[:, k, t * P:(t + 1) * P],
                                      ed[:, ds(e, 1), :].rearrange("p a d -> p (a d)"), start=True, stop=True)
                    m.then_inc(e_dn.sem, 1)

                steps(pe, EP, [(0, turn), (2, turn_hidden), (1, gate_up), (3, down_)])

            def attention(ph):
                if ph["a"] == 0:
                    pe.wait_ge(attn_in.sem, 16 * 8)
                    pe.wait_ge(raw_split.sem, raw_split.done(NE + 2))
                    pe.wait_ge(parity_step.sem, 2)
                for i in range(PB):
                    a, b = ph["a"] + i, ph["a"] // PB
                    x = a - b - 1
                    pe.wait_ge(ln_rows.sem, ln_rows.done(ph["ln"] + i))
                    pe.wait_ge(a_ot.sem, a_ot.freed(a, 1))
                    turn_pair(lambda t, c: xa[:, t, c * P:(c + 1) * P], 0, a_tr.sem)
                    pe.wait_ge(a_low.sem, a_low.done(a))
                    pe.wait_ge(a_out.sem, a_out.freed(a, 1))
                    for c in range(KC):
                        for k in range(KC):
                            m = three(bank[1][:, c * 2 * P:(c + 1) * 2 * P],
                                      wq_h[:, k, c * P:(c + 1) * P], wq_l[:, k, c * P:(c + 1) * P],
                                      xt_h[:, 0, k, :], xt_l[:, 0, k, :], k == 0, k == KC - 1)
                    m.then_inc(a_q.sem, 1)
                    if i == 0:
                        context(b)
                        self_scores(a, b)
                    else:
                        cross_scores(a, x)
                    pe.wait_ge(a_norm.sem, a_norm.done(a))
                    turn_pair(lambda t, c: xa[:, t, c * P:(c + 1) * P], 0, a_otr.sem)
                    pe.wait_ge(a_ot.sem, a_ot.done(a))
                    for t in range(2):
                        for k in range(KC):
                            m = pe.matmul(bank[1][:, t * D:(t + 1) * D], xt_f[:, k, t * P:(t + 1) * P], wo_s[:, k, :],
                                          start=k == 0, stop=k == KC - 1)
                    m.then_inc(a_wo.sem, 1)

            def context(b):
                pe.wait_ge(s_xf.sem, s_xf.done(b))
                for c in range(KC):
                    for k in range(KC):
                        m = pe.matmul(bank[2][:, c * CTX:(c + 1) * CTX], wk_s[:, k, c * P:(c + 1) * P], xf[:, k, :],
                                      start=k == 0, stop=k == KC - 1)
                m.then_inc(s_kv.sem, 1)
                for t in range(2):
                    for k in range(KC):
                        m = pe.matmul(bank[3][:, t * D:(t + 1) * D], xf[:, k, t * P:(t + 1) * P], wv_s[:, k, :],
                                      start=k == 0, stop=k == KC - 1)
                m.then_inc(s_kv.sem, 1)
                for k in range(KC):
                    m = pe.matmul(bank[4][:, 0:CTX], w1_s[:, k, :], xf[:, k, :], start=k == 0, stop=k == KC - 1)
                m.then_inc(s_h.sem, 1)
                pe.wait_ge(s_hm.sem, s_hm.done(b))
                for k in range(KC):
                    m = pe.matmul(bank[5][:, k * CK:(k + 1) * CK], w2_s[:, k * P:(k + 1) * P], hm[:],
                                  start=True, stop=True)
                m.then_inc(s_cp.sem, 1)
                pe.wait_ge(s_cm.sem, s_cm.done(b))
                for c in range(KC):
                    for k in range(KC):
                        m = pe.matmul(bank[6][:, c * CK:(c + 1) * CK], wk_s[:, k, c * P:(c + 1) * P], cm[:, k, 0, :],
                                      start=k == 0, stop=k == KC - 1)
                m.then_inc(s_ckv.sem, 1)
                for k in range(KC):
                    m = pe.matmul(bank[7][:, 0:D], flat(cm[:, k]), wv_s[:, k, :], start=k == 0, stop=k == KC - 1)
                m.then_inc(s_ckv.sem, 1)

            def turn_maxima(a):
                for t in range(2):
                    m = pe.transpose(bank[MT_BANK][:, t * P:(t + 1) * P], mx[:, t, :], ident[:])
                m.then_inc(a_mtr.sem, 1)

            def minus_max(out_, heads, cols, last):
                h, n = heads
                w = minus[:, h * CK:(h + n) * CK] if n > 1 else minus[:, h * CK:h * CK + 1].broadcast_to([P, P])
                return pe.matmul(out_, w, mt[:, cols[0]:cols[1]], start=False, stop=last)

            def self_scores(a, b):
                pe.wait_ge(a_ql.sem, a_ql.done(a))
                pe.wait_ge(s_kl.sem, s_kl.done(b))
                pe.wait_ge(s_va.sem, s_va.done(b))
                for n in range(12):
                    g, t = n % 4, int(n >= 4)
                    r = slice(32 * g, 32 * g + 32)
                    if n >= 4:
                        pe.wait_ge(s_mx.sem, s_mx.done(b, n - 3))
                    heads = [(c, m_) for c in range(2) for m_ in range(2)] if t == 0 else [(n // 4 - 1, m_) for m_ in range(2)]
                    keys = (t + 1) * P
                    for j, (c, m_) in enumerate(heads):
                        out_ = bank[n % 4][:, j * keys:(j + 1) * keys]
                        pe.matmul(out_, q_h[r, m_, c, t * P:(t + 1) * P], k_h[r, c, 0:keys], start=True, stop=False)
                        m = pe.matmul(out_[:, t * P:keys], ident_b[:], mask_q[:], start=False, stop=True)
                    m.then_inc(s_sm.sem, 1)
                pe.wait_ge(s_mx.sem, s_mx.done(b))
                turn_maxima(a)
                pe.wait_ge(a_mt.sem, a_mt.done(a))

                def values(n):
                    pe.wait_ge(s_exp.sem, s_exp.done(b, n + 1))
                    h = head_at(n % 4, n // 8, n // 4 % 2)
                    p_ = pt[:, n % 2, :]
                    o = slice(h * (HD + 1), (h + 1) * (HD + 1))
                    pe.matmul(bank[6][:, o], p_[:, 0:P], va[:, 0, h, :], start=True, stop=True)
                    pe.matmul(bank[7][:, o], p_[:, P:2 * P], va[:, 0, h, :], start=True, stop=False)
                    pe.matmul(bank[7][:, o], p_[:, 2 * P:3 * P], va[:, 1, h, :], start=False, stop=True)\
                        .then_inc(s_pv.sem, 1)

                for n in range(H):
                    g, c, m_ = n % 4, n // 8, n // 4 % 2
                    r = slice(32 * g, 32 * g + 32)
                    if n >= 4:
                        pe.wait_ge(s_exp.sem, s_exp.done(b, n - 3))
                    for t, cols, out_ in ((0, (0, 2 * P), bank[g][:, 0:2 * P]), (1, (P, 2 * P), bank[g][:, 2 * P:3 * P])):
                        three(out_, k_h[r, c, t * P:(t + 1) * P], k_l[r, c, t * P:(t + 1) * P],
                              q_h[r, m_, c, cols[0]:cols[1]], q_l[r, m_, c, cols[0]:cols[1]], True, False)
                        minus_max(out_, (4 * g + 2 * c + m_, 1), cols, False)
                        m = pe.matmul(out_[:, 0:P], ident_b[:], mask_k[:], start=False, stop=True)
                    m.then_inc(s_st.sem, 1)
                    if n:
                        values(n - 1)
                values(H - 1)
                pe.drain().then_inc(a_pv.sem, 2)

            def cross_scores(a, x):
                pe.wait_ge(a_ql.sem, a_ql.done(a))
                if a % PB == 1:
                    pe.wait_ge(s_ckl.sem, s_ckl.done(a // PB))
                    pe.wait_ge(s_vc.sem, s_vc.done(a // PB))
                for g in range(4):
                    r = slice(32 * g, 32 * g + 32)
                    for t in range(2):
                        for c in range(2):
                            m = pe.matmul(bank[2 + g][:, (2 * t + c) * P:(2 * t + c + 1) * P],
                                          q_h[r, 0, c, t * P:(t + 1) * P], kc_h[r, c, :], start=True, stop=True)
                    m.then_inc(x_sm.sem, 1)
                pe.wait_ge(x_mx.sem, x_mx.done(x))
                turn_maxima(a)
                pe.wait_ge(a_mt.sem, a_mt.done(a))

                def values(n):
                    pe.wait_ge(x_exp.sem, x_exp.done(x, n + 1))
                    for j in range(2):
                        g = 4 * j + n
                        o = slice(g * 2 * (HD + 1), (g + 1) * 2 * (HD + 1))
                        for t in range(2):
                            m = pe.matmul(bank[6 + t][:, o], pt[:, n % 2, (2 * j + t) * P:(2 * j + t + 1) * P],
                                          flat(vc[:, g]), start=True, stop=True)
                    m.then_inc(x_pv.sem, 1)

                for n in range(4):
                    for c in range(2):
                        r = slice(32 * n, 32 * n + 32)
                        out_ = bank[2 + n][:, c * 2 * P:(c + 1) * 2 * P]
                        three(out_, kc_h[r, c, :], kc_l[r, c, :], q_h[r, 0, c, :], q_l[r, 0, c, :], True, False)
                        m = minus_max(out_, (4 * n + 2 * c, 2), (0, 2 * P), True)
                    m.then_inc(x_st.sem, 1)
                    if n:
                        values(n - 1)
                values(3)
                pe.drain().then_inc(a_pv.sem, 2)

            for ph in phases:
                fence(pe, "pe", ph["n"])
                {"T": tokens, "E": experts, "C": lambda ph: None, "A": attention}[ph["kind"]](ph)
                pe.drain().then_inc(phase_done["pe"].sem, 1)


def head_at(group, chunk, odd):
    return 8 * chunk + 2 * group + odd


def flat(a):
    n = len(a.shape)
    if n == 2:
        return a
    names = " ".join("abcd"[:n - 1])
    return a.rearrange(f"p {names} -> p ({names})")


MT_BANK = 4

ROUTE_D = 2 * TB + 1
ROUTE_PICKED = 2 * TB + 5
ROUTE = 2 * TB + 5 + 20
GP_STEPS = 24

PLAN = [(kind, layer, b0 + b) for b0 in range(0, B, 2)
        for kind, layer, b in (("T", 0, 0), ("T", 0, 1), ("E", 0, 0), ("E", 0, 1), ("C", 0, 0), ("A", 0, 0), ("T", 1, 0),
                               ("C", 0, 1), ("A", 0, 1), ("T", 1, 1), ("E", 1, 0), ("E", 1, 1), ("C", 1, 0), ("C", 1, 1))]

_INS = ["L0_attn_hidden_states", "L0_attn_Wq", "L0_attn_Wk", "L0_attn_Wv", "L0_attn_Wo", "L0_attn_W1", "L0_attn_b1",
        "L0_attn_W2", "L0_attn_b2", "L0_ffn_router_w", "L0_ffn_router_bias", "L0_ffn_up_proj", "L0_ffn_gate_proj",
        "L0_ffn_down_proj", "L0_ffn_sh_gate", "L0_ffn_sh_up", "L0_ffn_sh_down"]
_TURNED = {"L0_ffn_router_w", "L0_ffn_sh_gate", "L0_ffn_sh_up", "L0_ffn_sh_down"}


def kernel(**inputs):
    import numpy as _np
    import concourse.bacc as _bacc
    from concourse.bass_utils import run_bass_kernel_spmd as _run

    nc = _bacc.Bacc("TRN2", target_bir_lowering=False, num_devices=1)
    arrays, args = {}, []
    for name in _INS:
        a = _np.ascontiguousarray(inputs[name].T if name in _TURNED else inputs[name])
        arrays[f"in_{name}"] = a
        args.append(nc.dram_tensor(f"in_{name}", a.shape, mybir.dt.from_np(a.dtype), kind="ExternalInput").ap())
    out = nc.dram_tensor("out", inputs[_INS[0]].shape, F32, kind="ExternalOutput").ap()
    macaron_kernel(nc, *args, out, PLAN)
    r = _run(nc, [arrays], core_ids=[0])
    return r.results[0]["out"]
```

```python
from contextlib import ExitStack

import concourse.bass as bass
from concourse import mybir

F32 = mybir.dt.float32
F32R = mybir.dt.float32r
BF16 = mybir.dt.bfloat16
I32 = mybir.dt.int32
U32 = mybir.dt.uint32
ALU = mybir.AluOpType
ACT = mybir.ActivationFunctionType
AX = mybir.AxisListType
ds = bass.ds

P = 128
B, S, D = 4, 2048, 256
KC = D // P
NE = 16
EH = 128
SH = 256
TB = S // P
PB = TB // 2
ET = 2 * S // P + NE
EP = ET // 2
H, HD = 16, 16
CTX = 256
CK = 64
EPS = 1e-5
SCALE = HD ** -0.5
MASKED = -1.0e30
RSQRT_GUESS = float(0x5F3759DF)
NEWTON = 3
ROUND = 8388608.0
LN_STEPS = 8 + 3 * NEWTON
NS = 4


class Signal:

    def __init__(self, sem, per=1, head=4):
        self.sem, self.per, self.head = sem, per, head

    def done(self, g, k=None):
        return (g + self.head) * self.per + (self.per if k is None else k)

    def freed(self, g, n):
        return (g - n + self.head + 1) * self.per


def steps(eng, n, todo, begin=None):
    last = max(lag for lag, _ in todo)
    head = (last + NS - 1) // NS * NS
    loops = (n - head) // NS

    def turn(i, r, inside):
        for lag, step in todo:
            if inside or 0 <= i - lag < n:
                step(i - lag, (r - lag) % NS)

    def ahead(i, inside):
        if begin:
            begin(i, inside)

    for i in range(head):
        if i % NS == 0:
            ahead(i, False)
        turn(i, i, False)
    if loops > 1:
        with eng.Fori(0, loops) as j:
            ahead(j * NS + head, True)
            for r in range(NS):
                turn(j * NS + (head + r), r, True)
    elif loops == 1:
        ahead(head, True)
        for r in range(NS):
            turn(head + r, r, True)
    if last:
        ahead(head + loops * NS, False)
    for i in range(head + loops * NS, n + last):
        turn(i, i, False)


def macaron_kernel(nc, x_in, wq, wk, wv, wo, w1, b1, w2, b2, rw_t, rbias, up, gate, down,
                   shg_t, shu_t, shd_t, out, plan, dbg=None):
    ctx = ExitStack()
    with ctx:
        def sb(name, shape, dt=F32):
            return ctx.enter_context(nc.sbuf_tensor(name, shape, dt))

        def signal(name, per=1, head=4):
            return Signal(ctx.enter_context(nc.semaphore(name)), per, head)

        xs = [nc.dram_tensor(f"slot_rows{i}", [ET * P, D], F32).ap() for i in range(2)]
        ys = [nc.dram_tensor(f"slot_results{i}", [ET * P, D], F32).ap() for i in range(2)]
        acc_d = nc.dram_tensor("partial_sums", [B * S, D], F32).ap()
        acc_v = acc_d.rearrange("(g t p) d -> g p t d", t=2, p=P)
        x_v = x_in.rearrange("b (g t p) d -> (b g) p t d", t=2, p=P)
        out_v = out.rearrange("b (g t p) d -> (b g) p t d", t=2, p=P)
        xs_v = [a.rearrange("(g t p) d -> g p t d", t=2, p=P) for a in xs]
        ys_v = [a.rearrange("(g t p) d -> g p t d", t=2, p=P) for a in ys]

        raw = sb("raw_weights", [P, 4, KC, 2 * EH])
        eg_h = sb("expert_gate_up_high", [P, NE, KC, 2 * EH], F32R)
        eg_l = sb("expert_gate_up_low", [P, NE, KC, 2 * EH], F32R)
        ed = sb("expert_down", [P, NE, D])
        sg_h = sb("shared_gate_up_high", [P, 2, KC, SH], F32R)
        sg_l = sb("shared_gate_up_low", [P, 2, KC, SH], F32R)
        sd = sb("shared_down", [P, SH // P, D])
        rw_h = sb("router_high", [P, KC, NE], F32R)
        rw_l = sb("router_low", [P, KC, NE], F32R)
        rb = sb("router_bias", [P, NE])
        wq_h = sb("wq_high", [P, KC, D], F32R)
        wq_l = sb("wq_low", [P, KC, D], F32R)
        wk_s = sb("wk", [P, KC, D])
        wv_s = sb("wv", [P, KC, D])
        wo_s = sb("wo", [P, KC, D])
        w1_s = sb("w1", [P, KC, P])
        w2_s = sb("w2", [P, D])
        b1_s = sb("b1", [P, 1])
        b2_s = sb("b2", [P, KC])
        ident = sb("identity", [P, P])
        ones_f = sb("ones", [P, NE])
        below = sb("strictly_below", [P, P], BF16)
        ones_b = sb("ones_bf16", [P, P], BF16)
        iota_f = sb("iota", [P, ET])
        restart = sb("restart", [P, NE, TB])
        ident_b = sb("identity_bf16", [P, P], BF16)
        mask_q = sb("mask_query_key", [P, P], BF16)
        mask_k = sb("mask_key_query", [P, P], BF16)
        minus = sb("minus_by_head", [P, H * CK], F32R)
        parity = sb("head_parity", [P, 2])
        ring = sb("rows_and_results", [P, 2 * NS, 2, D])
        rows, outs = ring[:, 0:NS], ring[:, NS:2 * NS]
        xn = sb("normalised_rows", [P, 2, TB, D])
        xt_h = sb("rows_transposed_high", [P, 2, KC, 2 * P], F32R)
        xt_l = sb("rows_transposed_low", [P, 2, KC, 2 * P], F32R)
        work = sb("hidden_work", [P, 3, 2, 2 * P])
        th, hid, ht = work[:, 0], work[:, 1], work[:, 2]
        gath = [xn[:, par, 0:8, :].rearrange("p (s t k) d -> p s t k d", s=2, t=2) for par in range(2)]
        pt = raw.rearrange("p a b c -> p a (b c)")
        xf = raw[:, 3]
        xln = work[:, 1:3].rearrange("p k a b -> p k (a b)").rearrange("p k (t d) -> p k t d", t=2)
        xa = [xn[:, par, 8:16, :].rearrange("p (s t) d -> p s t d", s=NS) for par in range(2)]
        xt_f = work[:, 0].rearrange("p a b -> p (a b)").rearrange("p (c n) -> p c n", c=KC)
        q_h = sb("queries_high", [P, 2, KC, 2 * P], F32R)
        q_l = sb("queries_low", [P, 2, KC, 2 * P], F32R)
        k_h = sb("keys_high", [P, KC, CTX], F32R)
        k_l = sb("keys_low", [P, KC, CTX], F32R)
        kc_h = sb("compressed_keys_high", [P, KC, 2 * CK], F32R)
        kc_l = sb("compressed_keys_low", [P, KC, 2 * CK], F32R)
        va = sb("values", [P, 2, H // 2, 2, 2, HD])
        sumk = sb("ones_by_head", [P, 2, 2 * HD])
        vc = sb("compressed_values", [P, H // 2, 2, HD])
        sumc = sb("ones_by_compressed_head", [P, 2, HD])
        hc = sb("compress_hidden", [P, CTX])
        zeros = hc
        hm = sb("compress_hidden_sums", [P, CK])
        iota_i = hm[:, 0:ET].bitcast(I32)
        cm = sb("compressed_transposed", [P, KC, 2, CK])
        rw = cm[:, :, 0, 0:NE]
        mx = sb("score_maxima", [P, 2, P])
        mt = sb("score_maxima_transposed", [P, 2 * P], F32R)
        bst = sb("bn_stats", [P, PB, 2, 6])
        lnd = sb("mean_difference", [P, PB, 2])
        lnm = sb("mean", [P, PB, 2])
        lnv = sb("variance", [P, PB, 2])
        lnw = sb("variance_of_halves", [P, PB, 2])
        rstd = sb("rstd", [P, PB, 2])
        lnb = sb("minus_mean_by_deviation", [P, PB, 2])
        rsq = sb("rsqrt_steps", [P, PB, 2])
        logits = sb("logits", [P, TB, NE])
        cmask = flat(logits[:])[:, 0:P]
        top = sb("top_values", [P, TB, 8])
        topi = sb("top_indices", [P, TB, 8], U32)
        topf = sb("top_indices_float", [P, 2, TB])
        route_work = work.rearrange("p a b c -> p (a b c)")
        onehot = route_work[:, 0:2 * NE * TB].rearrange("p (k e t) -> p k e t", k=2, e=NE)
        rank, tot, incl = (route_work[:, n * NE * TB:(n + 1) * NE * TB].rearrange("p (e t) -> p e t", e=NE) for n in (2, 3, 4))
        texp = route_work[0:1, ET * NE:ET * NE + ET]
        cmpb = route_work[0:1, 0:ET * NE].rearrange("p (t e) -> p t e", e=NE)
        picked = sb("picked", [P, NE, TB], BF16)
        tiles_of = sb("tiles_of_expert", [P, NE])
        tiles_in = sb("tiles_up_to_expert", [P, NE])
        base = sb("first_tile_of_expert", [P, NE])
        slotf = sb("slot_float", [P, 2, TB])
        slot = sb("slot", [P, 2, 2, TB], U32)
        wexp = sb("weight_exp", [P, 3, TB])
        wts = sb("weights", [P, 2, 2, TB])
        table = sb("expert_of_tile", [1, 2, ET], I32)

        bank = [ctx.enter_context(nc.psum_tensor(f"bank{i}", [P, 512], F32)) for i in range(8)]

        weights_in = signal("weights_in", 16, 0)
        raw_in = [signal(f"raw_in{i}", 16, 0) for i in range(4)]
        raw_split = signal("raw_split", 2, 4)
        router_split = signal("router_split", 2, 0)
        consts = signal("constants_ready", 1, 0)
        gp_step = signal("gpsimd_constant_steps", 1, 0)
        xs_zeroed = signal("slot_rows_zeroed", 16, 0)
        phase_done = {e: signal(f"phase_done_{e}", 1, 0) for e in ("pe", "act", "dve")}
        rows_in = [signal(f"rows_in{i}", 16, 0) for i in range(NS)]
        token_in = [signal(f"token_rows_in{i}", 16, 0) for i in range(PB)]
        token_stored = [signal(f"token_sums_stored{i}", 16, 0) for i in range(PB)]
        outs_stored = [signal(f"results_stored{i}", 16, 0) for i in range(NS)]
        ln_stats = signal("ln_stats", 2)
        ln_small = signal("ln_small_steps", LN_STEPS)
        ln_rows = signal("ln_rows_normalised", 2)
        tr_pe = signal("rows_transposed")
        tr_high = signal("transposed_high_split")
        tr_low = signal("transposed_low_split")
        logits_pe = signal("logits_multiplied")
        logits_dve = signal("logits_biased")
        gu_pe = signal("shared_gate_up_multiplied", 2)
        gu_tanh = signal("shared_tanh", 2)
        gu_hid = signal("shared_hidden", 4)
        dn_pe = signal("shared_down_multiplied")
        t_out = signal("token_sums_ready")
        route = signal("route_steps", 1, 0)
        route_pe = signal("ranks_counted", 1, 0)
        route_act = signal("route_exp", 1, 0)
        routed = signal("slots_ready", 1, 0)
        table_ready = signal("expert_table_ready", 1, 0)
        scattered = [signal(f"scattered{i}", 16 * 2 * TB, 0) for i in range(2)]
        gathered = [signal(f"gathered{i}", 64, 0) for i in range(2)]
        e_tr = signal("slot_rows_transposed")
        e_high = signal("slot_high_split")
        e_low = signal("slot_low_split")
        e_gu = signal("expert_gate_up_multiplied")
        e_tanh = signal("expert_tanh")
        e_hid = signal("expert_hidden", 2)
        e_htr = signal("expert_hidden_transposed")
        e_ht = signal("expert_hidden_evacuated")
        e_dn = signal("expert_down_multiplied")
        e_out = signal("expert_rows_ready")
        c_out = signal("combined_rows", 4)
        a_tr = signal("attention_rows_transposed")
        a_high = signal("attention_high_split")
        a_low = signal("attention_low_split")
        a_q = signal("queries_multiplied")
        a_qh = signal("queries_high_split", 2)
        a_ql = signal("queries_low_split", 2)
        a_mtr = signal("maxima_transposed")
        a_mt = signal("maxima_evacuated")
        a_den = signal("sums_inverted")
        a_norm = signal("heads_normalised")
        a_wo = signal("output_multiplied")
        a_out = signal("attention_sums_ready")
        x_sm = signal("cross_scores", 4)
        x_mx = signal("cross_maxima", 4)
        x_st = signal("cross_scores_transposed", 4)
        x_exp = signal("cross_exp", 4)
        x_pv = signal("cross_values_steps", 4)
        s_xf = signal("context_evacuated")
        s_kv = signal("context_keys_values_multiplied", 2)
        s_kh = signal("context_keys_high")
        s_kl = signal("context_keys_low")
        s_va = signal("context_values_evacuated")
        s_h = signal("compress_hidden_multiplied")
        s_hc = signal("compress_relu")
        s_hm = signal("compress_summed")
        s_cp = signal("compress_multiplied")
        s_cm = signal("compressed_evacuated")
        s_ckv = signal("compressed_keys_values_multiplied", 2)
        s_ckh = signal("compressed_keys_high")
        s_ckl = signal("compressed_keys_low")
        s_vc = signal("compressed_values_evacuated")
        s_sm = signal("self_scores", 12)
        s_mx = signal("self_maxima", 12)
        s_st = signal("self_scores_transposed", H)
        s_exp = signal("self_exp", H)
        s_pv = signal("self_values_steps", H)
        attn_in = signal("attention_weights_in", 16, 0)
        parity_step = signal("head_parity_steps", 2, 0)

        count = {"T": 0, "E": 0, "C": 0, "R": 0, "A": 0}
        all_pairs = 0
        phases = []
        groups = 0
        for n, (kind, layer, b) in enumerate(plan):
            ph = {"kind": kind, "layer": layer, "b": b, "n": n, "ring": all_pairs, "par": b % 2}
            ph["ln"] = count["T"] + count["A"]
            ph["tokens_before"] = count["R"]
            if kind == "T":
                ph.update(t=count["T"], r=count["R"])
                count["T"] += PB
                count["R"] += 1
            elif kind == "E":
                ph.update(e=count["E"], r=sum(1 for k, l, c in plan[:n] if k == "E"))
                count["E"] += EP
                all_pairs += EP
            elif kind == "C":
                ph.update(c=count["C"])
                count["C"] += PB
                all_pairs += PB
            elif kind == "A":
                ph.update(a=count["A"], c=count["C"])
                count["C"] += PB
                count["A"] += PB
                all_pairs += PB
            ph["ln_groups"] = groups
            groups += {"T": 2, "A": PB // 2}.get(kind, 0)
            phases.append(ph)

        def fence(eng, me, n):
            for other in phase_done:
                if other != me and n:
                    eng.wait_ge(phase_done[other].sem, n)

        LN_GROUPS = {"T": ((0, 2), (2, PB)), "A": tuple((i, i + 2) for i in range(0, PB, 2))}

        def ln_group(ph, i):
            return ph["ln_groups"] + next(n for n, (a, b) in enumerate(LN_GROUPS[ph["kind"]]) if a <= i < b)

        block = ctx.enter_context(nc.Block())

        def used(ph, i, s):
            return (i - s + ph["ring"]) * (16 // NS) + 16

        @block.sync
        def _(sp):
            for m, w in enumerate((shg_t, shu_t)):
                sp.dma_start(raw[:, m, :, :], w.rearrange("(k p) h -> p k h", p=P)).then_inc(raw_in[m].sem, 16)
            sp.dma_start(rw, rw_t.rearrange("(k p) e -> p k e", p=P)).then_inc(weights_in.sem, 16)
            sp.dma_start(rb[:], rbias.rearrange("(a e) -> a e", a=1).broadcast_to([P, NE])).then_inc(weights_in.sem, 16)
            sp.dma_start(sd[:], shd_t.rearrange("(k p) d -> p k d", p=P)).then_inc(weights_in.sem, 16)

            for dst, src in ((wk_s, wk), (wv_s, wv), (wo_s, wo), (w1_s, w1)):
                sp.dma_start(dst[:], src.rearrange("(k p) n -> p k n", p=P)).then_inc(attn_in.sem, 16)
            sp.dma_start(w2_s[:], w2).then_inc(attn_in.sem, 16)
            sp.dma_start(b1_s[:], b1.rearrange("(p a) -> p a", a=1)).then_inc(attn_in.sem, 16)
            for k in range(KC):
                sp.dma_start(b2_s[:, k:k + 1], b2[k * P:(k + 1) * P].rearrange("(p a) -> p a", a=1))\
                    .then_inc(attn_in.sem, 16)

            def load(ph):
                src = acc_v
                first = ph["b"] * PB
                if ph["kind"] == "E":
                    src, first = xs_v[ph["par"]], 0

                def step(i, s):
                    if ph["kind"] == "E":
                        sp.wait_ge(e_tr.sem, e_tr.freed(ph["e"] + i, NS))
                    else:
                        sp.wait_ge(c_out.sem, c_out.freed(ph["c"] + i, NS))
                    sp.dma_start(rows[:, s, :, :], src[ds(first + i, 1)].rearrange("a p t d -> p (a t) d"))\
                        .then_inc(rows_in[s].sem, 16)
                return step

            def store(ph):
                dst = out_v if ph["kind"] == "C" else acc_v
                first = ph["b"] * PB
                if ph["kind"] == "E":
                    dst, first = ys_v[ph["par"]], 0

                def step(i, s):
                    if ph["kind"] == "E":
                        sp.wait_ge(e_out.sem, e_out.done(ph["e"] + i))
                    elif ph["kind"] == "A":
                        sp.wait_ge(a_out.sem, a_out.done(ph["a"] + i))
                    else:
                        sp.wait_ge(c_out.sem, c_out.done(ph["c"] + i))
                    sp.dma_start(dst[ds(first + i, 1)].rearrange("a p t d -> p (a t) d"), outs[:, s, :, :])\
                        .then_inc(outs_stored[s].sem, 16)
                return step

            def tokens(ph):
                src, first = acc_v if ph["layer"] else x_v, ph["b"] * PB
                for i in range(PB):
                    sp.dma_start(ring[:, i], src[first + i]).then_inc(token_in[i].sem, 16)
                for i in range(PB):
                    sp.wait_ge(t_out.sem, t_out.done(ph["t"] + i))
                    sp.dma_start(acc_v[ph["b"] * PB + i], ring[:, i]).then_inc(token_stored[i].sem, 16)

            experts_left = list(range(NE))

            def load_expert(e):
                k = e + 2
                sp.wait_ge(raw_split.sem, raw_split.freed(k, 4))
                for m, w in enumerate((gate, up)):
                    sp.dma_start(raw[:, k % 4, :, m * EH:(m + 1) * EH],
                                 w[e].rearrange("(k p) h -> p k h", p=P)).then_inc(raw_in[k % 4].sem, 16)

            for ph in phases:
                if ph["n"]:
                    for other in phase_done:
                        sp.wait_ge(phase_done[other].sem, ph["n"])
                if ph["kind"] == "E":
                    sp.wait_ge(scattered[ph["par"]].sem, 16 * 2 * TB * (ph["r"] // 2 + 1))
                for s in range(NS):
                    sp.wait_ge(outs_stored[s].sem, ph["ring"] * (16 // NS))
                for sig in token_stored:
                    sp.wait_ge(sig.sem, 16 * ph["tokens_before"])
                if ph["kind"] == "T":
                    tokens(ph)
                else:
                    steps(sp, EP if ph["kind"] == "E" else PB,
                          [(0, load(ph)), ({"E": 5, "C": 3, "A": 5}[ph["kind"]], store(ph))])
                if ph["n"] == 0:
                    for e in experts_left:
                        load_expert(e)
                    k = NE + 2
                    sp.wait_ge(raw_split.sem, raw_split.freed(k, 4))
                    sp.dma_start(raw[:, k % 4], wq.rearrange("(k p) n -> p k n", p=P)).then_inc(raw_in[k % 4].sem, 16)
                    sp.dma_start(ed[:], down.rearrange("e p d -> p e d")).then_inc(weights_in.sem, 16)
            for s in range(NS):
                sp.wait_ge(outs_stored[s].sem, all_pairs * (16 // NS))
            for sig in token_stored:
                sp.wait_ge(sig.sem, 16 * count["R"])

        @block.gpsimd
        def _(gp):
            def made(ins):
                ins.then_inc(gp_step.sem, 1)
                made.n += 1
                gp.wait_ge(gp_step.sem, made.n)
            made.n = 0
            gp.sem_inc(raw_split.sem, raw_split.head * raw_split.per)
            made(gp.memset(ident[:], 0.0))
            made(gp.affine_select(out=ident[:], in_=ident[:], compare_op=ALU.not_equal, fill=1.0, base=0,
                                  pattern=[[-1, P]], channel_multiplier=1))
            made(gp.memset(zeros[:], 0.0))
            gp.memset(ones_b[:], 1.0).then_inc(consts.sem, 1)
            made(gp.memset(ones_f[:], 1.0))
            made(gp.memset(below[:], 1.0))
            made(gp.affine_select(out=below[:], in_=below[:], compare_op=ALU.is_gt, fill=0.0, base=0,
                                  pattern=[[1, P]], channel_multiplier=-1))
            made(gp.memset(restart[:], 1.0))
            made(gp.memset(restart[:, :, 0:1], 0.0))
            made(gp.iota(iota_i, pattern=[[1, ET]], base=0, channel_multiplier=0))
            made(gp.tensor_copy(iota_f[:], iota_i))
            gp.memset(zeros[:], 0.0).then_inc(consts.sem, 1)
            made(gp.tensor_copy(ident_b[:], ident[:]))
            made(gp.memset(mask_q[:], MASKED))
            made(gp.affine_select(out=mask_q[:], in_=mask_q[:], compare_op=ALU.is_gt, fill=0.0, base=0,
                                  pattern=[[1, P]], channel_multiplier=-1))
            made(gp.memset(mask_k[:], MASKED))
            made(gp.affine_select(out=mask_k[:], in_=mask_k[:], compare_op=ALU.is_gt, fill=0.0, base=0,
                                  pattern=[[-1, P]], channel_multiplier=1))
            made(gp.tensor_scalar(minus[:].rearrange("p (h k) -> p h k", h=H),
                                  ident[:, 0:H].unsqueeze(2).broadcast_to([P, H, CK]), -1.0, None, ALU.mult))
            made(gp.memset(mx[:], 0.0))
            made(gp.memset(va[:], 0.0))
            made(gp.memset(vc[:], 0.0))
            made(gp.memset(sumk[:], 0.0))
            made(gp.memset(sumk[:, 0, 0:HD], 1.0))
            made(gp.memset(sumk[:, 1, HD:2 * HD], 1.0))
            made(gp.memset(sumc[:], 0.0))
            made(gp.memset(sumc[0:CK, 0, :], 1.0))
            made(gp.memset(sumc[CK:P, 1, :], 1.0))
            made(gp.memset(cmask, 1.0))
            made(gp.memset(cmask.rearrange("p (g m r) -> p g m r", m=2, r=HD)[:, :, 1, :], 0.0))
            made(gp.tensor_tensor(cmask, cmask, ident[:], ALU.mult))

            gp.wait_ge(consts.sem, 2)
            for i in range(2):
                gp.dma_start(xs[i].rearrange("(t p) d -> p t d", p=P),
                             zeros[:].rearrange("p (a d) -> p a d", a=1).broadcast_to([P, ET, D]))\
                    .then_inc(xs_zeroed.sem, 16)

            gp.wait_ge(weights_in.sem, 16 * 3)
            gp.tensor_copy(rw_h[:], rw).then_inc(router_split.sem, 1)
            gp.wait_ge(router_split.sem, 1)
            gp.tensor_tensor(rw_l[:], rw, rw_h[:].bitcast(F32), ALU.subtract).then_inc(router_split.sem, 1)
            for k in range(NE + 3):
                e = k - 2
                gp.wait_ge(raw_in[k % 4].sem, 16 * (1 if k < 2 else (2 * ((k - 2) // 4 + 1) + (1 if k % 4 < 2 else 0)) - (1 if k == NE + 2 else 0)))
                hi, lo = (sg_h[:, k], sg_l[:, k]) if k < 2 else (eg_h[:, e], eg_l[:, e]) if e < NE else (wq_h[:], wq_l[:])
                gp.tensor_copy(hi, raw[:, k % 4]).then_inc(raw_split.sem, 1)
                gp.wait_ge(raw_split.sem, raw_split.done(k, 1))
                gp.tensor_tensor(lo, raw[:, k % 4], hi.bitcast(F32), ALU.subtract).then_inc(raw_split.sem, 1)

            gp.wait_ge(xs_zeroed.sem, 32)

            def scatter(ph):
                gp.wait_ge(routed.sem, ph["r"] + 1)
                par = ph["par"]
                for t in range(TB):
                    for k in range(2):
                        gp.indirect_dma_start(xs[par], bass.IndirectOffsetOnAxis(ap=slot[:, par, k, t:t + 1], axis=0),
                                              xn[:, par, t, :], None).then_inc(scattered[par].sem, 16)

            def gather(ph):
                par = ph["par"]
                gp.wait_ge(scattered[par].sem, 16 * 2 * TB * sum(q["kind"] == "T" and q["par"] == par for q in phases[:ph["n"]]))
                before = max(q["ring"] + EP for q in phases[:ph["n"]] if q["kind"] == "E" and q["b"] == ph["b"])
                for s in range(NS):
                    gp.wait_ge(outs_stored[s].sem, before * (16 // NS))
                for i in range(PB):
                    c = ph["c"] + i
                    gp.wait_ge(c_out.sem, c_out.freed(c, 2))
                    for t in range(2):
                        for k in range(2):
                            gp.indirect_dma_start(
                                gath[par][:, c % 2, t, k, :], None, ys[par],
                                bass.IndirectOffsetOnAxis(ap=slot[:, par, k, 2 * i + t:2 * i + t + 1], axis=0))\
                                .then_inc(gathered[c % 2].sem, 16)

            for ph in phases:
                if ph["kind"] == "T":
                    scatter(ph)
                elif ph["kind"] in "CA":
                    gather(ph)

        @block.scalar
        def _(act):
            for sig in (ln_rows, tr_high, gu_tanh, e_high, e_tanh, e_out, a_high, a_qh, a_mt, x_exp, s_xf, s_kh, s_va,
                        s_hc, s_cm, s_ckh, s_vc, s_exp):
                act.sem_inc(sig.sem, sig.head * sig.per)

            def apply_norm(ph, i, src, dst):
                act.wait_ge(ln_small.sem, ln_small.done(ln_group(ph, i)))
                for t in range(2):
                    act.activation(dst[:, t, :], src[:, t, :], ACT.Identity, bias=lnb[:, i, t:t + 1],
                                   scale=rstd[:, i, t:t + 1]).then_inc(ln_rows.sem, 1)

            def tokens(ph):
                def apply(i):
                    apply_norm(ph, i, ring[:, i], xn[:, ph["par"], 2 * i:2 * i + 2, :])

                def high(i, s):
                    g, k = ph["t"] + i, s % 2
                    act.wait_ge(tr_pe.sem, tr_pe.done(g))
                    act.wait_ge(gu_pe.sem, gu_pe.freed(g, 2))
                    act.activation(flat(xt_h[:, k]), bank[k][:], ACT.Copy)\
                        .then_inc(tr_high.sem, 1)

                def tanh(i, s):
                    g = ph["t"] + i
                    for h in range(SH // P):
                        act.wait_ge(gu_pe.sem, gu_pe.done(g, h + 1))
                        act.activation(th[:, h], bank[2 + h][:, 0:2 * P], ACT.Tanh, scale=0.5).then_inc(gu_tanh.sem, 1)

                apply(0)
                apply(1)
                for i in range(PB + 1):
                    if i < PB:
                        high(i, i % NS)
                    if i:
                        tanh(i - 1, (i - 1) % NS)
                    if i + 2 < PB:
                        apply(i + 2)
                act.wait_ge(route.sem, ph["r"] * ROUTE + ROUTE_D)
                act.activation(wexp[:, 1, :], wexp[:, 0, :], ACT.Exp).then_inc(route_act.sem, 1)

            def experts(ph):
                def high(i, s):
                    g, k = ph["e"] + i, s % 2
                    act.wait_ge(e_tr.sem, e_tr.done(g))
                    act.wait_ge(e_gu.sem, e_gu.freed(g, 2))
                    act.activation(flat(xt_h[:, k]), bank[k][:], ACT.Copy)\
                        .then_inc(e_high.sem, 1)

                def tanh(i, s):
                    g, k = ph["e"] + i, s % 2
                    act.wait_ge(e_gu.sem, e_gu.done(g))
                    act.wait_ge(e_hid.sem, e_hid.freed(g, 2))
                    act.activation(th[:, k].rearrange("p (t n) -> p t n", t=2),
                                   bank[2 + k][:].rearrange("p (t m n) -> p t m n", t=2, m=2)[:, :, 0, :],
                                   ACT.Tanh, scale=0.5).then_inc(e_tanh.sem, 1)

                def result(i, s):
                    g = ph["e"] + i
                    act.wait_ge(e_dn.sem, e_dn.done(g))
                    act.wait_ge(outs_stored[s].sem, used(ph, i, s) - 16)
                    act.activation(flat(outs[:, s]), bank[6 + s % 2][:], ACT.Copy)\
                        .then_inc(e_out.sem, 1)

                steps(act, EP, [(0, high), (1, tanh), (3, result)])

            def attention(ph):
                b = ph["a"] // PB

                def apply(i):
                    for j in range(2):
                        if i:
                            act.wait_ge(a_tr.sem, a_tr.done(ph["a"] + i + j - 2))
                        apply_norm(ph, i + j, xa[ph["par"]][:, (i + j) % NS], xln[:, (i + j) % 2])

                def high(i):
                    a = ph["a"] + i
                    act.wait_ge(a_tr.sem, a_tr.done(a))
                    act.activation(flat(xt_h[:, 0]), bank[0][:], ACT.Copy).then_inc(a_high.sem, 1)

                def queries_high(i):
                    a = ph["a"] + i
                    act.wait_ge(a_q.sem, a_q.done(a))
                    act.activation(flat(q_h[:, 0]), bank[1][:], ACT.Copy).then_inc(a_qh.sem, 2)

                def maxima(i):
                    a = ph["a"] + i
                    act.wait_ge(a_mtr.sem, a_mtr.done(a))
                    act.activation(mt[:], bank[0][:, 0:2 * P], ACT.Copy).then_inc(a_mt.sem, 1)

                def exps(i):
                    a = ph["a"] + i
                    x = a - b - 1
                    for n in range(4):
                        act.wait_ge(x_st.sem, x_st.done(x, n + 1))
                        if i > 1:
                            act.wait_ge(x_pv.sem, x_pv.done(x - 1, n + 1))
                        act.activation(pt[:, n, :], bank[2 + n][:], ACT.Exp, scale=SCALE).then_inc(x_exp.sem, 1)

                def context():
                    act.activation(flat(xf), bank[0][:], ACT.Copy).then_inc(s_xf.sem, 1)
                    act.wait_ge(a_q.sem, a_q.done(ph["a"]))
                    for m in range(2):
                        act.activation(flat(q_h[:, m]), bank[1][:], ACT.Copy, scale=parity[:, m:m + 1])\
                            .then_inc(a_qh.sem, 1)
                    act.wait_ge(s_kv.sem, s_kv.done(b, 1))
                    act.activation(flat(k_h[:]), bank[2][:], ACT.Copy).then_inc(s_kh.sem, 1)
                    act.wait_ge(s_kv.sem, s_kv.done(b, 2))
                    for m in range(2):
                        for t in range(2):
                            ins = act.activation(va[:, t, :, m, m, :], bank[3][:, t * D:(t + 1) * D]
                                                 .rearrange("p (g m d) -> p g m d", m=2, d=HD)[:, :, m, :], ACT.Copy)
                    ins.then_inc(s_va.sem, 1)
                    act.wait_ge(s_h.sem, s_h.done(b))
                    act.activation(hc[:], bank[4][:, 0:CTX], ACT.Relu, bias=b1_s[:, 0:1]).then_inc(s_hc.sem, 1)
                    act.wait_ge(s_cp.sem, s_cp.done(b))
                    for k in range(KC):
                        for m in range(2):
                            ins = act.activation(cm[:, k, m, :], bank[5][:, k * CK:(k + 1) * CK], ACT.Identity,
                                                 bias=b2_s[:, k:k + 1], scale=0.25)
                    ins.then_inc(s_cm.sem, 1)
                    act.wait_ge(s_ckv.sem, s_ckv.done(b, 1))
                    keys = bank[6][:, 0:KC * CK].rearrange("p (k n) -> p k n", k=KC)
                    for m in range(2):
                        ins = act.activation(kc_h[:, :, m * CK:(m + 1) * CK], keys, ACT.Copy, scale=parity[:, m:m + 1])
                    ins.then_inc(s_ckh.sem, 1)
                    act.wait_ge(s_ckv.sem, s_ckv.done(b, 2))
                    for m in range(2):
                        ins = act.activation(vc[m * CK:(m + 1) * CK, :, m, :],
                                             bank[7][m * CK:(m + 1) * CK, 0:D]
                                             .rearrange("p (g m d) -> p g m d", m=2, d=HD)[:, :, m, :], ACT.Copy)
                    ins.then_inc(s_vc.sem, 1)

                def self_exps():
                    for n in range(H):
                        act.wait_ge(s_st.sem, s_st.done(b, n + 1))
                        if n >= 2:
                            act.wait_ge(s_pv.sem, s_pv.done(b, n - 1))
                        act.activation(pt[:, n % 2, 0:3 * P], bank[2 + n % 4][:, 0:3 * P], ACT.Exp, scale=SCALE)\
                            .then_inc(s_exp.sem, 1)

                apply(0)
                high(0)
                context()
                maxima(0)
                self_exps()
                for i in range(PB):
                    if i:
                        maxima(i)
                        exps(i)
                    if i % 2 and i + 1 < PB:
                        apply(i + 1)
                    if i + 1 < PB:
                        high(i + 1)
                        queries_high(i + 1)

            for ph in phases:
                fence(act, "act", ph["n"])
                {"T": tokens, "E": experts, "C": lambda ph: None, "A": attention}[ph["kind"]](ph)
                act.drain().then_inc(phase_done["act"].sem, 1)

        @block.vector
        def _(dve):
            for sig in (ln_stats, ln_small, tr_low, logits_dve, gu_hid, t_out, e_low, e_hid, e_ht, c_out, a_low,
                        a_ql, a_den, a_norm, a_out, x_mx, s_kl, s_hm, s_ckl, s_mx):
                dve.sem_inc(sig.sem, sig.head * sig.per)

            def tokens(ph):
                par = ph["par"]

                def rows_statistics(i):
                    dve.wait_ge(token_in[i].sem, 16 * (ph["r"] + 1))
                    statistics(ring[:, i], i)

                def low(i, s):
                    g, k = ph["t"] + i, s % 2
                    dve.wait_ge(tr_high.sem, tr_high.done(g))
                    dve.tensor_tensor(flat(xt_l[:, k]), bank[k][:], flat(xt_h[:, k]).bitcast(F32), ALU.subtract)\
                        .then_inc(tr_low.sem, 1)

                def bias(i, s):
                    g = ph["t"] + i
                    dve.wait_ge(logits_pe.sem, logits_pe.done(g))
                    dve.tensor_tensor(logits[:, ds(2 * i, 2), :],
                                      bank[4][:, 0:2 * NE].rearrange("p (t e) -> p t e", t=2),
                                      rb[:].unsqueeze(1).broadcast_to([P, 2, NE]), ALU.add)\
                        .then_inc(logits_dve.sem, 1)

                def hidden(i, s):
                    g = ph["t"] + i
                    for h in range(SH // P):
                        dve.wait_ge(gu_tanh.sem, gu_tanh.done(g, h + 1))
                        dve.scalar_tensor_tensor(th[:, h], th[:, h], 1.0, bank[2 + h][:, 0:2 * P], ALU.add, ALU.mult)\
                            .then_inc(gu_hid.sem, 1)
                        dve.wait_ge(gu_hid.sem, gu_hid.done(g, 2 * h + 1))
                        dve.wait_ge(dn_pe.sem, dn_pe.freed(g, 1))
                        dve.tensor_tensor(hid[:, h], th[:, h], bank[2 + h][:, 2 * P:4 * P], ALU.mult)\
                            .then_inc(gu_hid.sem, 1)

                def sums(i, s):
                    g = ph["t"] + i
                    dve.wait_ge(dn_pe.sem, dn_pe.done(g))
                    dve.scalar_tensor_tensor(flat(ring[:, i]), bank[6 + s % 2][:], 0.25, flat(ring[:, i]),
                                             ALU.mult, ALU.add).then_inc(t_out.sem, 1)

                rows_statistics(0)
                rows_statistics(1)
                layer_norm(ph, 0)
                for i in range(2, 5):
                    rows_statistics(i)
                for i in range(PB + 2):
                    if i < PB:
                        low(i, i % NS)
                    if i == 0:
                        for n in range(5, PB):
                            rows_statistics(n)
                        layer_norm(ph, 2)
                    if 1 <= i <= PB:
                        bias(i - 1, (i - 1) % NS)
                        hidden(i - 1, (i - 1) % NS)
                    if i >= 2:
                        sums(i - 2, (i - 2) % NS)
                routing(ph)

            def statistics(x, i):
                for t in range(2):
                    dve.bn_stats(bst[:, i, t, :], x[:, t, :]).then_inc(ln_stats.sem, 1)

            def layer_norm(ph, i):
                g = ln_group(ph, i)
                k = slice(*LN_GROUPS[ph["kind"]][g - ph["ln_groups"]])
                even, odd = bst[:, k, :, 0:3], bst[:, k, :, 3:6]

                def small(n, ins):
                    ins.then_inc(ln_small.sem, 1)

                def after(n):
                    dve.wait_ge(ln_small.sem, ln_small.done(g, n))

                dve.wait_ge(ln_stats.sem, ln_stats.done(ph["ln"] + k.stop - 1))
                small(1, dve.tensor_tensor(lnd[:, k], even[:, :, :, 1], odd[:, :, :, 1], ALU.subtract))
                small(2, dve.tensor_tensor(lnm[:, k], even[:, :, :, 1], odd[:, :, :, 1], ALU.add))
                small(3, dve.tensor_tensor(lnv[:, k], even[:, :, :, 2], odd[:, :, :, 2], ALU.add))
                after(1)
                small(4, dve.scalar_tensor_tensor(lnw[:, k], lnd[:, k], 0.25, lnd[:, k], ALU.mult, ALU.mult))
                after(3)
                small(5, dve.tensor_scalar(lnv[:, k], lnv[:, k], 1.0 / D, EPS, ALU.mult, ALU.add))
                after(5)
                small(6, dve.tensor_tensor(lnv[:, k], lnv[:, k], lnw[:, k], ALU.add))
                after(6)
                small(7, dve.tensor_scalar(rstd[:, k].bitcast(I32), lnv[:, k].bitcast(I32), -0.5, RSQRT_GUESS,
                                           ALU.mult, ALU.add))
                n = 7
                for _ in range(NEWTON):
                    after(n)
                    small(n + 1, dve.tensor_tensor(rsq[:, k], rstd[:, k], rstd[:, k], ALU.mult))
                    after(n + 1)
                    small(n + 2, dve.scalar_tensor_tensor(rsq[:, k], rsq[:, k], -0.5, lnv[:, k], ALU.mult, ALU.mult))
                    after(n + 2)
                    small(n + 3, dve.scalar_tensor_tensor(rstd[:, k], rsq[:, k], 1.5, rstd[:, k], ALU.add, ALU.mult))
                    n += 3
                after(n)
                small(n + 1, dve.scalar_tensor_tensor(lnb[:, k], lnm[:, k], -0.5, rstd[:, k], ALU.mult, ALU.mult))
                assert n + 1 == LN_STEPS

            def routing(ph):
                par = ph["par"]
                start = ph["r"] * ROUTE
                n = [0]

                def step(ins):
                    n[0] += 1
                    ins.then_inc(route.sem, 1)
                    return n[0]

                def after(k):
                    dve.wait_ge(route.sem, start + k)

                dve.wait_ge(logits_dve.sem, logits_dve.done(ph["t"] + PB - 1))
                for t in range(TB):
                    a = step(dve.max(top[:, t, :], logits[:, t, :]))
                after(a)
                for t in range(TB):
                    a = step(dve.max_index(topi[:, t, :], top[:, t, :], logits[:, t, :]))
                d = step(dve.tensor_tensor(wexp[:, 0, :], top[:, :, 1], top[:, :, 0], ALU.subtract))
                assert d == ROUTE_D
                after(a)
                a = step(dve.tensor_copy(topf[:].rearrange("p k t -> p t k"), topi[:, :, 0:2]))
                after(a)
                for k in range(2):
                    a = step(dve.tensor_tensor(onehot[:, k], iota_f[:, 0:NE].unsqueeze(2).broadcast_to([P, NE, TB]),
                                               topf[:, k, :].unsqueeze(1).broadcast_to([P, NE, TB]), ALU.is_equal))
                after(a)
                a = step(dve.tensor_tensor(flat(picked[:]), flat(onehot[:, 0]), flat(onehot[:, 1]), ALU.add))
                assert a == ROUTE_PICKED
                dve.wait_ge(route_pe.sem, ph["r"] + 1)
                before, totals = bank[4][:, 0:NE * TB], bank[4][:, NE * TB:2 * NE * TB]
                a = step(dve.tensor_copy(flat(tot[:]), totals))
                after(a)
                step(dve.tensor_tensor(flat(rank[:]), before, flat(tot[:]), ALU.subtract))
                a = step(dve.tensor_tensor_scan(flat(incl[:]), flat(restart[:]), flat(tot[:]), 0.0, ALU.mult, ALU.add))
                after(a)
                step(dve.tensor_tensor(flat(rank[:]), flat(rank[:]), flat(incl[:]), ALU.add))
                a = step(dve.tensor_scalar(tiles_of[:], incl[:, :, TB - 1], (P - 1) / 2, 1.0 / P, ALU.add, ALU.mult))
                after(a)
                a = step(dve.tensor_scalar(tiles_of[:], tiles_of[:], ROUND, None, ALU.add))
                after(a)
                a = step(dve.tensor_scalar(tiles_of[:], tiles_of[:], -ROUND, None, ALU.add))
                after(a)
                a = step(dve.tensor_tensor_scan(tiles_in[:], ones_f[:, 0:NE], tiles_of[:], 0.0, ALU.mult, ALU.add))
                after(a)
                a = step(dve.tensor_tensor(base[:], tiles_in[:], tiles_of[:], ALU.subtract))
                after(a)
                a = step(dve.scalar_tensor_tensor(rank[:], base[:].unsqueeze(2).broadcast_to([P, NE, TB]), float(P),
                                                  rank[:], ALU.mult, ALU.add))
                after(a)
                for k in range(2):
                    a = step(dve.tensor_tensor(flat(onehot[:, k]), flat(onehot[:, k]), flat(rank[:]), ALU.mult))
                after(a)
                for k in range(2):
                    a = step(dve.tensor_reduce(slotf[:, k, :], onehot[:, k].rearrange("p e t -> p t e"), AX.X, ALU.add))
                after(a)
                dve.tensor_copy(slot[:, par], slotf[:]).then_inc(routed.sem, 1)
                dve.wait_ge(route_act.sem, ph["r"] + 1)
                a = step(dve.tensor_scalar(wexp[:, 2, :], wexp[:, 1, :], 1.0, None, ALU.add))
                after(a)
                a = step(dve.reciprocal(wexp[:, 2, :], wexp[:, 2, :]))
                after(a)
                step(dve.tensor_scalar(wts[:, par, 0, :], wexp[:, 2, :], 0.25, None, ALU.mult))
                step(dve.scalar_tensor_tensor(wts[:, par, 1, :], wexp[:, 1, :], 0.25, wexp[:, 2, :], ALU.mult, ALU.mult))
                a = step(dve.tensor_tensor(cmpb[:], iota_f[0:1, :].unsqueeze(2).broadcast_to([1, ET, NE]),
                                           tiles_in[0:1, :].unsqueeze(1).broadcast_to([1, ET, NE]), ALU.is_ge))
                after(a)
                a = step(dve.tensor_reduce(texp, cmpb[:], AX.X, ALU.add))
                after(a)
                dve.tensor_scalar(table[:, par, :], texp, NE - 1.0, None, ALU.min).then_inc(table_ready.sem, 1)
                assert n[0] == ROUTE

            def experts(ph):
                def low(i, s):
                    g, k = ph["e"] + i, s % 2
                    dve.wait_ge(e_high.sem, e_high.done(g))
                    dve.tensor_tensor(flat(xt_l[:, k]), bank[k][:], flat(xt_h[:, k]).bitcast(F32), ALU.subtract)\
                        .then_inc(e_low.sem, 1)

                def hidden(i, s):
                    g, k = ph["e"] + i, s % 2
                    gu = bank[2 + k][:].rearrange("p (t m n) -> p t m n", t=2, m=2)
                    t_ = th[:, k].rearrange("p (t n) -> p t n", t=2)
                    dve.wait_ge(e_tanh.sem, e_tanh.done(g))
                    dve.scalar_tensor_tensor(t_, t_, 1.0, gu[:, :, 0, :], ALU.add, ALU.mult).then_inc(e_hid.sem, 1)
                    dve.wait_ge(e_hid.sem, e_hid.done(g, 1))
                    dve.wait_ge(e_htr.sem, e_htr.freed(g, 2))
                    dve.tensor_tensor(hid[:, k].rearrange("p (t n) -> p t n", t=2), t_, gu[:, :, 1, :], ALU.mult)\
                        .then_inc(e_hid.sem, 1)

                def turned(i, s):
                    g, k = ph["e"] + i, s % 2
                    dve.wait_ge(e_htr.sem, e_htr.done(g))
                    dve.wait_ge(e_dn.sem, e_dn.freed(g, 2))
                    dve.tensor_copy(ht[:, k], bank[4 + k][:, 0:2 * P]).then_inc(e_ht.sem, 1)

                steps(dve, EP, [(0, low), (1, hidden), (2, turned)])

            def combine_pair(ph, i, s, g, dst):
                par = ph["par"]
                dve.wait_ge(rows_in[s].sem, used(ph, i, s))
                dve.wait_ge(gathered[s % 2].sem, (g - s % 2) * 32 + 64)
                for t in range(2):
                    dve.scalar_tensor_tensor(rows[:, s, t, :], gath[par][:, s % 2, t, 0, :],
                                             wts[:, par, 0, ds(2 * i + t, 1)], rows[:, s, t, :],
                                             ALU.mult, ALU.add).then_inc(c_out.sem, 1)
                for t in range(2):
                    dve.wait_ge(c_out.sem, c_out.done(g, 1 + t))
                    dve.scalar_tensor_tensor(dst(t), gath[par][:, s % 2, t, 1, :],
                                             wts[:, par, 1, ds(2 * i + t, 1)], rows[:, s, t, :],
                                             ALU.mult, ALU.add).then_inc(c_out.sem, 1)

            def combine(ph):

                def step(i, s):
                    g = ph["c"] + i
                    dve.wait_ge(outs_stored[s].sem, used(ph, i, s) - 16)
                    combine_pair(ph, i, s, g, lambda t: outs[:, s, t, :])

                steps(dve, PB, [(0, step)])

            def attention(ph):
                def ready(i):
                    s, g = i % NS, ph["c"] + i
                    combine_pair(ph, i, s, g, lambda t: xa[ph["par"]][:, s, t, :])
                    dve.wait_ge(c_out.sem, c_out.done(g))
                    statistics(xa[ph["par"]][:, s], i)

                def low(i):
                    a = ph["a"] + i
                    dve.wait_ge(a_high.sem, a_high.done(a))
                    if i == 0:
                        dve.wait_ge(s_xf.sem, s_xf.done(a // PB))
                    dve.tensor_tensor(flat(xt_l[:, 0]), bank[0][:], flat(xt_h[:, 0]).bitcast(F32), ALU.subtract)\
                        .then_inc(a_low.sem, 1)

                def queries_low(i):
                    a = ph["a"] + i
                    dve.wait_ge(a_qh.sem, a_qh.done(a))
                    dve.tensor_tensor(flat(q_l[:, 0]), bank[1][:], flat(q_h[:, 0]).bitcast(F32), ALU.subtract)\
                        .then_inc(a_ql.sem, 2)

                def maxima(i):
                    a = ph["a"] + i
                    x = a - a // PB - 1
                    dve.wait_ge(a_mtr.sem, a_mtr.freed(a, 1))
                    for n in range(4):
                        dve.wait_ge(x_sm.sem, x_sm.done(x, n + 1))
                        dve.tensor_reduce(mx[:, :, 4 * n:4 * n + 4],
                                          bank[2 + n][:].rearrange("p (t h k) -> p t h k", t=2, h=4),
                                          AX.X, ALU.max).then_inc(x_mx.sem, 1)

                def norm(i):
                    a = ph["a"] + i
                    if i == 0:
                        dve.wait_ge(s_pv.sem, s_pv.done(a // PB))
                    else:
                        dve.wait_ge(x_pv.sem, x_pv.done(a - a // PB - 1))
                        dve.wait_ge(a_wo.sem, a_wo.freed(a, 1))
                    dve.reciprocal(flat(xt_f), bank[7][:]).then_inc(a_den.sem, 1)
                    dve.wait_ge(a_den.sem, a_den.done(a))
                    dve.tensor_tensor(flat(xt_f), bank[6][:], flat(xt_f), ALU.mult).then_inc(a_norm.sem, 1)

                def add(i):
                    a, s = ph["a"] + i, i % NS
                    dve.wait_ge(a_wo.sem, a_wo.done(a))
                    dve.wait_ge(outs_stored[s].sem, used(ph, i, s) - 16)
                    dve.tensor_tensor(flat(outs[:, s]), bank[1][:], flat(xa[ph["par"]][:, s]), ALU.add).then_inc(a_out.sem, 1)

                def context(b):
                    dve.wait_ge(a_qh.sem, a_qh.done(ph["a"]))
                    for m in range(2):
                        dve.scalar_tensor_tensor(flat(q_l[:, m]), bank[1][:], parity[:, m:m + 1],
                                                 flat(q_h[:, m]).bitcast(F32), ALU.mult, ALU.subtract)\
                            .then_inc(a_ql.sem, 1)
                    dve.wait_ge(s_kh.sem, s_kh.done(b))
                    dve.tensor_tensor(flat(k_l[:]), bank[2][:], flat(k_h[:]).bitcast(F32), ALU.subtract)\
                        .then_inc(s_kl.sem, 1)
                    dve.wait_ge(s_hc.sem, s_hc.done(b))
                    dve.tensor_reduce(hm[:], hc[:].rearrange("p (n r) -> p n r", r=CTX // CK), AX.X, ALU.add)\
                        .then_inc(s_hm.sem, 1)
                    dve.wait_ge(s_ckh.sem, s_ckh.done(b))
                    keys = bank[6][:, 0:KC * CK].rearrange("p (k n) -> p k n", k=KC)
                    for m in range(2):
                        ins = dve.scalar_tensor_tensor(kc_l[:, :, m * CK:(m + 1) * CK], keys, parity[:, m:m + 1],
                                                       kc_h[:, :, m * CK:(m + 1) * CK].bitcast(F32),
                                                       ALU.mult, ALU.subtract)
                    ins.then_inc(s_ckl.sem, 1)
                    dve.wait_ge(a_mtr.sem, a_mtr.freed(ph["a"], 1))
                    for n in range(12):
                        t, w = (0, 4) if n < 4 else (1, 2)
                        h0 = 4 * (n % 4) + (2 * (n // 8))
                        dve.wait_ge(s_sm.sem, s_sm.done(b, n + 1))
                        dve.tensor_reduce(mx[:, t, h0:h0 + w], bank[2 + n % 4][:].rearrange("p (h k) -> p h k", h=w),
                                          AX.X, ALU.max).then_inc(s_mx.sem, 1)

                ready(0)
                ready(1)
                layer_norm(ph, 0)
                low(0)
                context(ph["a"] // PB)
                ready(2)
                low(1)
                queries_low(1)
                maxima(1)
                for i in range(1, PB):
                    if i + 2 < PB:
                        ready(i + 2)
                    if i % 2 and i + 1 < PB:
                        layer_norm(ph, i + 1)
                    norm(i - 1)
                    if i + 1 < PB:
                        low(i + 1)
                        queries_low(i + 1)
                        maxima(i + 1)
                    add(i - 1)
                norm(PB - 1)
                add(PB - 1)

            dve.wait_ge(gp_step.sem, GP_STEPS)
            dve.tensor_reduce(parity[:, 0:1], cmask, AX.X, ALU.add).then_inc(parity_step.sem, 1)
            dve.wait_ge(parity_step.sem, 1)
            dve.tensor_scalar(parity[:, 1:2], parity[:, 0:1], -1.0, 1.0, ALU.mult, ALU.add).then_inc(parity_step.sem, 1)

            for ph in phases:
                fence(dve, "dve", ph["n"])
                {"T": tokens, "E": experts, "C": combine, "A": attention}[ph["kind"]](ph)
                dve.drain().then_inc(phase_done["dve"].sem, 1)

        @block.tensor
        def _(pe):
            for sig in (tr_pe, logits_pe, gu_pe, dn_pe, e_tr, e_gu, e_htr, e_dn, a_tr, a_q, a_mtr,
                        a_wo, x_sm, x_st, x_pv, s_kv, s_h, s_cp, s_ckv, s_sm, s_st, s_pv):
                pe.sem_inc(sig.sem, sig.head * sig.per)
            pe.wait_ge(gp_step.sem, GP_STEPS)
            pe.wait_ge(consts.sem, 1)

            def turned(out_, in_):
                return pe.transpose(out_, in_, ident[:])

            def turn_pair(src, b, last_sem):
                for k in range(KC):
                    for t in range(2):
                        m = turned(bank[b][:, (2 * k + t) * P:(2 * k + t + 1) * P], src(t, k))
                m.then_inc(last_sem, 1)

            def three(out_, lh, ll, rh, rl, first, last):
                pe.matmul(out_, lh, rh, start=first, stop=False)
                pe.matmul(out_, lh, rl, start=False, stop=False)
                return pe.matmul(out_, ll, rh, start=False, stop=last)

            def tokens(ph):
                par = ph["par"]

                def turn(i, s):
                    g, k = ph["t"] + i, s % 2
                    pe.wait_ge(ln_rows.sem, ln_rows.done(ph["ln"] + i))
                    pe.wait_ge(tr_low.sem, tr_low.freed(g, 2))
                    turn_pair(lambda t, c: xn[:, par, ds(2 * i + t, 1), c * P:(c + 1) * P].rearrange("p a d -> p (a d)"),
                              k, tr_pe.sem)

                def gate_up(i, s):
                    g, k = ph["t"] + i, s % 2
                    pe.wait_ge(tr_low.sem, tr_low.done(g))
                    if isinstance(i, int) and i == 0:
                        pe.wait_ge(raw_split.sem, raw_split.done(1))
                        pe.wait_ge(router_split.sem, 2)
                        pe.wait_ge(weights_in.sem, 16 * 3)
                    pe.wait_ge(logits_dve.sem, logits_dve.freed(g, 1))
                    for t in range(2):
                        for c in range(KC):
                            m = three(bank[4][:, t * NE:(t + 1) * NE],
                                      xt_h[:, k, c, t * P:(t + 1) * P], xt_l[:, k, c, t * P:(t + 1) * P],
                                      rw_h[:, c, :], rw_l[:, c, :], c == 0, c == KC - 1)
                    m.then_inc(logits_pe.sem, 1)
                    for h in range(SH // P):
                        pe.wait_ge(gu_hid.sem, gu_hid.done(g - 1, 2 * h + 2))
                        for m_ in range(2):
                            for c in range(KC):
                                m = three(bank[2 + h][:, m_ * 2 * P:(m_ + 1) * 2 * P],
                                          sg_h[:, m_, c, h * P:(h + 1) * P], sg_l[:, m_, c, h * P:(h + 1) * P],
                                          xt_h[:, k, c, :], xt_l[:, k, c, :], c == 0, c == KC - 1)
                        m.then_inc(gu_pe.sem, 1)

                def down_(i, s):
                    g = ph["t"] + i
                    pe.wait_ge(gu_hid.sem, gu_hid.done(g))
                    pe.wait_ge(t_out.sem, t_out.freed(g, 2))
                    for t in range(2):
                        for h in range(SH // P):
                            m = pe.matmul(bank[6 + s % 2][:, t * D:(t + 1) * D], hid[:, h, t * P:(t + 1) * P],
                                          sd[:, h, :], start=h == 0, stop=h == SH // P - 1)
                    m.then_inc(dn_pe.sem, 1)

                for i in range(PB + 2):
                    if i < PB:
                        turn(i, i % NS)
                    if i >= 2:
                        down_(i - 2, (i - 2) % NS)
                    if 1 <= i <= PB:
                        gate_up(i - 1, (i - 1) % NS)
                pe.wait_ge(route.sem, ph["r"] * ROUTE + ROUTE_PICKED)
                pe.matmul(bank[4][:, 0:NE * TB], below[:], flat(picked[:]), start=True, stop=True)
                pe.matmul(bank[4][:, NE * TB:2 * NE * TB], ones_b[:], flat(picked[:]), start=True, stop=True)\
                    .then_inc(route_pe.sem, 1)

            def experts(ph):
                par = ph["par"]
                pe.wait_ge(table_ready.sem, ph["r"] + 1)
                if ph["r"] == 0:
                    pe.wait_ge(raw_split.sem, raw_split.done(NE + 1))
                    pe.wait_ge(weights_in.sem, 16 * 4)

                mine = {}

                def turn_of(s, lag):
                    return (s + lag) % NS - lag

                def look_up(i, inside):
                    first, end = (i - 3, i + NS - 1) if inside else (max(i - 3, 0), min(i + NS - 1, EP))
                    n = NS + 2 if inside else end - first
                    ids = nc.values_load_multi_w_load_instructions(
                        table[0:1, par, ds(2 * first, 2 * n)], engines=[mybir.EngineType.PE],
                        min_val=0, max_val=NE - 1)[1]
                    mine["of"] = {(first - i + k): ids[2 * k:2 * k + 2] for k in range(n)} if not inside else \
                        {k - 3: ids[2 * k:2 * k + 2] for k in range(n)}

                def turn(i, s):
                    g, k = ph["e"] + i, s % 2
                    pe.wait_ge(rows_in[s].sem, used(ph, i, s))
                    pe.wait_ge(e_low.sem, e_low.freed(g, 2))
                    turn_pair(lambda t, c: rows[:, s, t, c * P:(c + 1) * P], k, e_tr.sem)

                def gate_up(i, s):
                    g, k = ph["e"] + i, s % 2
                    pe.wait_ge(e_low.sem, e_low.done(g))
                    pe.wait_ge(e_hid.sem, e_hid.freed(g, 2))
                    for t, e in enumerate(mine["of"][turn_of(s, 1)]):
                        wh = eg_h[:, ds(e, 1)].rearrange("p a k n -> p (a k) n")
                        wl = eg_l[:, ds(e, 1)].rearrange("p a k n -> p (a k) n")
                        for c in range(KC):
                            m = three(bank[2 + k][:, t * 2 * EH:(t + 1) * 2 * EH],
                                      xt_h[:, k, c, t * P:(t + 1) * P], xt_l[:, k, c, t * P:(t + 1) * P],
                                      wh[:, c, :], wl[:, c, :], c == 0, c == KC - 1)
                    m.then_inc(e_gu.sem, 1)

                def turn_hidden(i, s):
                    g, k = ph["e"] + i, s % 2
                    pe.wait_ge(e_hid.sem, e_hid.done(g))
                    pe.wait_ge(e_ht.sem, e_ht.freed(g, 2))
                    for t in range(2):
                        m = turned(bank[4 + k][:, t * P:(t + 1) * P], hid[:, k, t * P:(t + 1) * P])
                    m.then_inc(e_htr.sem, 1)

                def down_(i, s):
                    g, k = ph["e"] + i, s % 2
                    pe.wait_ge(e_ht.sem, e_ht.done(g))
                    pe.wait_ge(e_out.sem, e_out.freed(g, 2))
                    for t, e in enumerate(mine["of"][turn_of(s, 3)]):
                        m = pe.matmul(bank[6 + k][:, t * D:(t + 1) * D], ht[:, k, t * P:(t + 1) * P],
                                      ed[:, ds(e, 1), :].rearrange("p a d -> p (a d)"), start=True, stop=True)
                    m.then_inc(e_dn.sem, 1)

                steps(pe, EP, [(0, turn), (2, turn_hidden), (1, gate_up), (3, down_)], look_up)

            def attention(ph):
                if ph["a"] == 0:
                    pe.wait_ge(attn_in.sem, 16 * 8)
                    pe.wait_ge(raw_split.sem, raw_split.done(NE + 2))
                    pe.wait_ge(parity_step.sem, 2)
                b = ph["a"] // PB
                rows_turned(ph, 0)
                queries(ph, 0)
                context(b)
                self_scores(ph["a"], b)
                rows_turned(ph, 1)
                queries(ph, 1)
                scores(ph, 1)
                for i in range(1, PB):
                    turn_maxima(ph["a"] + i)
                    scores_turned(ph, i)
                    if i + 1 < PB:
                        rows_turned(ph, i + 1)
                        queries(ph, i + 1)
                    values(ph, i)
                    if i + 1 < PB:
                        scores(ph, i + 1)
                    output(ph, i - 1)
                output(ph, PB - 1)

            def rows_turned(ph, i):
                a = ph["a"] + i
                pe.wait_ge(ln_rows.sem, ln_rows.done(ph["ln"] + i))
                pe.wait_ge(a_mt.sem, a_mt.freed(a, 1))
                turn_pair(lambda t, c: xln[:, i % 2, t, c * P:(c + 1) * P], 0, a_tr.sem)

            def queries(ph, i):
                a = ph["a"] + i
                pe.wait_ge(a_low.sem, a_low.done(a))
                pe.wait_ge(a_out.sem, a_out.freed(a, 3))
                for c in range(KC):
                    for k in range(KC):
                        m = three(bank[1][:, c * 2 * P:(c + 1) * 2 * P],
                                  wq_h[:, k, c * P:(c + 1) * P], wq_l[:, k, c * P:(c + 1) * P],
                                  xt_h[:, 0, k, :], xt_l[:, 0, k, :], k == 0, k == KC - 1)
                m.then_inc(a_q.sem, 1)

            def output(ph, i):
                a = ph["a"] + i
                pe.wait_ge(a_norm.sem, a_norm.done(a))
                for t in range(2):
                    for k in range(KC):
                        m = pe.matmul(bank[1][:, t * D:(t + 1) * D], xt_f[:, k, t * P:(t + 1) * P], wo_s[:, k, :],
                                      start=k == 0, stop=k == KC - 1)
                m.then_inc(a_wo.sem, 1)

            def context(b):
                pe.wait_ge(s_xf.sem, s_xf.done(b))
                for c in range(KC):
                    for k in range(KC):
                        m = pe.matmul(bank[2][:, c * CTX:(c + 1) * CTX], wk_s[:, k, c * P:(c + 1) * P], xf[:, k, :],
                                      start=k == 0, stop=k == KC - 1)
                m.then_inc(s_kv.sem, 1)
                for t in range(2):
                    for k in range(KC):
                        m = pe.matmul(bank[3][:, t * D:(t + 1) * D], xf[:, k, t * P:(t + 1) * P], wv_s[:, k, :],
                                      start=k == 0, stop=k == KC - 1)
                m.then_inc(s_kv.sem, 1)
                for k in range(KC):
                    m = pe.matmul(bank[4][:, 0:CTX], w1_s[:, k, :], xf[:, k, :], start=k == 0, stop=k == KC - 1)
                m.then_inc(s_h.sem, 1)
                pe.wait_ge(s_hm.sem, s_hm.done(b))
                for k in range(KC):
                    m = pe.matmul(bank[5][:, k * CK:(k + 1) * CK], w2_s[:, k * P:(k + 1) * P], hm[:],
                                  start=True, stop=True)
                m.then_inc(s_cp.sem, 1)
                pe.wait_ge(s_cm.sem, s_cm.done(b))
                for c in range(KC):
                    for k in range(KC):
                        m = pe.matmul(bank[6][:, c * CK:(c + 1) * CK], wk_s[:, k, c * P:(c + 1) * P], cm[:, k, 0, :],
                                      start=k == 0, stop=k == KC - 1)
                m.then_inc(s_ckv.sem, 1)
                for k in range(KC):
                    m = pe.matmul(bank[7][:, 0:D], flat(cm[:, k]), wv_s[:, k, :], start=k == 0, stop=k == KC - 1)
                m.then_inc(s_ckv.sem, 1)

            def turn_maxima(a):
                if a % PB:
                    pe.wait_ge(x_mx.sem, x_mx.done(a - a // PB - 1))
                for t in range(2):
                    m = turned(bank[0][:, t * P:(t + 1) * P], mx[:, t, :])
                m.then_inc(a_mtr.sem, 1)

            def minus_max(out_, heads, cols, last):
                h, n = heads
                w = minus[:, h * CK:(h + n) * CK] if n > 1 else minus[:, h * CK:h * CK + 1].broadcast_to([P, P])
                return pe.matmul(out_, w, mt[:, cols[0]:cols[1]], start=False, stop=last)

            def self_scores(a, b):
                pe.wait_ge(a_ql.sem, a_ql.done(a))
                pe.wait_ge(s_kl.sem, s_kl.done(b))
                pe.wait_ge(s_va.sem, s_va.done(b))
                for n in range(12):
                    g, t = n % 4, int(n >= 4)
                    r = slice(32 * g, 32 * g + 32)
                    if n >= 4:
                        pe.wait_ge(s_mx.sem, s_mx.done(b, n - 3))
                    heads = [(c, m_) for c in range(2) for m_ in range(2)] if t == 0 else [(n // 4 - 1, m_) for m_ in range(2)]
                    keys = (t + 1) * P
                    for j, (c, m_) in enumerate(heads):
                        out_ = bank[2 + n % 4][:, j * keys:(j + 1) * keys]
                        pe.matmul(out_, q_h[r, m_, c, t * P:(t + 1) * P], k_h[r, c, 0:keys], start=True, stop=False)
                        m = pe.matmul(out_[:, t * P:keys], ident_b[:], mask_q[:], start=False, stop=True)
                    m.then_inc(s_sm.sem, 1)
                pe.wait_ge(s_mx.sem, s_mx.done(b))
                turn_maxima(a)
                pe.wait_ge(a_mt.sem, a_mt.done(a))

                def values(n):
                    pe.wait_ge(s_exp.sem, s_exp.done(b, n + 1))
                    g, c, m_ = n % 4, n // 8, n // 4 % 2
                    p_ = pt[:, n % 2, :]
                    r, o = slice(32 * g, 32 * g + 32), c * 2 * P
                    for out_, w0, w1 in ((bank[6], flat(va[:, 0, 4 * c + g, m_]), flat(va[:, 1, 4 * c + g, m_])),
                                         (bank[7], sumk[:, m_, :], sumk[:, m_, :])):
                        pe.matmul(out_[r, o:o + 2 * P], w0, p_[:, 0:2 * P], start=m_ == 0, stop=False)
                        m = pe.matmul(out_[r, o + P:o + 2 * P], w1, p_[:, 2 * P:3 * P], start=False, stop=m_ == 1)
                    m.then_inc(s_pv.sem, 1)

                for n in range(H):
                    g, c, m_ = n % 4, n // 8, n // 4 % 2
                    r = slice(32 * g, 32 * g + 32)
                    if n >= 4:
                        pe.wait_ge(s_exp.sem, s_exp.done(b, n - 3))
                    for t, cols, out_ in ((0, (0, 2 * P), bank[2 + g][:, 0:2 * P]), (1, (P, 2 * P), bank[2 + g][:, 2 * P:3 * P])):
                        three(out_, k_h[r, c, t * P:(t + 1) * P], k_l[r, c, t * P:(t + 1) * P],
                              q_h[r, m_, c, cols[0]:cols[1]], q_l[r, m_, c, cols[0]:cols[1]], True, False)
                        minus_max(out_, (4 * g + 2 * c + m_, 1), cols, False)
                        m = pe.matmul(out_[:, 0:P], ident_b[:], mask_k[:], start=False, stop=True)
                    m.then_inc(s_st.sem, 1)
                    if n:
                        values(n - 1)
                values(H - 1)

            def scores(ph, i):
                a = ph["a"] + i
                b = a // PB
                pe.wait_ge(a_ql.sem, a_ql.done(a))
                if i == 1:
                    pe.wait_ge(s_ckl.sem, s_ckl.done(b))
                    pe.wait_ge(s_vc.sem, s_vc.done(b))
                    pe.wait_ge(s_exp.sem, s_exp.done(b))
                else:
                    pe.wait_ge(x_exp.sem, x_exp.done(a - b - 2))
                for g in range(4):
                    r = slice(32 * g, 32 * g + 32)
                    for t in range(2):
                        for c in range(2):
                            m = pe.matmul(bank[2 + g][:, (2 * t + c) * P:(2 * t + c + 1) * P],
                                          q_h[r, 0, c, t * P:(t + 1) * P], kc_h[r, c, :], start=True, stop=True)
                    m.then_inc(x_sm.sem, 1)

            def scores_turned(ph, i):
                pe.wait_ge(a_mt.sem, a_mt.done(ph["a"] + i))
                for n in range(4):
                    for c in range(2):
                        r = slice(32 * n, 32 * n + 32)
                        out_ = bank[2 + n][:, c * 2 * P:(c + 1) * 2 * P]
                        three(out_, kc_h[r, c, :], kc_l[r, c, :], q_h[r, 0, c, :], q_l[r, 0, c, :], True, False)
                        m = minus_max(out_, (4 * n + 2 * c, 2), (0, 2 * P), True)
                    m.then_inc(x_st.sem, 1)

            def values(ph, i):
                a = ph["a"] + i
                x = a - a // PB - 1
                pe.wait_ge(a_norm.sem, a_norm.freed(a, 1))
                for n in range(4):
                    pe.wait_ge(x_exp.sem, x_exp.done(x, n + 1))
                    for c in range(KC):
                        cols = slice(c * 2 * P, (c + 1) * 2 * P)
                        for out_, w in ((bank[6], flat(vc[:, 4 * c + n])), (bank[7], flat(sumc[:]))):
                            m = pe.matmul(out_[32 * n:32 * n + 32, cols], w, pt[:, n, cols], start=True, stop=True)
                    m.then_inc(x_pv.sem, 1)

            for ph in phases:
                fence(pe, "pe", ph["n"])
                {"T": tokens, "E": experts, "C": lambda ph: None, "A": attention}[ph["kind"]](ph)
                pe.drain().then_inc(phase_done["pe"].sem, 1)


def flat(a):
    n = len(a.shape)
    if n == 2:
        return a
    names = " ".join("abcd"[:n - 1])
    return a.rearrange(f"p {names} -> p ({names})")


ROUTE_D = 2 * TB + 1
ROUTE_PICKED = 2 * TB + 5
ROUTE = 2 * TB + 5 + 20
GP_STEPS = 28

PLAN = [(kind, layer, b0 + b) for b0 in range(0, B, 2)
        for kind, layer, b in (("T", 0, 0), ("T", 0, 1), ("E", 0, 0), ("E", 0, 1), ("A", 0, 0), ("T", 1, 0),
                               ("A", 0, 1), ("T", 1, 1), ("E", 1, 0), ("E", 1, 1), ("C", 1, 0), ("C", 1, 1))]

_INS = ["L0_attn_hidden_states", "L0_attn_Wq", "L0_attn_Wk", "L0_attn_Wv", "L0_attn_Wo", "L0_attn_W1", "L0_attn_b1",
        "L0_attn_W2", "L0_attn_b2", "L0_ffn_router_w", "L0_ffn_router_bias", "L0_ffn_up_proj", "L0_ffn_gate_proj",
        "L0_ffn_down_proj", "L0_ffn_sh_gate", "L0_ffn_sh_up", "L0_ffn_sh_down"]
_TURNED = {"L0_ffn_router_w", "L0_ffn_sh_gate", "L0_ffn_sh_up", "L0_ffn_sh_down"}


def kernel(**inputs):
    import numpy as _np
    import concourse.bacc as _bacc
    from concourse.bass_utils import run_bass_kernel_spmd as _run

    nc = _bacc.Bacc("TRN2", target_bir_lowering=False, num_devices=1)
    arrays, args = {}, []
    for name in _INS:
        a = _np.ascontiguousarray(inputs[name].T if name in _TURNED else inputs[name])
        arrays[f"in_{name}"] = a
        args.append(nc.dram_tensor(f"in_{name}", a.shape, mybir.dt.from_np(a.dtype), kind="ExternalInput").ap())
    out = nc.dram_tensor("out", inputs[_INS[0]].shape, F32, kind="ExternalOutput").ap()
    macaron_kernel(nc, *args, out, PLAN)
    r = _run(nc, [arrays], core_ids=[0])
    return r.results[0]["out"]
```

```python
from contextlib import ExitStack

import concourse.bass as bass
from concourse import mybir

F32 = mybir.dt.float32
F32R = mybir.dt.float32r
BF16 = mybir.dt.bfloat16
I32 = mybir.dt.int32
U32 = mybir.dt.uint32
ALU = mybir.AluOpType
ACT = mybir.ActivationFunctionType
AX = mybir.AxisListType
ds = bass.ds

P = 128
B, S, D = 4, 2048, 256
KC = D // P
NE = 16
EH = 128
SH = 256
TB = S // P
PB = TB // 2
ET = 2 * S // P + NE
EP = ET // 2
E2 = 2 * EP
H, HD = 16, 16
CTX = 256
CK = 64
EPS = 1e-5
SCALE = HD ** -0.5
MASKED = -1.0e30
RSQRT_GUESS = float(0x5F3759DF)
NEWTON = 3
ROUND = 8388608.0
LN_STEPS = 8 + 3 * NEWTON
NS = 4


class Signal:

    def __init__(self, sem, per=1, head=4):
        self.sem, self.per, self.head = sem, per, head

    def done(self, g, k=None):
        return (g + self.head) * self.per + (self.per if k is None else k)

    def freed(self, g, n):
        return (g - n + self.head + 1) * self.per


def steps(eng, n, todo, begin=None, spans=None):
    last = max(lag for lag, _ in todo)
    head = (last + NS - 1) // NS * NS
    loops = (n - head) // NS

    def turn(i, r, inside):
        for lag, step in todo:
            if inside or 0 <= i - lag < n:
                step(i - lag, (r - lag) % NS)

    def ahead(i, inside):
        if begin:
            begin(i, inside)

    for i in range(head):
        if i % NS == 0:
            ahead(i, False)
        turn(i, i, False)
    first = head
    for bodies, extra, enter in spans or [(loops, None, None)]:
        if enter:
            enter()
        with eng.Fori(0, bodies) as j:
            ahead(j * NS + first, True)
            for r in range(NS):
                turn(j * NS + (first + r), r, True)
            if extra:
                extra(j)
        first += bodies * NS
    if last:
        ahead(first, False)
    for i in range(first, n + last):
        turn(i, i, False)


def macaron_kernel(nc, x_in, wq, wk, wv, wo, w1, b1, w2, b2, rw_t, rbias, up, gate, down,
                   shg_t, shu_t, shd_t, out, plan):
    ctx = ExitStack()
    with ctx:
        def sb(name, shape, dt=F32):
            return ctx.enter_context(nc.sbuf_tensor(name, shape, dt))

        def signal(name, per=1, head=4):
            return Signal(ctx.enter_context(nc.semaphore(name)), per, head)

        xs = [nc.dram_tensor(f"slot_rows{i}", [ET * P, D], F32).ap() for i in range(2)]
        ys = [nc.dram_tensor(f"slot_results{i}", [ET * P, D], F32).ap() for i in range(2)]
        acc_d = nc.dram_tensor("partial_sums", [B * S, D], F32).ap()
        acc_v = acc_d.rearrange("(g t p) d -> g p t d", t=2, p=P)
        x_v = x_in.rearrange("b (g t p) d -> (b g) p t d", t=2, p=P)
        out_v = out.rearrange("b (g t p) d -> (b g) p t d", t=2, p=P)
        xs_v = [a.rearrange("(g t p) d -> g p t d", t=2, p=P) for a in xs]
        ys_v = [a.rearrange("(g t p) d -> g p t d", t=2, p=P) for a in ys]

        raw = sb("raw_weights", [P, 4, KC, 2 * EH])
        eg_h = sb("expert_gate_up_high", [P, NE, KC, 2 * EH], F32R)
        eg_l = sb("expert_gate_up_low", [P, NE, KC, 2 * EH], F32R)
        ed = sb("expert_down", [P, NE, D])
        sg_h = sb("shared_gate_up_high", [P, 2, KC, SH], F32R)
        sg_l = sb("shared_gate_up_low", [P, 2, KC, SH], F32R)
        sd = sb("shared_down", [P, SH // P, D])
        rw_h = sb("router_high", [P, KC, NE], F32R)
        rw_l = sb("router_low", [P, KC, NE], F32R)
        rb = sb("router_bias", [P, NE])
        wq_h = sb("wq_high", [P, KC, D], F32R)
        wq_l = sb("wq_low", [P, KC, D], F32R)
        wk_s = sb("wk", [P, KC, D])
        wv_s = sb("wv", [P, KC, D])
        wo_s = sb("wo", [P, KC, D])
        w1_s = sb("w1", [P, KC, P])
        w2_s = sb("w2", [P, D])
        b1_s = sb("b1", [P, 1])
        b2_s = sb("b2", [P, KC])
        ident = sb("identity", [P, P])
        ones_f = sb("ones", [P, NE])
        below = sb("strictly_below", [P, P], BF16)
        ones_b = sb("ones_bf16", [P, P], BF16)
        iota_f = sb("iota", [P, ET])
        restart = sb("restart", [P, NE, TB])
        ident_b = sb("identity_bf16", [P, P], BF16)
        mask_q = sb("mask_query_key", [P, P], BF16)
        mask_k = sb("mask_key_query", [P, P], BF16)
        minus = sb("minus_by_head", [P, 4 * CK], F32R)
        parity = sb("head_parity", [P, 2])
        ring = sb("rows_and_results", [P, 2 * NS, 2, D])
        rows, outs = ring[:, 0:NS], ring[:, NS:2 * NS]
        xn = sb("normalised_rows", [P, 2, TB, D])
        xt_h = sb("rows_transposed_high", [P, 2, KC, 2 * P], F32R)
        xt_l = sb("rows_transposed_low", [P, 2, KC, 2 * P], F32R)
        work = sb("hidden_work", [P, 3, 2, 2 * P])
        th, hid, ht = work[:, 0], work[:, 1], work[:, 2]
        gath = [xn[:, par, 0:8, :].rearrange("p (s t k) d -> p s t k d", s=2, t=2) for par in range(2)]
        pt = raw.rearrange("p a b c -> p a (b c)")
        xf = raw[:, 3]
        xln = work[:, 1:3].rearrange("p k a b -> p k (a b)").rearrange("p k (t d) -> p k t d", t=2)

        def finals(i):
            return xn[:, i // 4, 4 * (i % 4):4 * (i % 4) + 4, :].rearrange("p (t k) d -> p t k d", t=2)

        xa_fifth = sb("combined_rows", [P, 2, D])

        def xa(par, i):
            return xa_fifth if i % 5 == 4 else xn[:, par, 8 + 2 * (i % 5):10 + 2 * (i % 5), :]

        cx = [xn[:, par, 8:12, :].rearrange("p (s t) d -> p s t d", s=2) for par in range(2)]
        xt_f = work[:, 0].rearrange("p a b -> p (a b)").rearrange("p (c n) -> p c n", c=KC)
        q_h = sb("queries_high", [P, 2, KC, 2 * P], F32R)
        q_l = sb("queries_low", [P, 2, KC, 2 * P], F32R)
        k_h = sb("keys_high", [P, KC, CTX], F32R)
        k_l = sb("keys_low", [P, KC, CTX], F32R)
        kc_h = sb("compressed_keys_high", [P, KC, 2 * CK], F32R)
        kc_l = sb("compressed_keys_low", [P, KC, 2 * CK], F32R)
        va = sb("values", [P, 2, H // 2, 2, 2, HD])
        sumk = sb("ones_by_head", [P, 2, 2 * HD])
        vc = sb("compressed_values", [P, H // 2, 2, HD])
        sumc = sb("ones_by_compressed_head", [P, 2, HD])
        hc = sb("compress_hidden", [P, CTX])
        zeros = hc
        hm = sb("compress_hidden_sums", [P, CK])
        iota_i = hm[:, 0:ET].bitcast(I32)
        cm = sb("compressed_transposed", [P, KC, 2, CK])
        rw = cm[:, :, 0, 0:NE]
        mx = sb("score_maxima", [P, 2, P])
        mt = sb("score_maxima_transposed", [P, 2 * P], F32R)
        bst = sb("bn_stats", [P, PB, 2, 6])
        lnd = sb("mean_difference", [P, PB, 2])
        lnm = sb("mean", [P, PB, 2])
        lnv = sb("variance", [P, PB, 2])
        lnw = sb("variance_of_halves", [P, PB, 2])
        rstd = sb("rstd", [P, PB, 2])
        lnb = sb("minus_mean_by_deviation", [P, PB, 2])
        rsq = sb("rsqrt_steps", [P, PB, 2])
        logits = sb("logits", [P, TB, NE])
        cmask = flat(logits[:])[:, 0:P]
        top = sb("top_values", [P, TB, 8])
        topi = sb("top_indices", [P, TB, 8], U32)
        topf = sb("top_indices_float", [P, 2, TB])
        route_work = work.rearrange("p a b c -> p (a b c)")
        onehot = route_work[:, 0:2 * NE * TB].rearrange("p (k e t) -> p k e t", k=2, e=NE)
        rank, tot, incl = (route_work[:, n * NE * TB:(n + 1) * NE * TB].rearrange("p (e t) -> p e t", e=NE) for n in (2, 3, 4))
        texp = sb("expert_of_tile", [1, 2 * ET])
        cmpb = route_work[0:1, 0:ET * NE].rearrange("p (t e) -> p t e", e=NE)
        picked = sb("picked", [P, NE, TB], BF16)
        tiles_of = sb("tiles_of_expert", [P, NE])
        tiles_in = sb("tiles_up_to_expert", [P, NE])
        base = sb("first_tile_of_expert", [P, NE])
        slotf = sb("slot_float", [P, 2, TB])
        slot = sb("slot", [P, 2, 2, TB], U32)
        wexp = sb("weight_exp", [P, 3, TB])
        wts = sb("weights", [P, 2, 2, TB])
        table = sb("experts_of_three_pairs", [1, E2 - 2], I32)

        bank = [ctx.enter_context(nc.psum_tensor(f"bank{i}", [P, 512], F32)) for i in range(8)]

        weights_in = signal("weights_in", 16, 0)
        raw_in = [signal(f"raw_in{i}", 16, 0) for i in range(4)]
        raw_split = signal("raw_split", 2, 4)
        router_split = signal("router_split", 2, 0)
        consts = signal("constants_ready", 1, 0)
        gp_step = signal("gpsimd_constant_steps", 1, 0)
        xs_zeroed = signal("slot_rows_zeroed", 16, 0)
        phase_done = {e: signal(f"phase_done_{e}", 1, 0) for e in ("pe", "act", "dve")}
        rows_in = [signal(f"rows_in{i}", 16, 0) for i in range(NS)]
        token_in = [signal(f"token_rows_in{i}", 16, 0) for i in range(PB)]
        token_stored = [signal(f"token_sums_stored{i}", 16, 0) for i in range(PB)]
        outs_stored = [signal(f"results_stored{i}", 16, 0) for i in range(NS)]
        ln_stats = signal("ln_stats", 2)
        ln_small = signal("ln_small_steps", LN_STEPS)
        ln_rows = signal("ln_rows_normalised", 2)
        tr_pe = signal("rows_transposed")
        tr_high = signal("transposed_high_split")
        tr_low = signal("transposed_low_split")
        logits_pe = signal("logits_multiplied")
        logits_dve = signal("logits_biased")
        gu_pe = signal("shared_gate_up_multiplied", 2)
        gu_tanh = signal("shared_tanh", 2)
        gu_hid = signal("shared_hidden", 4)
        dn_pe = signal("shared_down_multiplied")
        t_out = signal("token_sums_ready")
        route = signal("route_steps", 1, 0)
        route_pe = signal("ranks_counted", 1, 0)
        route_act = signal("route_exp", 1, 0)
        routed = signal("slots_ready", 1, 0)
        table_ready = signal("expert_table_ready", 1, 0)
        scattered = [signal(f"scattered{i}", 16 * 2 * TB, 0) for i in range(2)]
        gathered = [signal(f"gathered{i}", 64, 0) for i in range(2)]
        finals_in = [signal(f"final_results_gathered{i}", 64, 0) for i in range(PB)]
        e_tr = signal("slot_rows_transposed")
        e_high = signal("slot_high_split")
        e_low = signal("slot_low_split")
        e_gu = signal("expert_gate_up_multiplied")
        e_tanh = signal("expert_tanh")
        e_hid = signal("expert_hidden", 2)
        e_htr = signal("expert_hidden_transposed")
        e_ht = signal("expert_hidden_evacuated")
        e_dn = signal("expert_down_multiplied")
        e_out = signal("expert_rows_ready")
        sums_in = [signal(f"partial_sums_in{i}", 16, 0) for i in range(2)]
        sums_stored = [signal(f"layer_stored{i}", 16, 0) for i in range(2)]
        c_out = signal("combined_rows", 4)
        a_tr = signal("attention_rows_transposed")
        a_high = signal("attention_high_split")
        a_low = signal("attention_low_split")
        a_q = signal("queries_multiplied")
        a_qh = signal("queries_high_split", 2)
        a_ql = signal("queries_low_split", 2)
        a_mtr = signal("maxima_transposed")
        a_mt = signal("maxima_evacuated")
        a_den = signal("sums_inverted")
        a_norm = signal("heads_normalised")
        a_wo = signal("output_multiplied")
        a_out = signal("attention_sums_ready")
        x_sm = signal("cross_scores", 4)
        x_mx = signal("cross_maxima", 4)
        x_st = signal("cross_scores_transposed", 4)
        x_exp = signal("cross_exp", 4)
        x_pv = signal("cross_values_steps", 4)
        s_xf = signal("context_evacuated")
        s_kv = signal("context_keys_values_multiplied", 2)
        s_kh = signal("context_keys_high")
        s_kl = signal("context_keys_low")
        s_va = signal("context_values_evacuated")
        s_h = signal("compress_hidden_multiplied")
        s_hc = signal("compress_relu")
        s_hm = signal("compress_summed")
        s_cp = signal("compress_multiplied")
        s_cm = signal("compressed_evacuated")
        s_ckv = signal("compressed_keys_values_multiplied", 2)
        s_ckh = signal("compressed_keys_high")
        s_ckl = signal("compressed_keys_low")
        s_vc = signal("compressed_values_evacuated")
        s_sm = signal("self_scores", 12)
        s_mx = signal("self_maxima", 12)
        s_st = signal("self_scores_transposed", H)
        s_exp = signal("self_exp", H)
        s_pv = signal("self_values_steps", H)
        attn_in = signal("attention_weights_in", 16, 0)
        parity_step = signal("head_parity_steps", 2, 0)

        count = {"T": 0, "E": 0, "C": 0, "R": 0, "A": 0}
        all_pairs = 0
        phases = []
        groups = combined = 0
        for n, (kind, layer, b, last) in enumerate(plan):
            ph = {"kind": kind, "layer": layer, "b": b, "n": n, "ring": all_pairs, "par": b % 2}
            ph["ln"] = count["T"] + count["A"]
            ph["e_before"] = count["E"]
            ph["tokens_before"] = count["R"]
            ph["combined"] = combined
            if kind == "T":
                ph.update(t=count["T"], r=count["R"])
                count["T"] += PB
                count["R"] += 1
            elif kind == "E":
                ph.update(e=count["E"], r=count["E"] // E2)
                count["E"] += E2
                all_pairs += E2
            elif kind == "A":
                ph.update(a=count["A"], c=count["C"])
                count["C"] += PB
                count["A"] += PB
                all_pairs += PB
            elif kind == "C":
                ph.update(c=count["C"])
                count["C"] += PB
            if last is not None:
                ph["last"] = {"b": last, "par": last % 2, "c": count["C"], "before": combined, "n": n}
                count["C"] += PB
                combined += PB
            ph["ln_groups"] = groups
            groups += {"T": 2, "A": PB // 2 + 1}.get(kind, 0)
            phases.append(ph)

        def fence(eng, me, n):
            for other in phase_done:
                if other != me and n:
                    eng.wait_ge(phase_done[other].sem, n)

        LN_GROUPS = {"T": ((0, 2), (2, PB)), "A": ((0, 1), (1, 2)) + tuple((i, i + 2) for i in range(2, PB, 2))}

        def ln_group(ph, i):
            return ph["ln_groups"] + next(n for n, (a, b) in enumerate(LN_GROUPS[ph["kind"]]) if a <= i < b)

        block = ctx.enter_context(nc.Block())

        def used(ph, i, s):
            return (i - s + ph["ring"]) * (16 // NS) + 16

        @block.sync
        def _(sp):
            for m, w in enumerate((shg_t, shu_t)):
                sp.dma_start(raw[:, m, :, :], w.rearrange("(k p) h -> p k h", p=P)).then_inc(raw_in[m].sem, 16)
            sp.dma_start(rw, rw_t.rearrange("(k p) e -> p k e", p=P)).then_inc(weights_in.sem, 16)
            sp.dma_start(rb[:], rbias.rearrange("(a e) -> a e", a=1).broadcast_to([P, NE])).then_inc(weights_in.sem, 16)
            sp.dma_start(sd[:], shd_t.rearrange("(k p) d -> p k d", p=P)).then_inc(weights_in.sem, 16)

            for dst, src in ((wk_s, wk), (wv_s, wv), (wo_s, wo), (w1_s, w1)):
                sp.dma_start(dst[:], src.rearrange("(k p) n -> p k n", p=P)).then_inc(attn_in.sem, 16)
            sp.dma_start(w2_s[:], w2).then_inc(attn_in.sem, 16)
            sp.dma_start(b1_s[:], b1.rearrange("(p a) -> p a", a=1)).then_inc(attn_in.sem, 16)
            for k in range(KC):
                sp.dma_start(b2_s[:, k:k + 1], b2[k * P:(k + 1) * P].rearrange("(p a) -> p a", a=1))\
                    .then_inc(attn_in.sem, 16)

            def load_rows(ph, i, s):
                sp.wait_ge(c_out.sem, c_out.freed(ph["c"] + i, NS))
                sp.dma_start(rows[:, s], acc_v[ph["b"] * PB + i]).then_inc(rows_in[s].sem, 16)

            def store_rows(ph, i, s):
                sp.wait_ge(a_out.sem, a_out.done(ph["a"] + i))
                sp.dma_start(acc_v[ph["b"] * PB + i], outs[:, s]).then_inc(outs_stored[s].sem, 16)

            def load_slots(ph, par):
                def step(i, s):
                    sp.wait_ge(e_tr.sem, e_tr.freed(ph["e"] + par * EP + i, NS))
                    sp.dma_start(rows[:, s, :, :], xs_v[par][ds(i, 1)].rearrange("a p t d -> p (a t) d"))\
                        .then_inc(rows_in[s].sem, 16)
                return step

            def load_tokens(ph, pairs):
                src, first = acc_v if ph["layer"] else x_v, ph["b"] * PB
                for i in pairs:
                    sp.dma_start(ring[:, i], src[first + i]).then_inc(token_in[i].sem, 16)

            def tokens(ph):
                before = phases[ph["n"] - 1]["kind"] if ph["n"] else ""
                after = phases[ph["n"] + 1]
                load_tokens(ph, range({"": 0, "T": PB}.get(before, NS), PB))

                def load_when_stored(i):
                    sp.wait_ge(token_stored[i].sem, 16 * (ph["r"] + 1))
                    load_tokens(after, [i])

                for i in range(PB):
                    if ph["n"] == 0:
                        for e in range(i * NE // PB, (i + 1) * NE // PB):
                            load_expert(e)
                    sp.wait_ge(t_out.sem, t_out.done(ph["t"] + i))
                    sp.dma_start(acc_v[ph["b"] * PB + i], ring[:, i]).then_inc(token_stored[i].sem, 16)
                    if after["kind"] == "T" and i >= 2:
                        load_when_stored(i - 2)
                if after["kind"] == "T":
                    for i in range(PB - 2, PB):
                        load_when_stored(i)

                if ph["n"] == 0:
                    k = NE + 2
                    sp.wait_ge(raw_split.sem, raw_split.freed(k, 4))
                    sp.dma_start(raw[:, k % 4], wq.rearrange("(k p) n -> p k n", p=P)).then_inc(raw_in[k % 4].sem, 16)
                    sp.dma_start(ed[:], down.rearrange("e p d -> p e d")).then_inc(weights_in.sem, 16)

            def load_expert(e):
                k = e + 2
                sp.wait_ge(raw_split.sem, raw_split.freed(k, 4))
                for m, w in enumerate((gate, up)):
                    sp.dma_start(raw[:, k % 4, :, m * EH:(m + 1) * EH],
                                 w[e].rearrange("(k p) h -> p k h", p=P)).then_inc(raw_in[k % 4].sem, 16)

            for ph in phases:
                if ph["kind"] == "A":
                    for sig in token_stored:
                        sp.wait_ge(sig.sem, 16 * ph["tokens_before"])
                    sp.wait_ge(e_tr.sem, e_tr.done(ph["e_before"] - 1))
                    for i in range(NS):
                        load_rows(ph, i, i)
                if ph["kind"] == "T" and ph["n"] and phases[ph["n"] - 1]["kind"] == "E":
                    sp.wait_ge(e_tr.sem, e_tr.done(ph["e_before"] - 1))
                    load_tokens(ph, range(NS))
                if ph["n"]:
                    for other in phase_done:
                        sp.wait_ge(phase_done[other].sem, ph["n"])
                for s in range(NS):
                    sp.wait_ge(outs_stored[s].sem, ph["ring"] * (16 // NS))
                for sig in token_stored:
                    sp.wait_ge(sig.sem, 16 * ph["tokens_before"])
                if ph["kind"] == "T":
                    tokens(ph)
                elif ph["kind"] == "E":
                    for par in range(2):
                        sp.wait_ge(scattered[par].sem, 16 * 2 * TB * (ph["r"] + 1))
                        steps(sp, EP, [(0, load_slots(ph, par))])
                elif ph["kind"] == "A":
                    for i in range(PB + 5):
                        if NS <= i < PB:
                            load_rows(ph, i, i % NS)
                        if i == PB + 4:
                            sp.wait_ge(c_out.sem, c_out.done(ph["c"] + PB - 1))
                            for s in range(NS):
                                sp.wait_ge(outs_stored[s].sem, used(ph, s, s))
                            load_tokens(phases[ph["n"] + 1], range(NS))
                        if i >= 5:
                            store_rows(ph, i - 5, (i - 5) % NS)
                elif ph["kind"] == "C":
                    for i in range(PB):
                        sp.dma_start(ring[:, i], acc_v[ph["b"] * PB + i]).then_inc(token_in[i].sem, 16)
                    for i in range(PB):
                        sp.wait_ge(c_out.sem, c_out.done(ph["c"] + i))
                        sp.dma_start(out_v[ph["b"] * PB + i], ring[:, i]).then_inc(token_stored[i].sem, 16)
            for s in range(NS):
                sp.wait_ge(outs_stored[s].sem, all_pairs * (16 // NS))
            for sig in token_stored:
                sp.wait_ge(sig.sem, 16 * (count["R"] + 1))

        @block.gpsimd
        def _(gp):
            def made(ins):
                ins.then_inc(gp_step.sem, 1)
                made.n += 1
                gp.wait_ge(gp_step.sem, made.n)
            made.n = 0
            gp.sem_inc(raw_split.sem, raw_split.head * raw_split.per)
            made(gp.memset(ident[:], 0.0))
            made(gp.affine_select(out=ident[:], in_=ident[:], compare_op=ALU.not_equal, fill=1.0, base=0,
                                  pattern=[[-1, P]], channel_multiplier=1))
            gp.memset(ones_b[:], 1.0).then_inc(consts.sem, 1)
            made(gp.memset(ones_f[:], 1.0))
            made(gp.memset(below[:], 1.0))
            made(gp.affine_select(out=below[:], in_=below[:], compare_op=ALU.is_gt, fill=0.0, base=0,
                                  pattern=[[1, P]], channel_multiplier=-1))
            made(gp.memset(restart[:], 1.0))
            made(gp.memset(restart[:, :, 0:1], 0.0))
            made(gp.iota(iota_i, pattern=[[1, ET]], base=0, channel_multiplier=0))
            made(gp.tensor_copy(iota_f[:], iota_i))
            gp.memset(zeros[:], 0.0).then_inc(consts.sem, 1)
            made(gp.tensor_copy(ident_b[:], ident[:]))
            made(gp.memset(mask_q[:], MASKED))
            made(gp.affine_select(out=mask_q[:], in_=mask_q[:], compare_op=ALU.is_gt, fill=0.0, base=0,
                                  pattern=[[1, P]], channel_multiplier=-1))
            made(gp.memset(mask_k[:], MASKED))
            made(gp.affine_select(out=mask_k[:], in_=mask_k[:], compare_op=ALU.is_gt, fill=0.0, base=0,
                                  pattern=[[-1, P]], channel_multiplier=1))
            for g in range(4):
                r = slice(32 * g, 32 * g + 32)
                made(gp.tensor_scalar(minus[r].rearrange("p (h k) -> p h k", h=4),
                                      ident[r, 32 * g:32 * g + 4].unsqueeze(2).broadcast_to([32, 4, CK]),
                                      -1.0, None, ALU.mult))
            made(gp.memset(mx[:], 0.0))
            made(gp.memset(va[:], 0.0))
            made(gp.memset(vc[:], 0.0))
            made(gp.memset(sumk[:], 0.0))
            made(gp.memset(sumk[:, 0, 0:HD], 1.0))
            made(gp.memset(sumk[:, 1, HD:2 * HD], 1.0))
            made(gp.memset(sumc[:], 0.0))
            made(gp.memset(sumc[0:CK, 0, :], 1.0))
            made(gp.memset(sumc[CK:P, 1, :], 1.0))
            made(gp.memset(cmask, 1.0))
            made(gp.memset(cmask.rearrange("p (g m r) -> p g m r", m=2, r=HD)[:, :, 1, :], 0.0))
            made(gp.tensor_tensor(cmask, cmask, ident[:], ALU.mult))

            gp.wait_ge(consts.sem, 2)
            for i in range(2):
                gp.dma_start(xs[i].rearrange("(t p) d -> p t d", p=P),
                             zeros[:].rearrange("p (a d) -> p a d", a=1).broadcast_to([P, ET, D]))\
                    .then_inc(xs_zeroed.sem, 16)

            gp.wait_ge(weights_in.sem, 16 * 3)
            gp.tensor_copy(rw_h[:], rw).then_inc(router_split.sem, 1)
            gp.wait_ge(router_split.sem, 1)
            gp.tensor_tensor(rw_l[:], rw, rw_h[:].bitcast(F32), ALU.subtract).then_inc(router_split.sem, 1)
            loads = [1, 1] + [2] * NE + [1]
            for k in range(NE + 3):
                e = k - 2
                gp.wait_ge(raw_in[k % 4].sem, 16 * sum(loads[k % 4:k + 1:4]))
                hi, lo = (sg_h[:, k], sg_l[:, k]) if k < 2 else (eg_h[:, e], eg_l[:, e]) if e < NE else (wq_h[:], wq_l[:])
                gp.tensor_copy(hi, raw[:, k % 4]).then_inc(raw_split.sem, 1)
                gp.wait_ge(raw_split.sem, raw_split.done(k, 1))
                gp.tensor_tensor(lo, raw[:, k % 4], hi.bitcast(F32), ALU.subtract).then_inc(raw_split.sem, 1)

            gp.wait_ge(xs_zeroed.sem, 32)

            def scatter(ph, tiles):
                par = ph["par"]
                gp.wait_ge(routed.sem, ph["r"] + 1)
                for t in tiles:
                    for k in range(2):
                        gp.indirect_dma_start(xs[par], bass.IndirectOffsetOnAxis(ap=slot[:, par, k, t:t + 1], axis=0),
                                              xn[:, par, t, :], None).then_inc(scattered[par].sem, 16)

            def results_stored(b, n):
                before = max(q["ring"] for q in phases[:n + 1] if q["kind"] == "E" and q["b"] // 2 == b // 2)
                for s in range(NS):
                    gp.wait_ge(outs_stored[s].sem, (before + (b % 2 + 1) * EP) * (16 // NS))

            def gather_pair(c, par, i):
                for t in range(2):
                    for k in range(2):
                        gp.indirect_dma_start(
                            gath[par][:, c % 2, t, k, :], None, ys[par],
                            bass.IndirectOffsetOnAxis(ap=slot[:, par, k, 2 * i + t:2 * i + t + 1], axis=0))\
                            .then_inc(gathered[c % 2].sem, 16)

            def last_sums(last):
                par, first, done = last["par"], last["b"] * PB, last["before"]
                results_stored(last["b"], last["n"])

                def store(i):
                    gp.wait_ge(c_out.sem, c_out.done(last["c"] + i))
                    gp.dma_start(out_v[first + i], cx[par][:, i % 2]).then_inc(sums_stored[i % 2].sem, 16)

                for i in range(0, PB, 2):
                    for j in range(2):
                        if i:
                            store(i - 2 + j)
                    for j in range(2):
                        gp.wait_ge(sums_stored[j].sem, 8 * (done + i))
                        gp.dma_start(cx[par][:, j], acc_v[first + i + j]).then_inc(sums_in[j].sem, 16)
                        gather_pair(last["c"] + i + j, par, i + j)
                for j in range(2):
                    store(PB - 2 + j)

            def gather(ph, waiting):
                par = ph["par"]
                gp.wait_ge(scattered[par].sem, 16 * 2 * TB * sum(q["kind"] == "T" and q["par"] == par for q in phases[:ph["n"]]))
                results_stored(ph["b"], ph["n"])
                for i in range(PB):
                    c = ph["c"] + i
                    gp.wait_ge(c_out.sem, c_out.freed(c, 2))
                    gather_pair(c, par, i)
                    if waiting and i:
                        scatter(waiting, range(2 * i - 2, 2 * i))
                if waiting:
                    scatter(waiting, range(TB - 2, TB))

            def gather_all(ph):
                results_stored(ph["b"], ph["n"])
                for sig in sums_stored:
                    gp.wait_ge(sig.sem, 8 * combined)
                for i in range(PB):
                    for t in range(2):
                        for k in range(2):
                            gp.indirect_dma_start(
                                finals(i)[:, t, k, :], None, ys[ph["par"]],
                                bass.IndirectOffsetOnAxis(ap=slot[:, ph["par"], k, 2 * i + t:2 * i + t + 1], axis=0))\
                                .then_inc(finals_in[i].sem, 16)

            for ph in phases:
                if "last" in ph:
                    last_sums(ph["last"])
                if ph["kind"] == "C":
                    gather_all(ph)
                after = phases[ph["n"] + 1]["kind"] if ph["n"] + 1 < len(phases) else ""
                if ph["kind"] == "T" and after != "A":
                    scatter(ph, range(TB))
                elif ph["kind"] == "A":
                    before = phases[ph["n"] - 1]
                    gather(ph, before if before["kind"] == "T" else None)
            for sig in sums_stored:
                gp.wait_ge(sig.sem, 8 * combined)

        @block.scalar
        def _(act):
            for sig in (ln_rows, tr_high, gu_tanh, e_high, e_tanh, e_out, a_high, a_qh, a_mt, x_exp, s_xf, s_kh, s_va,
                        s_hc, s_cm, s_ckh, s_vc, s_exp):
                act.sem_inc(sig.sem, sig.head * sig.per)

            def apply_norm(ph, i, src, dst):
                act.wait_ge(ln_small.sem, ln_small.done(ln_group(ph, i)))
                for t in range(2):
                    act.activation(dst[:, t, :], src[:, t, :], ACT.Identity, bias=lnb[:, i, t:t + 1],
                                   scale=rstd[:, i, t:t + 1]).then_inc(ln_rows.sem, 1)

            def tokens(ph):
                def apply(i):
                    apply_norm(ph, i, ring[:, i], xn[:, ph["par"], 2 * i:2 * i + 2, :])

                def high(i, s):
                    g, k = ph["t"] + i, s % 2
                    act.wait_ge(tr_pe.sem, tr_pe.done(g))
                    act.wait_ge(gu_pe.sem, gu_pe.freed(g, 2))
                    act.activation(flat(xt_h[:, k]), bank[k][:], ACT.Copy)\
                        .then_inc(tr_high.sem, 1)

                def tanh(i, s):
                    g = ph["t"] + i
                    for h in range(SH // P):
                        act.wait_ge(gu_pe.sem, gu_pe.done(g, h + 1))
                        act.activation(th[:, h], bank[2 + h][:, 0:2 * P], ACT.Tanh, scale=0.5).then_inc(gu_tanh.sem, 1)

                for sig in sums_stored:
                    act.wait_ge(sig.sem, 8 * ph["combined"])
                apply(0)
                apply(1)
                for i in range(PB + 1):
                    if i < PB:
                        high(i, i % NS)
                    if i:
                        tanh(i - 1, (i - 1) % NS)
                    if i + 2 < PB:
                        apply(i + 2)
                act.drain().then_inc(phase_done["act"].sem, 1)
                act.wait_ge(route.sem, ph["r"] * ROUTE + ROUTE_D)
                act.activation(wexp[:, 1, :], wexp[:, 0, :], ACT.Exp).then_inc(route_act.sem, 1)

            def experts(ph):
                def high(i, s):
                    g, k = ph["e"] + i, s % 2
                    act.wait_ge(e_tr.sem, e_tr.done(g))
                    act.wait_ge(e_gu.sem, e_gu.freed(g, 2))
                    act.activation(flat(xt_h[:, k]), bank[k][:], ACT.Copy)\
                        .then_inc(e_high.sem, 1)

                def tanh(i, s):
                    g, k = ph["e"] + i, s % 2
                    act.wait_ge(e_gu.sem, e_gu.done(g))
                    act.wait_ge(e_hid.sem, e_hid.freed(g, 2))
                    act.activation(th[:, k].rearrange("p (t n) -> p t n", t=2),
                                   bank[2 + k][:].rearrange("p (t m n) -> p t m n", t=2, m=2)[:, :, 0, :],
                                   ACT.Tanh, scale=0.5).then_inc(e_tanh.sem, 1)

                def result(i, s):
                    g = ph["e"] + i
                    act.wait_ge(e_dn.sem, e_dn.done(g))
                    act.wait_ge(outs_stored[s].sem, used(ph, i, s) - 16)
                    act.activation(flat(outs[:, s]), bank[6 + s % 2][:], ACT.Copy)\
                        .then_inc(e_out.sem, 1)

                batch = [0]

                def second_batch():
                    batch[0] = 1

                def store(i, s):
                    act.wait_ge(e_out.sem, e_out.done(ph["e"] + i))
                    act.dma_start(ys_v[batch[0]][ds(i - batch[0] * EP, 1)].rearrange("a p t d -> p (a t) d"), outs[:, s])\
                        .then_inc(outs_stored[s].sem, 16)

                steps(act, E2, [(4, store), (0, high), (1, tanh), (3, result)],
                      spans=[(EP // NS, None, None), (EP // NS - 1, None, second_batch)])

            def attention(ph):
                b = ph["a"] // PB

                def apply(i):
                    if i > 1:
                        act.wait_ge(a_tr.sem, a_tr.done(ph["a"] + i - 2))
                    apply_norm(ph, i, xa(ph["par"], i), xln[:, i % 2])

                def high(i):
                    a = ph["a"] + i
                    act.wait_ge(a_tr.sem, a_tr.done(a))
                    act.activation(flat(xt_h[:, 0]), bank[0][:], ACT.Copy).then_inc(a_high.sem, 1)

                def queries_high(i):
                    a = ph["a"] + i
                    act.wait_ge(a_q.sem, a_q.done(a))
                    act.activation(flat(q_h[:, 0]), bank[1][:], ACT.Copy).then_inc(a_qh.sem, 2)

                def maxima(i):
                    a = ph["a"] + i
                    act.wait_ge(a_mtr.sem, a_mtr.done(a))
                    act.activation(mt[:], bank[0][:, 0:2 * P], ACT.Copy).then_inc(a_mt.sem, 1)

                def exps(i, half):
                    a = ph["a"] + i
                    x = a - b - 1
                    for n in (2 * half, 2 * half + 1):
                        act.wait_ge(x_st.sem, x_st.done(x, n + 1))
                        if i > 1:
                            act.wait_ge(x_pv.sem, x_pv.done(x - 1, n + 1))
                        act.activation(pt[:, n, :], bank[2 + n][:], ACT.Exp, scale=SCALE).then_inc(x_exp.sem, 1)

                def context():
                    act.activation(flat(xf), bank[0][:], ACT.Copy).then_inc(s_xf.sem, 1)
                    act.wait_ge(a_q.sem, a_q.done(ph["a"]))
                    for m in range(2):
                        act.activation(flat(q_h[:, m]), bank[1][:], ACT.Copy, scale=parity[:, m:m + 1])\
                            .then_inc(a_qh.sem, 1)
                    act.wait_ge(s_kv.sem, s_kv.done(b, 1))
                    act.activation(flat(k_h[:]), bank[2][:], ACT.Copy).then_inc(s_kh.sem, 1)
                    act.wait_ge(s_h.sem, s_h.done(b))
                    act.activation(hc[:], bank[7][:, 0:CTX], ACT.Relu, bias=b1_s[:, 0:1]).then_inc(s_hc.sem, 1)
                    act.wait_ge(s_kv.sem, s_kv.done(b, 2))
                    for m in range(2):
                        for t in range(2):
                            ins = act.activation(va[:, t, :, m, m, :], bank[6][:, t * D:(t + 1) * D]
                                                 .rearrange("p (g m d) -> p g m d", m=2, d=HD)[:, :, m, :], ACT.Copy)
                    ins.then_inc(s_va.sem, 1)
                    act.wait_ge(s_cp.sem, s_cp.done(b))
                    for k in range(KC):
                        for m in range(2):
                            ins = act.activation(cm[:, k, m, :], bank[7][:, CTX + k * CK:CTX + (k + 1) * CK], ACT.Identity,
                                                 bias=b2_s[:, k:k + 1], scale=0.25)
                    ins.then_inc(s_cm.sem, 1)
                    act.wait_ge(s_ckv.sem, s_ckv.done(b, 1))
                    keys = bank[7][:, 6 * CK:8 * CK].rearrange("p (k n) -> p k n", k=KC)
                    for m in range(2):
                        ins = act.activation(kc_h[:, :, m * CK:(m + 1) * CK], keys, ACT.Copy, scale=parity[:, m:m + 1])
                    ins.then_inc(s_ckh.sem, 1)
                    act.wait_ge(s_ckv.sem, s_ckv.done(b, 2))
                    for m in range(2):
                        ins = act.activation(vc[m * CK:(m + 1) * CK, :, m, :],
                                             bank[6][m * CK:(m + 1) * CK, 0:D]
                                             .rearrange("p (g m d) -> p g m d", m=2, d=HD)[:, :, m, :], ACT.Copy)
                    ins.then_inc(s_vc.sem, 1)

                def self_exps():
                    for n in range(H):
                        act.wait_ge(s_st.sem, s_st.done(b, n + 1))
                        if n >= 4:
                            act.wait_ge(s_pv.sem, s_pv.done(b, n - 3))
                        act.activation(pt[:, n % 4, 0:3 * P], bank[2 + n % 4][:, 0:3 * P], ACT.Exp, scale=SCALE)\
                            .then_inc(s_exp.sem, 1)

                apply(0)
                high(0)
                context()
                apply(1)
                maxima(0)
                self_exps()
                for i in range(PB):
                    if i:
                        maxima(i)
                        exps(i, 0)
                        if i % 2:
                            if i + 1 < PB:
                                apply(i + 1)
                                apply(i + 2)
                            exps(i, 1)
                        if i + 1 < PB:
                            high(i + 1)
                        if i % 2 == 0:
                            exps(i, 1)
                    else:
                        high(1)
                    if i + 1 < PB:
                        queries_high(i + 1)

            for ph in phases:
                fence(act, "act", ph["n"])
                {"T": tokens, "E": experts, "C": lambda ph: None, "A": attention}[ph["kind"]](ph)
                if ph["kind"] != "T":
                    act.drain().then_inc(phase_done["act"].sem, 1)

        @block.vector
        def _(dve):
            for sig in (ln_stats, ln_small, tr_low, logits_dve, gu_hid, t_out, e_low, e_hid, e_ht, c_out, a_low,
                        a_ql, a_den, a_norm, a_out, x_mx, s_kl, s_hm, s_ckl, s_mx):
                dve.sem_inc(sig.sem, sig.head * sig.per)

            def tokens(ph):
                par = ph["par"]

                def rows_statistics(i):
                    dve.wait_ge(token_in[i].sem, 16 * (ph["r"] + 1))
                    statistics(ring[:, i], i)

                def low(i, s):
                    g, k = ph["t"] + i, s % 2
                    dve.wait_ge(tr_high.sem, tr_high.done(g))
                    dve.tensor_tensor(flat(xt_l[:, k]), bank[k][:], flat(xt_h[:, k]).bitcast(F32), ALU.subtract)\
                        .then_inc(tr_low.sem, 1)

                def bias(i, s):
                    g = ph["t"] + i
                    dve.wait_ge(logits_pe.sem, logits_pe.done(g))
                    dve.tensor_tensor(logits[:, ds(2 * i, 2), :],
                                      bank[4][:, 0:2 * NE].rearrange("p (t e) -> p t e", t=2),
                                      rb[:].unsqueeze(1).broadcast_to([P, 2, NE]), ALU.add)\
                        .then_inc(logits_dve.sem, 1)

                def hidden(i, s):
                    g = ph["t"] + i
                    for h in range(SH // P):
                        dve.wait_ge(gu_tanh.sem, gu_tanh.done(g, h + 1))
                        dve.scalar_tensor_tensor(th[:, h], th[:, h], 1.0, bank[2 + h][:, 0:2 * P], ALU.add, ALU.mult)\
                            .then_inc(gu_hid.sem, 1)
                        dve.wait_ge(gu_hid.sem, gu_hid.done(g, 2 * h + 1))
                        dve.wait_ge(dn_pe.sem, dn_pe.freed(g, 2))
                        dve.tensor_tensor(work[:, 1 + i % 2, h], th[:, h], bank[2 + h][:, 2 * P:4 * P], ALU.mult)\
                            .then_inc(gu_hid.sem, 1)

                def sums(i, s):
                    g = ph["t"] + i
                    dve.wait_ge(dn_pe.sem, dn_pe.done(g))
                    dve.scalar_tensor_tensor(flat(ring[:, i]), bank[6 + s % 2][:], 0.25, flat(ring[:, i]),
                                             ALU.mult, ALU.add).then_inc(t_out.sem, 1)

                rows_statistics(0)
                rows_statistics(1)
                layer_norm(ph, 0)
                for i in range(2, 5):
                    rows_statistics(i)
                for i in range(PB + 2):
                    if i < PB:
                        low(i, i % NS)
                    if i == 0:
                        for n in range(5, PB):
                            rows_statistics(n)
                        layer_norm(ph, 2)
                    if 1 <= i <= PB:
                        bias(i - 1, (i - 1) % NS)
                        hidden(i - 1, (i - 1) % NS)
                    if i >= 2:
                        sums(i - 2, (i - 2) % NS)
                        if "last" in ph:
                            last_sums(ph["last"], i - 2, i % 2)
                dve.drain().then_inc(phase_done["dve"].sem, 1)
                routing(ph)

            def statistics(x, i):
                for t in range(2):
                    dve.bn_stats(bst[:, i, t, :], x[:, t, :]).then_inc(ln_stats.sem, 1)

            def layer_norm(ph, i):
                g = ln_group(ph, i)
                k = slice(*LN_GROUPS[ph["kind"]][g - ph["ln_groups"]])
                even, odd = bst[:, k, :, 0:3], bst[:, k, :, 3:6]

                def small(n, ins):
                    ins.then_inc(ln_small.sem, 1)

                def after(n):
                    dve.wait_ge(ln_small.sem, ln_small.done(g, n))

                dve.wait_ge(ln_stats.sem, ln_stats.done(ph["ln"] + k.stop - 1))
                small(1, dve.tensor_tensor(lnd[:, k], even[:, :, :, 1], odd[:, :, :, 1], ALU.subtract))
                small(2, dve.tensor_tensor(lnm[:, k], even[:, :, :, 1], odd[:, :, :, 1], ALU.add))
                small(3, dve.tensor_tensor(lnv[:, k], even[:, :, :, 2], odd[:, :, :, 2], ALU.add))
                after(1)
                small(4, dve.scalar_tensor_tensor(lnw[:, k], lnd[:, k], 0.25, lnd[:, k], ALU.mult, ALU.mult))
                after(3)
                small(5, dve.tensor_scalar(lnv[:, k], lnv[:, k], 1.0 / D, EPS, ALU.mult, ALU.add))
                after(5)
                small(6, dve.tensor_tensor(lnv[:, k], lnv[:, k], lnw[:, k], ALU.add))
                after(6)
                small(7, dve.tensor_scalar(rstd[:, k].bitcast(I32), lnv[:, k].bitcast(I32), -0.5, RSQRT_GUESS,
                                           ALU.mult, ALU.add))
                n = 7
                for _ in range(NEWTON):
                    after(n)
                    small(n + 1, dve.tensor_tensor(rsq[:, k], rstd[:, k], rstd[:, k], ALU.mult))
                    after(n + 1)
                    small(n + 2, dve.scalar_tensor_tensor(rsq[:, k], rsq[:, k], -0.5, lnv[:, k], ALU.mult, ALU.mult))
                    after(n + 2)
                    small(n + 3, dve.scalar_tensor_tensor(rstd[:, k], rsq[:, k], 1.5, rstd[:, k], ALU.add, ALU.mult))
                    n += 3
                after(n)
                small(n + 1, dve.scalar_tensor_tensor(lnb[:, k], lnm[:, k], -0.5, rstd[:, k], ALU.mult, ALU.mult))
                assert n + 1 == LN_STEPS

            def routing(ph):
                par = ph["par"]
                start = ph["r"] * ROUTE
                n = [0]

                def step(ins):
                    n[0] += 1
                    ins.then_inc(route.sem, 1)
                    return n[0]

                def after(k):
                    dve.wait_ge(route.sem, start + k)

                dve.wait_ge(logits_dve.sem, logits_dve.done(ph["t"] + PB - 1))
                for t in range(TB):
                    a = step(dve.max(top[:, t, :], logits[:, t, :]))
                after(a)
                for t in range(TB):
                    a = step(dve.max_index(topi[:, t, :], top[:, t, :], logits[:, t, :]))
                d = step(dve.tensor_tensor(wexp[:, 0, :], top[:, :, 1], top[:, :, 0], ALU.subtract))
                assert d == ROUTE_D
                after(a)
                a = step(dve.tensor_copy(topf[:].rearrange("p k t -> p t k"), topi[:, :, 0:2]))
                after(a)
                for k in range(2):
                    a = step(dve.tensor_tensor(onehot[:, k], iota_f[:, 0:NE].unsqueeze(2).broadcast_to([P, NE, TB]),
                                               topf[:, k, :].unsqueeze(1).broadcast_to([P, NE, TB]), ALU.is_equal))
                after(a)
                a = step(dve.tensor_tensor(flat(picked[:]), flat(onehot[:, 0]), flat(onehot[:, 1]), ALU.add))
                assert a == ROUTE_PICKED
                dve.wait_ge(route_pe.sem, ph["r"] + 1)
                before, totals = bank[4][:, 0:NE * TB], bank[4][:, NE * TB:2 * NE * TB]
                a = step(dve.tensor_copy(flat(tot[:]), totals))
                after(a)
                step(dve.tensor_tensor(flat(rank[:]), before, flat(tot[:]), ALU.subtract))
                a = step(dve.tensor_tensor_scan(flat(incl[:]), flat(restart[:]), flat(tot[:]), 0.0, ALU.mult, ALU.add))
                after(a)
                step(dve.tensor_tensor(flat(rank[:]), flat(rank[:]), flat(incl[:]), ALU.add))
                a = step(dve.tensor_scalar(tiles_of[:], incl[:, :, TB - 1], (P - 1) / 2, 1.0 / P, ALU.add, ALU.mult))
                after(a)
                a = step(dve.tensor_scalar(tiles_of[:], tiles_of[:], ROUND, None, ALU.add))
                after(a)
                a = step(dve.tensor_scalar(tiles_of[:], tiles_of[:], -ROUND, None, ALU.add))
                after(a)
                a = step(dve.tensor_tensor_scan(tiles_in[:], ones_f[:, 0:NE], tiles_of[:], 0.0, ALU.mult, ALU.add))
                after(a)
                a = step(dve.tensor_tensor(base[:], tiles_in[:], tiles_of[:], ALU.subtract))
                after(a)
                a = step(dve.scalar_tensor_tensor(rank[:], base[:].unsqueeze(2).broadcast_to([P, NE, TB]), float(P),
                                                  rank[:], ALU.mult, ALU.add))
                after(a)
                for k in range(2):
                    a = step(dve.tensor_tensor(flat(onehot[:, k]), flat(onehot[:, k]), flat(rank[:]), ALU.mult))
                after(a)
                for k in range(2):
                    a = step(dve.tensor_reduce(slotf[:, k, :], onehot[:, k].rearrange("p e t -> p t e"), AX.X, ALU.add))
                after(a)
                dve.tensor_copy(slot[:, par], slotf[:]).then_inc(routed.sem, 1)
                dve.wait_ge(route_act.sem, ph["r"] + 1)
                a = step(dve.tensor_scalar(wexp[:, 2, :], wexp[:, 1, :], 1.0, None, ALU.add))
                after(a)
                a = step(dve.reciprocal(wexp[:, 2, :], wexp[:, 2, :]))
                after(a)
                step(dve.tensor_scalar(wts[:, par, 0, :], wexp[:, 2, :], 0.25, None, ALU.mult))
                step(dve.scalar_tensor_tensor(wts[:, par, 1, :], wexp[:, 1, :], 0.25, wexp[:, 2, :], ALU.mult, ALU.mult))
                a = step(dve.tensor_tensor(cmpb[:], iota_f[0:1, :].unsqueeze(2).broadcast_to([1, ET, NE]),
                                           tiles_in[0:1, :].unsqueeze(1).broadcast_to([1, ET, NE]), ALU.is_ge))
                after(a)
                mine = texp[:, par * ET:(par + 1) * ET]
                a = step(dve.tensor_reduce(mine, cmpb[:], AX.X, ALU.add))
                after(a)
                a = step(dve.tensor_scalar(mine, mine, NE - 1.0, None, ALU.min))
                first, end = (0, EP - 2) if par == 0 else (EP - 2, E2 - 2)
                word = route_work[0:1, 0:end - first]
                tiles = texp[:].rearrange("a (p t) -> a p t", t=2)
                for m in range(4, -1, -1):
                    after(a)
                    high = tiles[:, first + 2:end + 2, 1] if m == 4 else word
                    a = step(dve.scalar_tensor_tensor(word, high, float(NE), tiles[:, first + m // 2:end + m // 2, m % 2],
                                                      ALU.mult, ALU.add))
                after(a)
                dve.tensor_copy(table[:, first:end], word).then_inc(table_ready.sem, 1)
                assert n[0] == ROUTE

            def experts(ph):
                def low(i, s):
                    g, k = ph["e"] + i, s % 2
                    dve.wait_ge(e_high.sem, e_high.done(g))
                    dve.tensor_tensor(flat(xt_l[:, k]), bank[k][:], flat(xt_h[:, k]).bitcast(F32), ALU.subtract)\
                        .then_inc(e_low.sem, 1)

                def hidden(i, s):
                    g, k = ph["e"] + i, s % 2
                    gu = bank[2 + k][:].rearrange("p (t m n) -> p t m n", t=2, m=2)
                    t_ = th[:, k].rearrange("p (t n) -> p t n", t=2)
                    dve.wait_ge(e_tanh.sem, e_tanh.done(g))
                    dve.scalar_tensor_tensor(t_, t_, 1.0, gu[:, :, 0, :], ALU.add, ALU.mult).then_inc(e_hid.sem, 1)
                    dve.wait_ge(e_hid.sem, e_hid.done(g, 1))
                    dve.wait_ge(e_htr.sem, e_htr.freed(g, 2))
                    dve.tensor_tensor(hid[:, k].rearrange("p (t n) -> p t n", t=2), t_, gu[:, :, 1, :], ALU.mult)\
                        .then_inc(e_hid.sem, 1)

                def turned(i, s):
                    g, k = ph["e"] + i, s % 2
                    dve.wait_ge(e_htr.sem, e_htr.done(g))
                    dve.wait_ge(e_dn.sem, e_dn.freed(g, 2))
                    dve.tensor_copy(ht[:, k], bank[4 + k][:, 0:2 * P]).then_inc(e_ht.sem, 1)

                def sum_two(j):
                    for s in range(2):
                        last_sums(ph["last"], 2 * j + s, s)

                spans = [(E2 // NS - 1 - PB // 2, None, None), (PB // 2, sum_two, None)] if "last" in ph else None
                steps(dve, E2, [(0, low), (1, hidden), (2, turned)], spans=spans)

            def combine_pair(par, i, s, g, src, dst):
                dve.wait_ge(gathered[s % 2].sem, (g - s % 2) * 32 + 64)
                add_results(gath[par][:, s % 2], par, i, g, src, dst)

            def add_results(results, par, i, g, src, dst):
                for t in range(2):
                    dve.scalar_tensor_tensor(src(t), results[:, t, 0, :],
                                             wts[:, par, 0, ds(2 * i + t, 1)], src(t),
                                             ALU.mult, ALU.add).then_inc(c_out.sem, 1)
                for t in range(2):
                    dve.wait_ge(c_out.sem, c_out.done(g, 1 + t))
                    dve.scalar_tensor_tensor(dst(t), results[:, t, 1, :],
                                             wts[:, par, 1, ds(2 * i + t, 1)], src(t),
                                             ALU.mult, ALU.add).then_inc(c_out.sem, 1)

            def last_sums(last, i, s):
                buf = cx[last["par"]]
                dve.wait_ge(sums_in[s].sem, (last["before"] + i - s) * 8 + 16)
                combine_pair(last["par"], i, s, last["c"] + i, lambda t: buf[:, s, t, :], lambda t: buf[:, s, t, :])

            def combine(ph):
                for i in range(PB):
                    dve.wait_ge(token_in[i].sem, 16 * (count["R"] + 1))
                    dve.wait_ge(finals_in[i].sem, 64)
                    add_results(finals(i), ph["par"], i, ph["c"] + i, lambda t: ring[:, i, t, :],
                                lambda t: ring[:, i, t, :])

            def attention(ph):
                def ready(i):
                    s, g = i % NS, ph["c"] + i
                    dve.wait_ge(rows_in[s].sem, used(ph, i, s))
                    combine_pair(ph["par"], i, s, g, lambda t: rows[:, s, t, :],
                                 lambda t: xa(ph["par"], i)[:, t, :])
                    dve.wait_ge(c_out.sem, c_out.done(g))
                    statistics(xa(ph["par"], i), i)

                def low(i):
                    a = ph["a"] + i
                    dve.wait_ge(a_high.sem, a_high.done(a))
                    if i == 0:
                        dve.wait_ge(s_xf.sem, s_xf.done(a // PB))
                    dve.tensor_tensor(flat(xt_l[:, 0]), bank[0][:], flat(xt_h[:, 0]).bitcast(F32), ALU.subtract)\
                        .then_inc(a_low.sem, 1)

                def queries_low(i):
                    a = ph["a"] + i
                    dve.wait_ge(a_qh.sem, a_qh.done(a))
                    dve.tensor_tensor(flat(q_l[:, 0]), bank[1][:], flat(q_h[:, 0]).bitcast(F32), ALU.subtract)\
                        .then_inc(a_ql.sem, 2)

                def maxima(i):
                    a = ph["a"] + i
                    x = a - a // PB - 1
                    dve.wait_ge(a_mtr.sem, a_mtr.freed(a, 1))
                    for n in range(4):
                        dve.wait_ge(x_sm.sem, x_sm.done(x, n + 1))
                        dve.tensor_reduce(mx[:, :, 32 * n:32 * n + 4],
                                          bank[2 + n][:].rearrange("p (t h k) -> p t h k", t=2, h=4),
                                          AX.X, ALU.max).then_inc(x_mx.sem, 1)

                def norm(i):
                    a = ph["a"] + i
                    if i == 0:
                        dve.wait_ge(s_pv.sem, s_pv.done(a // PB))
                    else:
                        dve.wait_ge(x_pv.sem, x_pv.done(a - a // PB - 1))
                        dve.wait_ge(a_wo.sem, a_wo.freed(a, 1))
                    dve.reciprocal(flat(xt_f), bank[7][:]).then_inc(a_den.sem, 1)
                    dve.wait_ge(a_den.sem, a_den.done(a))
                    dve.tensor_tensor(flat(xt_f), bank[6][:], flat(xt_f), ALU.mult).then_inc(a_norm.sem, 1)

                def add(i):
                    a, s = ph["a"] + i, i % NS
                    dve.wait_ge(a_wo.sem, a_wo.done(a))
                    dve.wait_ge(outs_stored[s].sem, used(ph, i, s) - 16)
                    dve.tensor_tensor(flat(outs[:, s]), bank[0][:], flat(xa(ph["par"], i)[:]), ALU.add)\
                        .then_inc(a_out.sem, 1)

                def context(b):
                    dve.wait_ge(s_kh.sem, s_kh.done(b))
                    dve.tensor_tensor(flat(k_l[:]), bank[2][:], flat(k_h[:]).bitcast(F32), ALU.subtract)\
                        .then_inc(s_kl.sem, 1)
                    dve.wait_ge(s_hc.sem, s_hc.done(b))
                    dve.tensor_reduce(hm[:], hc[:].rearrange("p (n r) -> p n r", r=CTX // CK), AX.X, ALU.add)\
                        .then_inc(s_hm.sem, 1)
                    dve.wait_ge(a_qh.sem, a_qh.done(ph["a"]))
                    for m in range(2):
                        dve.scalar_tensor_tensor(flat(q_l[:, m]), bank[1][:], parity[:, m:m + 1],
                                                 flat(q_h[:, m]).bitcast(F32), ALU.mult, ALU.subtract)\
                            .then_inc(a_ql.sem, 1)
                    dve.wait_ge(a_mtr.sem, a_mtr.freed(ph["a"], 1))
                    for n in range(12):
                        if n == 4:
                            layer_norm(ph, 1)
                        if n == 8:
                            dve.wait_ge(s_ckh.sem, s_ckh.done(b))
                            keys = bank[7][:, 6 * CK:8 * CK].rearrange("p (k n) -> p k n", k=KC)
                            for m in range(2):
                                ins = dve.scalar_tensor_tensor(kc_l[:, :, m * CK:(m + 1) * CK], keys, parity[:, m:m + 1],
                                                               kc_h[:, :, m * CK:(m + 1) * CK].bitcast(F32),
                                                               ALU.mult, ALU.subtract)
                            ins.then_inc(s_ckl.sem, 1)
                        t, w = (0, 4) if n < 4 else (1, 2)
                        h0 = 32 * (n % 4) + 2 * (n // 8)
                        dve.wait_ge(s_sm.sem, s_sm.done(b, n + 1))
                        dve.tensor_reduce(mx[:, t, h0:h0 + w], bank[2 + n % 4][:].rearrange("p (h k) -> p h k", h=w),
                                          AX.X, ALU.max).then_inc(s_mx.sem, 1)

                ready(0)
                layer_norm(ph, 0)
                ready(1)
                low(0)
                context(ph["a"] // PB)
                ready(2)
                ready(3)
                layer_norm(ph, 2)
                low(1)
                queries_low(1)
                maxima(1)
                for i in range(1, PB):
                    norm(i - 1)
                    if i + 1 < PB:
                        low(i + 1)
                    if i + 3 < PB:
                        ready(i + 3)
                    if i + 1 < PB:
                        queries_low(i + 1)
                    if i + 1 < PB:
                        maxima(i + 1)
                    add(i - 1)
                    if i % 2 == 0 and i + 2 < PB:
                        layer_norm(ph, i + 2)
                norm(PB - 1)
                add(PB - 1)

            dve.wait_ge(gp_step.sem, GP_STEPS)
            dve.tensor_reduce(parity[:, 0:1], cmask, AX.X, ALU.add).then_inc(parity_step.sem, 1)
            dve.wait_ge(parity_step.sem, 1)
            dve.tensor_scalar(parity[:, 1:2], parity[:, 0:1], -1.0, 1.0, ALU.mult, ALU.add).then_inc(parity_step.sem, 1)

            for ph in phases:
                fence(dve, "dve", ph["n"])
                {"T": tokens, "E": experts, "C": combine, "A": attention}[ph["kind"]](ph)
                if ph["kind"] != "T":
                    dve.drain().then_inc(phase_done["dve"].sem, 1)

        @block.tensor
        def _(pe):
            for sig in (tr_pe, logits_pe, gu_pe, dn_pe, e_tr, e_gu, e_htr, e_dn, a_tr, a_q, a_mtr,
                        a_wo, x_sm, x_st, x_pv, s_kv, s_h, s_cp, s_ckv, s_sm, s_st, s_pv):
                pe.sem_inc(sig.sem, sig.head * sig.per)
            pe.wait_ge(gp_step.sem, GP_STEPS)
            pe.wait_ge(consts.sem, 1)

            def turned(out_, in_):
                return pe.transpose(out_, in_, ident[:])

            def turn_pair(src, b, last_sem):
                for k in range(KC):
                    for t in range(2):
                        m = turned(bank[b][:, (2 * k + t) * P:(2 * k + t + 1) * P], src(t, k))
                m.then_inc(last_sem, 1)

            def three(out_, lh, ll, rh, rl, first, last):
                pe.matmul(out_, lh, rh, start=first, stop=False)
                pe.matmul(out_, lh, rl, start=False, stop=False)
                return pe.matmul(out_, ll, rh, start=False, stop=last)

            def tokens(ph):
                par = ph["par"]

                def turn(i, s):
                    g, k = ph["t"] + i, s % 2
                    pe.wait_ge(ln_rows.sem, ln_rows.done(ph["ln"] + i))
                    pe.wait_ge(tr_low.sem, tr_low.freed(g, 2))
                    turn_pair(lambda t, c: xn[:, par, ds(2 * i + t, 1), c * P:(c + 1) * P].rearrange("p a d -> p (a d)"),
                              k, tr_pe.sem)

                def gate_up(i, s):
                    g, k = ph["t"] + i, s % 2
                    pe.wait_ge(tr_low.sem, tr_low.done(g))
                    if isinstance(i, int) and i == 0:
                        pe.wait_ge(raw_split.sem, raw_split.done(1))
                        pe.wait_ge(router_split.sem, 2)
                        pe.wait_ge(weights_in.sem, 16 * 3)
                    pe.wait_ge(logits_dve.sem, logits_dve.freed(g, 1))
                    for t in range(2):
                        for c in range(KC):
                            m = three(bank[4][:, t * NE:(t + 1) * NE],
                                      xt_h[:, k, c, t * P:(t + 1) * P], xt_l[:, k, c, t * P:(t + 1) * P],
                                      rw_h[:, c, :], rw_l[:, c, :], c == 0, c == KC - 1)
                    m.then_inc(logits_pe.sem, 1)
                    for h in range(SH // P):
                        pe.wait_ge(gu_hid.sem, gu_hid.done(g - 1, 2 * h + 2))
                        for m_ in range(2):
                            for c in range(KC):
                                m = three(bank[2 + h][:, m_ * 2 * P:(m_ + 1) * 2 * P],
                                          sg_h[:, m_, c, h * P:(h + 1) * P], sg_l[:, m_, c, h * P:(h + 1) * P],
                                          xt_h[:, k, c, :], xt_l[:, k, c, :], c == 0, c == KC - 1)
                        m.then_inc(gu_pe.sem, 1)

                def down_(i, s):
                    g = ph["t"] + i
                    pe.wait_ge(gu_hid.sem, gu_hid.done(g))
                    pe.wait_ge(t_out.sem, t_out.freed(g, 2))
                    for t in range(2):
                        for h in range(SH // P):
                            m = pe.matmul(bank[6 + s % 2][:, t * D:(t + 1) * D], work[:, 1 + i % 2, h, t * P:(t + 1) * P],
                                          sd[:, h, :], start=h == 0, stop=h == SH // P - 1)
                    m.then_inc(dn_pe.sem, 1)

                for i in range(PB + 2):
                    if i < PB:
                        turn(i, i % NS)
                    if 1 <= i <= PB:
                        gate_up(i - 1, (i - 1) % NS)
                    if i >= 2:
                        down_(i - 2, (i - 2) % NS)
                pe.drain().then_inc(phase_done["pe"].sem, 1)
                pe.wait_ge(route.sem, ph["r"] * ROUTE + ROUTE_PICKED)
                pe.matmul(bank[4][:, 0:NE * TB], below[:], flat(picked[:]), start=True, stop=True)
                pe.matmul(bank[4][:, NE * TB:2 * NE * TB], ones_b[:], flat(picked[:]), start=True, stop=True)\
                    .then_inc(route_pe.sem, 1)

            def experts(ph):
                par = ph["par"]
                pe.wait_ge(table_ready.sem, 2 * (ph["r"] + 1))
                if ph["r"] == 0:
                    pe.wait_ge(raw_split.sem, raw_split.done(NE + 1))
                    pe.wait_ge(weights_in.sem, 16 * 4)

                mine = {}

                def turn_of(s, lag):
                    return (s + lag) % NS - lag

                def look_up(i, inside):
                    first = i - 3 if inside else {0: 0, E2: E2 - 3}[i]
                    n = 2 if inside else 1
                    words = [nc.values_load_multi_w_load_instructions(
                        table[0:1, ds(first + 3 * k, 1)], engines=[mybir.EngineType.PE],
                        min_val=0, max_val=NE ** 6 - 1)[1][0] for k in range(n)]
                    mine["of"] = {first - i + k if not inside else k - 3:
                                  [((words[k // 3] >> 4 * (2 * (k % 3) + t)) & (NE - 1))
                                   for t in range(2)] for k in range(3 * n)}

                def turn(i, s):
                    g, k = ph["e"] + i, s % 2
                    pe.wait_ge(rows_in[s].sem, used(ph, i, s))
                    pe.wait_ge(e_low.sem, e_low.freed(g, 2))
                    turn_pair(lambda t, c: rows[:, s, t, c * P:(c + 1) * P], k, e_tr.sem)

                def gate_up(i, s):
                    g, k = ph["e"] + i, s % 2
                    pe.wait_ge(e_low.sem, e_low.done(g))
                    pe.wait_ge(e_hid.sem, e_hid.freed(g, 2))
                    for t, e in enumerate(mine["of"][turn_of(s, 1)]):
                        wh = eg_h[:, ds(e, 1)].rearrange("p a k n -> p (a k) n")
                        wl = eg_l[:, ds(e, 1)].rearrange("p a k n -> p (a k) n")
                        for c in range(KC):
                            m = three(bank[2 + k][:, t * 2 * EH:(t + 1) * 2 * EH],
                                      xt_h[:, k, c, t * P:(t + 1) * P], xt_l[:, k, c, t * P:(t + 1) * P],
                                      wh[:, c, :], wl[:, c, :], c == 0, c == KC - 1)
                    m.then_inc(e_gu.sem, 1)

                def turn_hidden(i, s):
                    g, k = ph["e"] + i, s % 2
                    pe.wait_ge(e_hid.sem, e_hid.done(g))
                    pe.wait_ge(e_ht.sem, e_ht.freed(g, 2))
                    for t in range(2):
                        m = turned(bank[4 + k][:, t * P:(t + 1) * P], hid[:, k, t * P:(t + 1) * P])
                    m.then_inc(e_htr.sem, 1)

                def down_(i, s):
                    g, k = ph["e"] + i, s % 2
                    pe.wait_ge(e_ht.sem, e_ht.done(g))
                    pe.wait_ge(e_out.sem, e_out.freed(g, 2))
                    for t, e in enumerate(mine["of"][turn_of(s, 3)]):
                        m = pe.matmul(bank[6 + k][:, t * D:(t + 1) * D], ht[:, k, t * P:(t + 1) * P],
                                      ed[:, ds(e, 1), :].rearrange("p a d -> p (a d)"), start=True, stop=True)
                    m.then_inc(e_dn.sem, 1)

                steps(pe, E2, [(0, turn), (2, turn_hidden), (1, gate_up), (3, down_)], look_up)

            def attention(ph):
                if ph["a"] == 0:
                    pe.wait_ge(attn_in.sem, 16 * 8)
                    pe.wait_ge(raw_split.sem, raw_split.done(NE + 2))
                    pe.wait_ge(parity_step.sem, 2)
                b = ph["a"] // PB
                rows_turned(ph, 0)
                queries(ph, 0)
                context(b)
                self_scores(ph["a"], b, 0)
                compressed(b)
                self_scores(ph["a"], b, 1)
                compressed_keys_values(b)
                self_scores(ph["a"], b, 2)
                self_scores_turned(ph["a"], b)
                rows_turned(ph, 1)
                queries(ph, 1)
                scores(ph, 1)
                for i in range(1, PB):
                    turn_maxima(ph["a"] + i)
                    scores_turned(ph, i, 0)
                    if i % 2:
                        scores_turned(ph, i, 1)
                    if i + 1 < PB:
                        rows_turned(ph, i + 1)
                    if i % 2 == 0:
                        scores_turned(ph, i, 1)
                    if i + 1 < PB:
                        queries(ph, i + 1)
                    values(ph, i)
                    if i + 1 < PB:
                        scores(ph, i + 1)
                    output(ph, i - 1)
                output(ph, PB - 1)

            def rows_turned(ph, i):
                a = ph["a"] + i
                pe.wait_ge(ln_rows.sem, ln_rows.done(ph["ln"] + i))
                pe.wait_ge(a_mt.sem, a_mt.freed(a, 1))
                turn_pair(lambda t, c: xln[:, i % 2, t, c * P:(c + 1) * P], 0, a_tr.sem)

            def queries(ph, i):
                a = ph["a"] + i
                pe.wait_ge(a_low.sem, a_low.done(a))
                pe.wait_ge(a_ql.sem, a_ql.freed(a, 1))
                for c in range(KC):
                    for k in range(KC):
                        m = three(bank[1][:, c * 2 * P:(c + 1) * 2 * P],
                                  wq_h[:, k, c * P:(c + 1) * P], wq_l[:, k, c * P:(c + 1) * P],
                                  xt_h[:, 0, k, :], xt_l[:, 0, k, :], k == 0, k == KC - 1)
                m.then_inc(a_q.sem, 1)

            def output(ph, i):
                a = ph["a"] + i
                pe.wait_ge(a_norm.sem, a_norm.done(a))
                if i + 2 < PB:
                    pe.wait_ge(a_low.sem, a_low.done(a + 2))
                for t in range(2):
                    for k in range(KC):
                        m = pe.matmul(bank[0][:, t * D:(t + 1) * D], xt_f[:, k, t * P:(t + 1) * P], wo_s[:, k, :],
                                      start=k == 0, stop=k == KC - 1)
                m.then_inc(a_wo.sem, 1)

            def context(b):
                pe.wait_ge(s_xf.sem, s_xf.done(b))
                for c in range(KC):
                    for k in range(KC):
                        m = pe.matmul(bank[2][:, c * CTX:(c + 1) * CTX], wk_s[:, k, c * P:(c + 1) * P], xf[:, k, :],
                                      start=k == 0, stop=k == KC - 1)
                m.then_inc(s_kv.sem, 1)
                for k in range(KC):
                    m = pe.matmul(bank[7][:, 0:CTX], w1_s[:, k, :], xf[:, k, :], start=k == 0, stop=k == KC - 1)
                m.then_inc(s_h.sem, 1)
                for t in range(2):
                    for k in range(KC):
                        m = pe.matmul(bank[6][:, t * D:(t + 1) * D], xf[:, k, t * P:(t + 1) * P], wv_s[:, k, :],
                                      start=k == 0, stop=k == KC - 1)
                m.then_inc(s_kv.sem, 1)

            def compressed(b):
                pe.wait_ge(s_hm.sem, s_hm.done(b))
                for k in range(KC):
                    m = pe.matmul(bank[7][:, CTX + k * CK:CTX + (k + 1) * CK], w2_s[:, k * P:(k + 1) * P], hm[:],
                                  start=True, stop=True)
                m.then_inc(s_cp.sem, 1)

            def compressed_keys_values(b):
                pe.wait_ge(s_cm.sem, s_cm.done(b))
                for c in range(KC):
                    for k in range(KC):
                        m = pe.matmul(bank[7][:, (6 + c) * CK:(7 + c) * CK], wk_s[:, k, c * P:(c + 1) * P], cm[:, k, 0, :],
                                      start=k == 0, stop=k == KC - 1)
                m.then_inc(s_ckv.sem, 1)
                pe.wait_ge(s_va.sem, s_va.done(b))
                for k in range(KC):
                    m = pe.matmul(bank[6][:, 0:D], flat(cm[:, k]), wv_s[:, k, :], start=k == 0, stop=k == KC - 1)
                m.then_inc(s_ckv.sem, 1)

            def turn_maxima(a):
                if a % PB:
                    pe.wait_ge(x_mx.sem, x_mx.done(a - a // PB - 1))
                    pe.wait_ge(a_out.sem, a_out.freed(a, 2))
                for t in range(2):
                    m = turned(bank[0][:, t * P:(t + 1) * P], mx[:, t, :])
                m.then_inc(a_mtr.sem, 1)

            group = [slice(32 * g, 32 * g + 32) for g in range(4)]

            def minus_max(g, out_, heads, cols, last):
                h, n = heads
                w = minus[group[g], h * CK:(h + n) * CK] if n > 1 else \
                    minus[group[g], h * CK:h * CK + 1].broadcast_to([32, P])
                return pe.matmul(out_, w, mt[group[g], cols], start=False, stop=last)

            def self_scores(a, b, w):
                t = int(w > 0)
                keys = (t + 1) * P
                heads = [(c, m_) for c in range(2) for m_ in range(2)] if t == 0 else [(w - 1, m_) for m_ in range(2)]
                if w == 0:
                    pe.wait_ge(a_qh.sem, a_qh.done(a))
                    pe.wait_ge(s_kl.sem, s_kl.done(b))
                for g in range(4):
                    if w:
                        pe.wait_ge(s_mx.sem, s_mx.done(b, 4 * w - 3 + g))
                for j, (c, m_) in enumerate(heads):
                    for g in range(4):
                        pe.matmul(bank[2 + g][:, j * keys:(j + 1) * keys], q_h[group[g], m_, c, t * P:(t + 1) * P],
                                  k_h[group[g], c, 0:keys], start=True, stop=False)
                    for g in range(4):
                        m = pe.matmul(bank[2 + g][:, (j + 1) * keys - P:(j + 1) * keys], ident_b[:], mask_q[:],
                                      start=False, stop=True)
                        if j == len(heads) - 1:
                            m.then_inc(s_sm.sem, 1)

            def self_scores_turned(a, b):
                pe.wait_ge(a_ql.sem, a_ql.done(a))
                pe.wait_ge(s_ckl.sem, s_ckl.done(b))
                pe.wait_ge(s_vc.sem, s_vc.done(b))
                pe.wait_ge(s_mx.sem, s_mx.done(b))
                turn_maxima(a)
                pe.wait_ge(a_mt.sem, a_mt.done(a))
                waves = [(c, m_) for c in range(2) for m_ in range(2)]

                def score(w, half):
                    c, m_ = waves[w]
                    parts = ((0, slice(0, 2 * P), slice(0, 2 * P)), (1, slice(P, 2 * P), slice(2 * P, 3 * P)))
                    for t, queries_, cols in parts:
                        keys = slice(t * P, (t + 1) * P)
                        for n, (k_, q_) in enumerate(((k_h, q_h), (k_h, q_l), (k_l, q_h))):
                            for g in (2 * half, 2 * half + 1):
                                if w and t == 0 and n == 0:
                                    pe.wait_ge(s_exp.sem, s_exp.done(b, 4 * w - 3 + g))
                                pe.matmul(bank[2 + g][:, cols], k_[group[g], c, keys], q_[group[g], m_, c, queries_],
                                          start=n == 0, stop=False)
                        for g in (2 * half, 2 * half + 1):
                            minus_max(g, bank[2 + g][:, cols], (2 * c + m_, 1), queries_, False)
                        for g in (2 * half, 2 * half + 1):
                            m = pe.matmul(bank[2 + g][:, cols.start:cols.start + P], ident_b[:], mask_k[:],
                                          start=False, stop=True)
                            if t:
                                m.then_inc(s_st.sem, 1)

                def value(w):
                    c, m_ = waves[w]
                    o = c * 2 * P
                    for out_, w0, w1 in ((bank[6], lambda g: flat(va[:, 0, 4 * c + g, m_]), lambda g: flat(va[:, 1, 4 * c + g, m_])),
                                         (bank[7], lambda g: sumk[:, m_, :], lambda g: sumk[:, m_, :])):
                        for g in range(4):
                            pe.wait_ge(s_exp.sem, s_exp.done(b, 4 * w + g + 1))
                            pe.matmul(out_[group[g], o:o + 2 * P], w0(g), pt[:, g, 0:2 * P], start=m_ == 0, stop=False)
                        for g in range(4):
                            m = pe.matmul(out_[group[g], o + P:o + 2 * P], w1(g), pt[:, g, 2 * P:3 * P],
                                          start=False, stop=m_ == 1)
                            if out_ is bank[7]:
                                m.then_inc(s_pv.sem, 1)

                score(0, 0)
                score(0, 1)
                for w in range(1, 4):
                    score(w, 0)
                    value(w - 1)
                    score(w, 1)
                value(3)

            def scores(ph, i):
                a = ph["a"] + i
                b = a // PB
                pe.wait_ge(a_ql.sem, a_ql.done(a))
                if i == 1:
                    pe.wait_ge(s_exp.sem, s_exp.done(b))
                else:
                    pe.wait_ge(x_exp.sem, x_exp.done(a - b - 2))
                for t in range(2):
                    for c in range(2):
                        for g in range(4):
                            m = pe.matmul(bank[2 + g][:, (2 * t + c) * P:(2 * t + c + 1) * P],
                                          q_h[group[g], 0, c, t * P:(t + 1) * P], kc_h[group[g], c, :],
                                          start=True, stop=True)
                            if t and c:
                                m.then_inc(x_sm.sem, 1)

            def scores_turned(ph, i, half):
                for c in range(2):
                    cols = slice(c * 2 * P, (c + 1) * 2 * P)
                    for n, (k_, q_) in enumerate(((kc_h, q_h), (kc_h, q_l), (kc_l, q_h))):
                        for g in (2 * half, 2 * half + 1):
                            pe.matmul(bank[2 + g][:, cols], k_[group[g], c, :], q_[group[g], 0, c, :],
                                      start=n == 0, stop=False)
                    pe.wait_ge(a_mt.sem, a_mt.done(ph["a"] + i))
                    for g in (2 * half, 2 * half + 1):
                        m = minus_max(g, bank[2 + g][:, cols], (2 * c, 2), slice(0, 2 * P), True)
                        if c:
                            m.then_inc(x_st.sem, 1)

            def values(ph, i):
                a = ph["a"] + i
                x = a - a // PB - 1
                pe.wait_ge(a_norm.sem, a_norm.freed(a, 1))
                for c in range(KC):
                    cols = slice(c * 2 * P, (c + 1) * 2 * P)
                    for g in range(4):
                        if c == 0:
                            pe.wait_ge(x_exp.sem, x_exp.done(x, g + 1))
                        pe.matmul(bank[6][group[g], cols], flat(vc[:, 4 * c + g]), pt[:, g, cols], start=True, stop=True)
                    for g in range(4):
                        m = pe.matmul(bank[7][group[g], cols], flat(sumc[:]), pt[:, g, cols], start=True, stop=True)
                        if c:
                            m.then_inc(x_pv.sem, 1)

            for ph in phases:
                fence(pe, "pe", ph["n"])
                {"T": tokens, "E": experts, "C": lambda ph: None, "A": attention}[ph["kind"]](ph)
                if ph["kind"] != "T":
                    pe.drain().then_inc(phase_done["pe"].sem, 1)


def flat(a):
    n = len(a.shape)
    if n == 2:
        return a
    names = " ".join("abcd"[:n - 1])
    return a.rearrange(f"p {names} -> p ({names})")


ROUTE_D = 2 * TB + 1
ROUTE_PICKED = 2 * TB + 5
ROUTE = 2 * TB + 5 + 26
GP_STEPS = 30

def make_plan():
    plan = []
    for b in range(0, B, 2):
        plan += [("T", 0, b, b - 1 if b else None), ("T", 0, b + 1, None), ("E", 0, b, None), ("A", 0, b, None),
                 ("T", 1, b, None), ("A", 0, b + 1, None), ("T", 1, b + 1, None), ("E", 1, b, b)]
    return plan + [("C", 1, B - 1, None)]


PLAN = make_plan()

_INS = ["L0_attn_hidden_states", "L0_attn_Wq", "L0_attn_Wk", "L0_attn_Wv", "L0_attn_Wo", "L0_attn_W1", "L0_attn_b1",
        "L0_attn_W2", "L0_attn_b2", "L0_ffn_router_w", "L0_ffn_router_bias", "L0_ffn_up_proj", "L0_ffn_gate_proj",
        "L0_ffn_down_proj", "L0_ffn_sh_gate", "L0_ffn_sh_up", "L0_ffn_sh_down"]
_TURNED = {"L0_ffn_router_w", "L0_ffn_sh_gate", "L0_ffn_sh_up", "L0_ffn_sh_down"}


def kernel(**inputs):
    import numpy as _np
    import concourse.bacc as _bacc
    from concourse.bass_utils import run_bass_kernel_spmd as _run

    nc = _bacc.Bacc("TRN2", target_bir_lowering=False, num_devices=1)
    arrays, args = {}, []
    for name in _INS:
        a = _np.ascontiguousarray(inputs[name].T if name in _TURNED else inputs[name])
        arrays[f"in_{name}"] = a
        args.append(nc.dram_tensor(f"in_{name}", a.shape, mybir.dt.from_np(a.dtype), kind="ExternalInput").ap())
    out = nc.dram_tensor("out", inputs[_INS[0]].shape, F32, kind="ExternalOutput").ap()
    macaron_kernel(nc, *args, out, PLAN)
    r = _run(nc, [arrays], core_ids=[0])
    return r.results[0]["out"]
```
